# Optimizing a Trainium2 kernel written in Bass

```python
import numpy as np
import jax
import jax.numpy as jnp

def _softmax(x, axis=-1):
    return jax.nn.softmax(x, axis=axis)

def _gelu(x):
    return jax.nn.gelu(x, approximate=True)

def _silu(x):
    return jax.nn.silu(x)

def _sigmoid(x):
    return jax.nn.sigmoid(x)

def _layernorm(x, axis=-1, eps=1e-05):
    m = jnp.mean(x, axis=axis, keepdims=True)
    v = jnp.var(x, axis=axis, keepdims=True)
    return (x - m) / jnp.sqrt(v + eps)

def _scatter_add(tgt, idx, src, axis=0):
    return tgt.at[idx].add(src)

def _segment_sum(src, seg, n):
    return jax.ops.segment_sum(src, seg, n)
kernel_name = 'mk_gnn_ffn_d2_gnn_r32_327130'

def setup_inputs(seed: int=0):
    np.random.seed(seed)
    _w = jnp.asarray

    def _rec_inputs():
        import jax
        import jax.numpy as jnp
        _gk = jax.random.key(seed)
        x = -0.0003713 + 1 * jax.random.normal(jax.random.fold_in(_gk, 1), (3125, 256), jnp.float32)
        src = jax.random.randint(jax.random.fold_in(_gk, 2), (50000,), 0, 3125, jnp.int32)
        dst = jax.random.randint(jax.random.fold_in(_gk, 3), (50000,), 0, 3125, jnp.int32)
        _o = jnp.argsort(dst, stable=True)
        src = src[_o]
        dst = dst[_o]
        edge_type_64 = jax.random.randint(jax.random.fold_in(_gk, 12), (50000,), 0, 64, jnp.int32)
        return (x, src, dst, edge_type_64)
    x, src, dst, edge_type_64 = _rec_inputs()

    def _L0_gnn_setup():
        import jax, jax.numpy as jnp
        import numpy as np
        N = 50000
        NEG_SLOPE = 0.2

        def _gat_conv(x, src, dst, W, a_src, a_dst, b, heads, out_c):
            n = x.shape[0]
            h = (x @ W).reshape(n, heads, out_c)
            s = jnp.einsum('nhc,hc->nh', h, a_src)
            d = jnp.einsum('nhc,hc->nh', h, a_dst)
            e = jax.nn.leaky_relu(s[src] + d[dst], NEG_SLOPE)
            e_max = jax.ops.segment_max(e, dst, num_segments=n)
            e = jnp.exp(e - e_max[dst])
            denom = jax.ops.segment_sum(e, dst, num_segments=n)
            alpha = e / (denom[dst] + 1e-16)
            msg = h[src] * alpha[:, :, None]
            out = jax.ops.segment_sum(msg, dst, num_segments=n)
            return out.reshape(n, heads * out_c) + b
        key = jax.random.key(seed)
        ks = jax.random.split(key, 11)
        E = 25000
        return {'x': jax.random.normal(ks[0], (N, 256), jnp.float32), 'edge_index': jax.random.randint(ks[1], (2, E), 0, N, jnp.int32), 'W1': jax.random.normal(ks[2], (256, 256), jnp.float32) * 0.06, 'att_src1': jax.random.normal(ks[3], (8, 32), jnp.float32) * 0.1, 'att_dst1': jax.random.normal(ks[4], (8, 32), jnp.float32) * 0.1, 'b1': jax.random.normal(ks[5], (256,), jnp.float32) * 0.02, 'W2': jax.random.normal(ks[6], (256, 256), jnp.float32) * 0.06, 'att_src2': jax.random.normal(ks[7], (1, 256), jnp.float32) * 0.05, 'att_dst2': jax.random.normal(ks[8], (1, 256), jnp.float32) * 0.05, 'b2': jax.random.normal(ks[9], (256,), jnp.float32) * 0.02}
    _L0_gnn_all = _L0_gnn_setup()
    _L0_gnn_in = {k: v for k, v in _L0_gnn_all.items() if k in ('W1', 'att_src1', 'att_dst1', 'b1', 'W2', 'att_src2', 'att_dst2', 'b2')}
    del _L0_gnn_all

    def _L0_ffn_setup():
        import jax, jax.numpy as jnp
        import numpy as np
        B, N, D = (16, 128, 256)
        NUM_EXPERTS, TOP_K, HEADS = (4, 2, 4)
        N_EDGES = 32768
        LN_EPS = 1e-05

        def _layernorm(x, g, b):
            mu = x.mean(-1, keepdims=True)
            var = ((x - mu) ** 2).mean(-1, keepdims=True)
            return (x - mu) * jax.lax.rsqrt(var + LN_EPS) * g + b

        def _forward(x, edge_index, W_gat, att_src, att_dst, b_gat, ln_gamma, ln_beta, W1, b1, W2, b2):
            Bc, Nc, Dc = x.shape
            M = Bc * Nc
            x_flat = x.reshape(M, Dc)
            h = (x_flat @ W_gat).reshape(M, HEADS, NUM_EXPERTS)
            loops = jnp.arange(M, dtype=edge_index.dtype)
            src = jnp.concatenate([edge_index[0], loops])
            dst = jnp.concatenate([edge_index[1], loops])
            a_src = (h * att_src).sum(-1)
            a_dst = (h * att_dst).sum(-1)
            e = jax.nn.leaky_relu(a_src[src] + a_dst[dst], negative_slope=0.2)
            e_max = jax.ops.segment_max(e, dst, num_segments=M)
            ee = jnp.exp(e - e_max[dst])
            denom = jax.ops.segment_sum(ee, dst, num_segments=M)
            alpha = ee / (denom[dst] + 1e-16)
            msg = h[src] * alpha[:, :, None]
            agg = jax.ops.segment_sum(msg, dst, num_segments=M).reshape(M, HEADS * NUM_EXPERTS) + b_gat
            scores = _layernorm(agg, ln_gamma, ln_beta).reshape(M, HEADS, NUM_EXPERTS).mean(1)
            scores = scores.reshape(Bc, Nc, NUM_EXPERTS)
            topk_s, topk_i = jax.lax.top_k(scores, TOP_K)
            w = jax.nn.softmax(topk_s, axis=-1)
            out = jnp.zeros_like(x)
            for ei in range(NUM_EXPERTS):
                g = jnp.where(topk_i == ei, w, 0.0).sum(-1)
                hh = jax.nn.gelu(x @ W1[ei] + b1[ei], approximate=False)
                out = out + g[..., None] * (hh @ W2[ei] + b2[ei])
            return out
        key = jax.random.key(seed)
        ks = jax.random.split(key, 8)
        s = 0.05
        return {'x': jax.random.normal(ks[0], (B, N, D), jnp.float32), 'W_gat': jax.random.normal(ks[1], (D, HEADS * NUM_EXPERTS), jnp.float32) * s, 'att_src': jax.random.normal(ks[2], (HEADS, NUM_EXPERTS), jnp.float32) * s, 'att_dst': jax.random.normal(ks[3], (HEADS, NUM_EXPERTS), jnp.float32) * s, 'b_gat': jnp.zeros((HEADS * NUM_EXPERTS,), jnp.float32), 'ln_gamma': jnp.ones((HEADS * NUM_EXPERTS,), jnp.float32), 'ln_beta': jnp.zeros((HEADS * NUM_EXPERTS,), jnp.float32), 'W1': jax.random.normal(ks[4], (NUM_EXPERTS, D, 2 * D), jnp.float32) * s, 'b1': jnp.zeros((NUM_EXPERTS, 2 * D), jnp.float32), 'W2': jax.random.normal(ks[5], (NUM_EXPERTS, 2 * D, D), jnp.float32) * s, 'b2': jnp.zeros((NUM_EXPERTS, D), jnp.float32), 'edge_index': jax.random.randint(ks[6], (2, N_EDGES), 0, B * N, jnp.int32)}
    _L0_ffn_all = _L0_ffn_setup()
    _L0_ffn_in = {k: v for k, v in _L0_ffn_all.items() if k in ('W_gat', 'att_src', 'att_dst', 'b_gat', 'ln_gamma', 'ln_beta', 'W1', 'b1', 'W2', 'b2', 'edge_index')}
    del _L0_ffn_all

    def _L1_gnn_setup():
        import jax, jax.numpy as jnp
        import numpy as np
        N_NODES = 50000
        N_EDGES = 15625
        IN_DIM = 256
        HID = 64
        HEADS = 4
        N_REL = 64
        key = jax.random.key(seed)
        ks = jax.random.split(key, 16)
        s = 0.02
        return {'node_features': jax.random.normal(ks[0], (N_NODES, IN_DIM), jnp.float32), 'edge_index': jax.random.randint(ks[1], (2, N_EDGES), 0, N_NODES, jnp.int32), 'edge_relations': jax.random.randint(ks[2], (N_EDGES,), 0, N_REL, jnp.int32), 'query_emb': jax.random.normal(ks[3], (IN_DIM,), jnp.float32), 'Wq': jax.random.normal(ks[4], (IN_DIM, HID * HEADS), jnp.float32) * s, 'bq': jnp.zeros((HID * HEADS,), jnp.float32), 'Wk': jax.random.normal(ks[5], (IN_DIM, HID * HEADS), jnp.float32) * s, 'bk': jnp.zeros((HID * HEADS,), jnp.float32), 'Wv': jax.random.normal(ks[6], (IN_DIM, HID * HEADS), jnp.float32) * s, 'bv': jnp.zeros((HID * HEADS,), jnp.float32), 'rel_w': jax.random.normal(ks[7], (N_REL, HID), jnp.float32) * s, 'Wo': jax.random.normal(ks[8], (HID * HEADS, IN_DIM), jnp.float32) * s, 'bo': jnp.zeros((IN_DIM,), jnp.float32), 'gamma': jnp.ones((IN_DIM,), jnp.float32), 'beta': jnp.zeros((IN_DIM,), jnp.float32)}
    _L1_gnn_all = _L1_gnn_setup()
    _L1_gnn_in = {k: v for k, v in _L1_gnn_all.items() if k in ('query_emb', 'Wq', 'bq', 'Wk', 'bk', 'Wv', 'bv', 'rel_w', 'Wo', 'bo', 'gamma', 'beta')}
    del _L1_gnn_all

    def _L1_ffn_setup():
        import jax, jax.numpy as jnp
        import numpy as np
        BN_EPS = 0.001

        def _bn(h, g, b, m, v):
            return g * (h - m) * jax.lax.rsqrt(v + BN_EPS) + b
        key = jax.random.key(seed)
        ks = jax.random.split(key, 8)
        B, F, Df = (256, 64, 256)
        E, H, D = (8, 256, 256)
        s1 = 1.0 / np.sqrt(Df)
        s2 = 1.0 / np.sqrt(H)
        return {'x': jax.random.normal(ks[0], (B, F, Df), jnp.float32), 'Wr': jax.random.normal(ks[1], (Df, E), jnp.float32) * s1, 'br': jnp.zeros((E,), jnp.float32), 'W1': jax.random.normal(ks[2], (E, Df, H), jnp.float32) * s1, 'b1': jnp.zeros((E, H), jnp.float32), 'g1': jnp.ones((E, H), jnp.float32), 'be1': jnp.zeros((E, H), jnp.float32), 'm1': jnp.zeros((E, H), jnp.float32), 'v1': jnp.ones((E, H), jnp.float32), 'W2': jax.random.normal(ks[3], (E, H, H), jnp.float32) * s2, 'b2': jnp.zeros((E, H), jnp.float32), 'g2': jnp.ones((E, H), jnp.float32), 'be2': jnp.zeros((E, H), jnp.float32), 'm2': jnp.zeros((E, H), jnp.float32), 'v2': jnp.ones((E, H), jnp.float32), 'Wo': jax.random.normal(ks[4], (E, H, D), jnp.float32) * s2, 'bo': jnp.zeros((E, D), jnp.float32)}
    _L1_ffn_all = _L1_ffn_setup()
    _L1_ffn_in = {k: v for k, v in _L1_ffn_all.items() if k in ('Wr', 'br', 'W1', 'b1', 'g1', 'be1', 'm1', 'v1', 'W2', 'b2', 'g2', 'be2', 'm2', 'v2', 'Wo', 'bo')}
    del _L1_ffn_all
    return {'x': x, 'src': src, 'dst': dst, 'edge_type_64': edge_type_64, 'L0_gnn_W1': _L0_gnn_in['W1'], 'L0_gnn_att_src1': _L0_gnn_in['att_src1'], 'L0_gnn_att_dst1': _L0_gnn_in['att_dst1'], 'L0_gnn_b1': _L0_gnn_in['b1'], 'L0_gnn_W2': _L0_gnn_in['W2'], 'L0_gnn_att_src2': _L0_gnn_in['att_src2'], 'L0_gnn_att_dst2': _L0_gnn_in['att_dst2'], 'L0_gnn_b2': _L0_gnn_in['b2'], 'L0_ffn_W_gat': _L0_ffn_in['W_gat'], 'L0_ffn_att_src': _L0_ffn_in['att_src'], 'L0_ffn_att_dst': _L0_ffn_in['att_dst'], 'L0_ffn_b_gat': _L0_ffn_in['b_gat'], 'L0_ffn_ln_gamma': _L0_ffn_in['ln_gamma'], 'L0_ffn_ln_beta': _L0_ffn_in['ln_beta'], 'L0_ffn_W1': _L0_ffn_in['W1'], 'L0_ffn_b1': _L0_ffn_in['b1'], 'L0_ffn_W2': _L0_ffn_in['W2'], 'L0_ffn_b2': _L0_ffn_in['b2'], 'L0_ffn_edge_index': _L0_ffn_in['edge_index'], 'L1_gnn_query_emb': _L1_gnn_in['query_emb'], 'L1_gnn_Wq': _L1_gnn_in['Wq'], 'L1_gnn_bq': _L1_gnn_in['bq'], 'L1_gnn_Wk': _L1_gnn_in['Wk'], 'L1_gnn_bk': _L1_gnn_in['bk'], 'L1_gnn_Wv': _L1_gnn_in['Wv'], 'L1_gnn_bv': _L1_gnn_in['bv'], 'L1_gnn_rel_w': _L1_gnn_in['rel_w'], 'L1_gnn_Wo': _L1_gnn_in['Wo'], 'L1_gnn_bo': _L1_gnn_in['bo'], 'L1_gnn_gamma': _L1_gnn_in['gamma'], 'L1_gnn_beta': _L1_gnn_in['beta'], 'L1_ffn_Wr': _L1_ffn_in['Wr'], 'L1_ffn_br': _L1_ffn_in['br'], 'L1_ffn_W1': _L1_ffn_in['W1'], 'L1_ffn_b1': _L1_ffn_in['b1'], 'L1_ffn_g1': _L1_ffn_in['g1'], 'L1_ffn_be1': _L1_ffn_in['be1'], 'L1_ffn_m1': _L1_ffn_in['m1'], 'L1_ffn_v1': _L1_ffn_in['v1'], 'L1_ffn_W2': _L1_ffn_in['W2'], 'L1_ffn_b2': _L1_ffn_in['b2'], 'L1_ffn_g2': _L1_ffn_in['g2'], 'L1_ffn_be2': _L1_ffn_in['be2'], 'L1_ffn_m2': _L1_ffn_in['m2'], 'L1_ffn_v2': _L1_ffn_in['v2'], 'L1_ffn_Wo': _L1_ffn_in['Wo'], 'L1_ffn_bo': _L1_ffn_in['bo']}

def reference(x, src, dst, edge_type_64, L0_gnn_W1, L0_gnn_att_src1, L0_gnn_att_dst1, L0_gnn_b1, L0_gnn_W2, L0_gnn_att_src2, L0_gnn_att_dst2, L0_gnn_b2, L0_ffn_W_gat, L0_ffn_att_src, L0_ffn_att_dst, L0_ffn_b_gat, L0_ffn_ln_gamma, L0_ffn_ln_beta, L0_ffn_W1, L0_ffn_b1, L0_ffn_W2, L0_ffn_b2, L0_ffn_edge_index, L1_gnn_query_emb, L1_gnn_Wq, L1_gnn_bq, L1_gnn_Wk, L1_gnn_bk, L1_gnn_Wv, L1_gnn_bv, L1_gnn_rel_w, L1_gnn_Wo, L1_gnn_bo, L1_gnn_gamma, L1_gnn_beta, L1_ffn_Wr, L1_ffn_br, L1_ffn_W1, L1_ffn_b1, L1_ffn_g1, L1_ffn_be1, L1_ffn_m1, L1_ffn_v1, L1_ffn_W2, L1_ffn_b2, L1_ffn_g2, L1_ffn_be2, L1_ffn_m2, L1_ffn_v2, L1_ffn_Wo, L1_ffn_bo):
    import jax
    import jax.numpy as jnp

    def _L0_gnn_ref(x, edge_index, W1, att_src1, att_dst1, b1, W2, att_src2, att_dst2, b2):
        import jax, jax.numpy as jnp
        import numpy as np
        N = 50000
        NEG_SLOPE = 0.2

        def _gat_conv(x, src, dst, W, a_src, a_dst, b, heads, out_c):
            n = x.shape[0]
            h = (x @ W).reshape(n, heads, out_c)
            s = jnp.einsum('nhc,hc->nh', h, a_src)
            d = jnp.einsum('nhc,hc->nh', h, a_dst)
            e = jax.nn.leaky_relu(s[src] + d[dst], NEG_SLOPE)
            e_max = jax.ops.segment_max(e, dst, num_segments=n)
            e = jnp.exp(e - e_max[dst])
            denom = jax.ops.segment_sum(e, dst, num_segments=n)
            alpha = e / (denom[dst] + 1e-16)
            msg = h[src] * alpha[:, :, None]
            out = jax.ops.segment_sum(msg, dst, num_segments=n)
            return out.reshape(n, heads * out_c) + b
        n = x.shape[0]
        loop = jnp.arange(n, dtype=edge_index.dtype)
        src = jnp.concatenate([edge_index[0], loop])
        dst = jnp.concatenate([edge_index[1], loop])
        h = _gat_conv(x, src, dst, W1, att_src1, att_dst1, b1, heads=8, out_c=32)
        h = jax.nn.relu(h)
        out = _gat_conv(h, src, dst, W2, att_src2, att_dst2, b2, heads=1, out_c=256)
        return out

    def _L0_ffn_ref(x, W_gat, att_src, att_dst, b_gat, ln_gamma, ln_beta, W1, b1, W2, b2, edge_index):
        import jax, jax.numpy as jnp
        import numpy as np
        B, N, D = (16, 128, 256)
        NUM_EXPERTS, TOP_K, HEADS = (4, 2, 4)
        N_EDGES = 32768
        LN_EPS = 1e-05

        def _layernorm(x, g, b):
            mu = x.mean(-1, keepdims=True)
            var = ((x - mu) ** 2).mean(-1, keepdims=True)
            return (x - mu) * jax.lax.rsqrt(var + LN_EPS) * g + b

        def _forward(x, edge_index, W_gat, att_src, att_dst, b_gat, ln_gamma, ln_beta, W1, b1, W2, b2):
            Bc, Nc, Dc = x.shape
            M = Bc * Nc
            x_flat = x.reshape(M, Dc)
            h = (x_flat @ W_gat).reshape(M, HEADS, NUM_EXPERTS)
            loops = jnp.arange(M, dtype=edge_index.dtype)
            src = jnp.concatenate([edge_index[0], loops])
            dst = jnp.concatenate([edge_index[1], loops])
            a_src = (h * att_src).sum(-1)
            a_dst = (h * att_dst).sum(-1)
            e = jax.nn.leaky_relu(a_src[src] + a_dst[dst], negative_slope=0.2)
            e_max = jax.ops.segment_max(e, dst, num_segments=M)
            ee = jnp.exp(e - e_max[dst])
            denom = jax.ops.segment_sum(ee, dst, num_segments=M)
            alpha = ee / (denom[dst] + 1e-16)
            msg = h[src] * alpha[:, :, None]
            agg = jax.ops.segment_sum(msg, dst, num_segments=M).reshape(M, HEADS * NUM_EXPERTS) + b_gat
            scores = _layernorm(agg, ln_gamma, ln_beta).reshape(M, HEADS, NUM_EXPERTS).mean(1)
            scores = scores.reshape(Bc, Nc, NUM_EXPERTS)
            topk_s, topk_i = jax.lax.top_k(scores, TOP_K)
            w = jax.nn.softmax(topk_s, axis=-1)
            out = jnp.zeros_like(x)
            for ei in range(NUM_EXPERTS):
                g = jnp.where(topk_i == ei, w, 0.0).sum(-1)
                hh = jax.nn.gelu(x @ W1[ei] + b1[ei], approximate=False)
                out = out + g[..., None] * (hh @ W2[ei] + b2[ei])
            return out
        return _forward(x, edge_index, W_gat, att_src, att_dst, b_gat, ln_gamma, ln_beta, W1, b1, W2, b2)

    def _L1_gnn_ref(node_features, edge_index, edge_relations, query_emb, Wq, bq, Wk, bk, Wv, bv, rel_w, Wo, bo, gamma, beta):
        import jax, jax.numpy as jnp
        import numpy as np
        N_NODES = 50000
        N_EDGES = 15625
        IN_DIM = 256
        HID = 64
        HEADS = 4
        N_REL = 64
        N = node_features.shape[0]
        D = rel_w.shape[1]
        H = Wq.shape[1] // D
        enh = node_features + 0.1 * query_emb[None, :]
        Q = (enh @ Wq + bq).reshape(N, H, D)
        K = (enh @ Wk + bk).reshape(N, H, D)
        V = (enh @ Wv + bv).reshape(N, H, D)
        src, dst = (edge_index[0], edge_index[1])
        rel = rel_w[edge_relations]
        mod_k = K[src] + 0.2 * rel[:, None, :]
        scores = jnp.einsum('ehd,ehd->eh', Q[dst], mod_k) / D ** 0.5
        seg_max = jax.ops.segment_max(scores, dst, num_segments=N)
        ex = jnp.exp(scores - seg_max[dst])
        denom = jax.ops.segment_sum(ex, dst, num_segments=N)
        w = ex / denom[dst]
        agg = jax.ops.segment_sum(w[:, :, None] * V[src], dst, num_segments=N)
        deg = jax.ops.segment_sum(jnp.ones((src.shape[0],), jnp.float32), dst, num_segments=N)
        msgs = jnp.where(deg[:, None, None] > 0, agg, V)
        out = msgs.reshape(N, H * D) @ Wo + bo
        x = out + node_features
        mu = jnp.mean(x, axis=-1, keepdims=True)
        var = jnp.var(x, axis=-1, keepdims=True)
        return (x - mu) / jnp.sqrt(var + 1e-05) * gamma + beta

    def _L1_ffn_ref(x, Wr, br, W1, b1, g1, be1, m1, v1, W2, b2, g2, be2, m2, v2, Wo, bo):
        import jax, jax.numpy as jnp
        import numpy as np
        BN_EPS = 0.001

        def _bn(h, g, b, m, v):
            return g * (h - m) * jax.lax.rsqrt(v + BN_EPS) + b
        feat = jnp.mean(x, axis=0)
        w = jax.nn.softmax(feat @ Wr + br, axis=-1)
        h = jnp.einsum('bfd,edh->bfeh', x, W1) + b1
        h = jax.nn.relu(_bn(h, g1, be1, m1, v1))
        h = jnp.einsum('bfeh,ehk->bfek', h, W2) + b2
        h = jax.nn.relu(_bn(h, g2, be2, m2, v2))
        y = jnp.einsum('bfeh,ehd->bfed', h, Wo) + bo
        return jnp.einsum('bfed,fe->bfd', y, w)
    edge_index = jnp.stack([src, dst])
    x = x + _L0_gnn_ref(_layernorm(x, axis=-1), edge_index, L0_gnn_W1, L0_gnn_att_src1, L0_gnn_att_dst1, L0_gnn_b1, L0_gnn_W2, L0_gnn_att_src2, L0_gnn_att_dst2, L0_gnn_b2)
    x = x + _L0_ffn_ref(_layernorm(x, axis=-1)[None], L0_ffn_W_gat, L0_ffn_att_src, L0_ffn_att_dst, L0_ffn_b_gat, L0_ffn_ln_gamma, L0_ffn_ln_beta, L0_ffn_W1, L0_ffn_b1, L0_ffn_W2, L0_ffn_b2, L0_ffn_edge_index)[0]
    x = x + _L1_gnn_ref(_layernorm(x, axis=-1), edge_index, edge_type_64, L1_gnn_query_emb, L1_gnn_Wq, L1_gnn_bq, L1_gnn_Wk, L1_gnn_bk, L1_gnn_Wv, L1_gnn_bv, L1_gnn_rel_w, L1_gnn_Wo, L1_gnn_bo, L1_gnn_gamma, L1_gnn_beta)
    x = x + _L1_ffn_ref(_layernorm(x, axis=-1)[None], L1_ffn_Wr, L1_ffn_br, L1_ffn_W1, L1_ffn_b1, L1_ffn_g1, L1_ffn_be1, L1_ffn_m1, L1_ffn_v1, L1_ffn_W2, L1_ffn_b2, L1_ffn_g2, L1_ffn_be2, L1_ffn_m2, L1_ffn_v2, L1_ffn_Wo, L1_ffn_bo)[0]
    return x

_drawn_inputs = setup_inputs


def setup_inputs(seed=0):
    import zlib

    import numpy as np

    out = dict(_drawn_inputs(seed))
    spreads = {'L0_ffn_b_gat': (0.0, 0.1),
     'L0_ffn_ln_gamma': (1.0, 0.2),
     'L0_ffn_ln_beta': (0.0, 0.1),
     'L0_ffn_b1': (0.0, 0.1),
     'L0_ffn_b2': (0.0, 0.1),
     'L1_gnn_bq': (0.0, 0.8),
     'L1_gnn_bk': (0.0, 2.0),
     'L1_gnn_bv': (0.0, 0.524),
     'L1_gnn_bo': (0.0, 0.1),
     'L1_gnn_gamma': (1.0, 0.2),
     'L1_gnn_beta': (0.0, 0.1),
     'L1_ffn_br': (0.0, 0.8),
     'L1_ffn_b1': (0.0, 0.625),
     'L1_ffn_g1': (1.0, 0.6),
     'L1_ffn_be1': (0.0, 0.689),
     'L1_ffn_m1': (0.0, 0.649),
     'L1_ffn_v1': (1.0, 0.6),
     'L1_ffn_b2': (0.0, 0.467),
     'L1_ffn_g2': (1.0, 0.6),
     'L1_ffn_be2': (0.0, 0.518),
     'L1_ffn_m2': (0.0, 0.458),
     'L1_ffn_v2': (1.0, 0.6),
     'L1_ffn_bo': (0.0, 0.35)}
    factors = {'L0_gnn_att_dst1': 4.105,
     'L0_gnn_att_src2': 5.161,
     'L0_gnn_att_dst2': 5.371,
     'L1_gnn_query_emb': 8.0,
     'L1_gnn_Wq': 8.0,
     'L1_gnn_Wk': 8.0,
     'L1_gnn_Wv': 3.628,
     'L1_gnn_rel_w': 64.0}
    for name, (base, spread) in spreads.items():
        noise = np.random.default_rng([zlib.crc32(name.encode()), seed]).standard_normal(out[name].shape)
        drawn = base * np.exp(spread * noise) if base else spread * noise
        out[name] = jnp.asarray(drawn.astype(out[name].dtype))
    for name, factor in factors.items():
        out[name] = (out[name] * factor).astype(out[name].dtype)
    return out
```

```python
import numpy as np
from contextlib import ExitStack

import concourse.bass as bass
from concourse import mybir

F32 = mybir.dt.float32
BF16 = mybir.dt.bfloat16
I32 = mybir.dt.int32
ALU = mybir.AluOpType
ACT = mybir.ActivationFunctionType
AX = mybir.AxisListType

P = 128
D = 256
KD = D // P
N = 3125
NT = (N + P - 1) // P
NP = NT * P
LAST = N - (NT - 1) * P
SLOPE = 0.2
LN_EPS = 1e-5
SOFT_EPS = 1e-16
NEG = -1e30
QUAD = 4
FIELDS = 4


class Graph:

    def __init__(self, name, edges, tiles, lanes, group):
        self.name = name
        self.tiles = tiles
        self.lanes = lanes
        self.cols = edges // lanes
        self.group = group
        self.chunks = -(-(edges // P + tiles) // (2 * QUAD)) * (2 * QUAD)
        self.cp = self.chunks // 4
        assert edges == lanes * self.cols and self.chunks == 4 * self.cp
        assert self.chunks % (2 * QUAD) == 0 and self.cp <= P
        assert self.cols % (2 * group) == 0 and self.cols % (2 * QUAD) == 0 and group * tiles <= 512


class Steps:

    def __init__(self, eng, sem):
        self.eng, self.sem, self.n = eng, sem, 0

    def mark(self, ins):
        ins.then_inc(self.sem, 1)
        self.n += 1
        return self.n

    def link(self, ins):
        self.mark(ins)
        self.eng.wait_ge(self.sem, self.n)


def lasting(nc, c, name, count):
    return [c.ctx.enter_context(nc.semaphore(f"{name}{b}")) for b in range(count)]


def make_constants(nc, c):
    with ExitStack() as s:
        filled = s.enter_context(nc.semaphore("const_filled"))
        masked = s.enter_context(nc.semaphore("const_masked"))
        block = s.enter_context(nc.Block())

        @block.gpsimd
        def _(pool):
            step = Steps(pool, filled)
            step.mark(nc.gpsimd.iota(c.iota[:, :], pattern=[[1, P]], base=0, channel_multiplier=0,
                                     allow_small_or_imprecise_dtypes=True))
            step.mark(nc.gpsimd.iota(c.iota_chunk[:, :], pattern=[[1, c.iota_chunk.shape[1]]], base=0,
                                     channel_multiplier=0, allow_small_or_imprecise_dtypes=True))
            step.mark(nc.gpsimd.memset(c.ones[:, :], 1.0))
            step.mark(nc.gpsimd.memset(c.zeros[:, :], 0.0))
            step.mark(nc.gpsimd.memset(c.ident[:, :], 0.0))
            step.mark(nc.gpsimd.memset(c.identb[:, :], 0.0))
            step.mark(nc.gpsimd.memset(c.below[:, :], 0.0))
            step.mark(nc.gpsimd.memset(c.above[:, :], 0.0))
            pool.wait_ge(filled, step.n)
            for t in (c.ident, c.identb):
                nc.gpsimd.affine_select(out=t[:, :], in_=t[:, :], compare_op=ALU.not_equal, fill=1.0, base=0,
                                        pattern=[[-1, P]], channel_multiplier=1).then_inc(masked, 1)
            nc.gpsimd.affine_select(out=c.below[:, :], in_=c.below[:, :], compare_op=ALU.is_ge, fill=1.0, base=0,
                                    pattern=[[1, P]], channel_multiplier=-1).then_inc(masked, 1)
            nc.gpsimd.affine_select(out=c.above[:, :], in_=c.above[:, :], compare_op=ALU.is_ge, fill=1.0, base=0,
                                    pattern=[[-1, P]], channel_multiplier=1).then_inc(masked, 1)
            pool.wait_ge(masked, 4)


def sort_edges(nc, c, g, dst_d, src_d, type_d, meta):
    L, C, T, G = g.lanes, g.cols, g.tiles, g.group
    groups = C // G
    quads = C // QUAD
    nm = g.name
    with ExitStack() as s:
        def sb(name, shape, dt):
            return s.enter_context(nc.sbuf_tensor(f"{nm}_{name}", shape, dt))

        def ps(name, shape, dt=F32):
            return s.enter_context(nc.psum_tensor(f"{nm}_{name}", shape, dt))

        def sem(name):
            return s.enter_context(nc.semaphore(f"{nm}_{name}"))

        rec = sb("rec", [L, C, FIELDS], I32)
        dst = sb("dst", [L, C], I32)
        src = sb("src", [L, C], I32)
        typ = sb("typ", [L, C], I32)
        part = sb("part", [L, C], I32)
        dstf = sb("dstf", [L, C], F32)
        lo = sb("lo", [L, C], F32)
        hi = sb("hi", [L, C], F32)
        fill = sb("fill", [P, g.cp // 4 * 4, FIELDS], I32)
        onelo = sb("onelo", [L, 2, G, P], BF16)
        onehi = sb("onehi", [L, 2, G, T], BF16)
        count = sb("count", [P, C + 1, T], F32)
        count_flat = count[:, :, :].rearrange("p c t -> p (c t)")
        total = sb("total", [P, T], F32)
        tiny = sb("tiny", [P, 4, T], F32)
        whole = sb("whole", [P, T], I32)
        quaddst = sb("quaddst", [L, 2, QUAD], F32)
        quadlo = sb("quadlo", [L, 2, QUAD, P], BF16)
        quadT = sb("quadT", [P, 2, QUAD, P], F32)
        quadhi = sb("quadhi", [L, 2, QUAD, T], F32)
        found = sb("found", [L, 2, QUAD, T], F32)
        first = sb("first", [L, 2, QUAD], F32)
        rank = sb("rank", [L, 2, QUAD], F32)
        junk = sb("junk", [L, 2, QUAD, P], F32)
        place = sb("place", [L, 2, QUAD], I32)
        slot = sb("slot", [L, 2, QUAD, FIELDS], I32)
        chunk_t = sb("chunk_t", [1, g.chunks], F32)
        psC = ps("psC", [P, 2, 512])
        psT = ps("psT", [P, 2, 1024], BF16)
        psR = ps("psR", [P, 2, QUAD * P])
        psL = ps("psL", [P, 2, 512])
        assert meta.shape[0] == g.chunks * P + 2

        loaded = sem("loaded")
        dve = sem("dve")
        filled = sem("filled")
        ready = sem("ready")
        one_ready = sem("one_ready")
        counted = sem("counted")
        evacuated = sem("evacuated")
        totals = sem("totals")
        summed = sem("summed")
        with nc.Block() as block:
            @block.sync
            def _(sp):
                sp.dma_start(dst[:, :], dst_d.rearrange("(l c) -> l c", l=L)).then_inc(loaded, 16)
                sp.dma_start(src[:, :], src_d.rearrange("(l c) -> l c", l=L)).then_inc(loaded, 16)
                if type_d is not None:
                    sp.dma_start(typ[:, :], type_d.rearrange("(l c) -> l c", l=L)).then_inc(loaded, 16)
                sp.wait_ge(ready, 1)
                rows = g.chunks * P // P
                for a in range(0, rows, fill.shape[1]):
                    b = min(a + fill.shape[1], rows)
                    sp.dma_start(meta[1:1 + g.chunks * P, :].rearrange("(p r) f -> p r f", p=P)[:, a:b, :],
                                 fill[:, 0:b - a, :]).then_inc(filled, 16)
                sp.dma_start(meta[0:1, :], fill[0:1, 0, :]).then_inc(filled, 16)
                sp.dma_start(meta[1 + g.chunks * P:2 + g.chunks * P, :], fill[0:1, 0, :]).then_inc(filled, 16)
                sp.wait_ge(filled, 16 * (2 + (rows + fill.shape[1] - 1) // fill.shape[1]))

            @block.vector
            def _(v):
                step = Steps(v, dve)
                step.link(nc.vector.memset(fill[:, :, :], 0))
                step.link(nc.vector.memset(fill[:, :, 1:3], -1))
                v.sem_inc(ready, 1)
                if type_d is None:
                    step.link(nc.vector.memset(rec[:, :, 3], 0))
                v.wait_ge(loaded, 48 if type_d is not None else 32)
                nc.vector.tensor_copy(dstf[:, :], dst[:, :])
                nc.vector.tensor_copy(rec[:, :, 0], src[:, :])
                nc.vector.tensor_copy(rec[:, :, 2], dst[:, :])
                if type_d is not None:
                    nc.vector.tensor_copy(rec[:, :, 3], typ[:, :])
                step.link(nc.vector.tensor_scalar(part[:, :], dst[:, :], P - 1, None, ALU.bitwise_and))
                nc.vector.tensor_copy(rec[:, :, 1], part[:, :])
                step.link(nc.vector.tensor_copy(lo[:, :], part[:, :]))
                step.link(nc.vector.tensor_scalar(part[:, :], dst[:, :], P.bit_length() - 1, None, ALU.arith_shift_right))
                step.link(nc.vector.tensor_copy(hi[:, :], part[:, :]))
                with v.Fori(0, groups // 2, 1) as j:
                    for b in range(2):
                        v.wait_ge(counted, 2 * j + b + 1)
                        col = bass.ds((2 * j + b) * G, G)
                        nc.vector.tensor_tensor(
                            onelo[:, b, :, :], c.iota[0:L, :].unsqueeze(1).broadcast_to([L, G, P]),
                            lo[:, col].unsqueeze(2).broadcast_to([L, G, P]), ALU.is_equal)
                        nc.vector.tensor_tensor(
                            onehi[:, b, :, :], c.iota[0:L, 0:T].unsqueeze(1).broadcast_to([L, G, T]),
                            hi[:, col].unsqueeze(2).broadcast_to([L, G, T]), ALU.is_equal).then_inc(one_ready, 1)
                v.wait_ge(evacuated, groups + 2)
                step.link(nc.vector.memset(count[:, 0, :], 0.0))
                for t in range(T):
                    last = nc.vector.tensor_tensor_scan(count[:, 1:, t], count[:, 1:, t], c.zeros[:, 0:C], 0.0,
                                                        ALU.add, ALU.add)
                    step.mark(last)
                v.wait_ge(dve, step.n)
                step.link(nc.vector.tensor_copy(total[:, :], count[:, C, :]))
                v.sem_inc(totals, 1)
                n_t, after, first_c, base = (tiny[:, k, :] for k in range(4))
                v.wait_ge(summed, 1)
                step.link(nc.vector.tensor_scalar(whole[:, :], psL[:, 0, 0:T], float(P - 1), None, ALU.add))
                step.link(nc.vector.tensor_scalar(whole[:, :], whole[:, :], -P, None, ALU.bitwise_and))
                step.link(nc.vector.tensor_copy(n_t, whole[:, :]))
                step.link(nc.vector.tensor_tensor_scan(after, n_t, c.zeros[:, 0:T], 0.0, ALU.add, ALU.add))
                step.link(nc.vector.tensor_tensor(first_c, after, n_t, ALU.subtract))
                step.link(nc.vector.tensor_tensor(base, first_c, psL[:, 1, 0:T], ALU.add))
                step.link(nc.vector.tensor_scalar(base, base, 1.0, None, ALU.add))
                step.link(nc.vector.memset(chunk_t[:, :], -1.0))
                step.link(nc.vector.tensor_scalar(first_c, first_c, 1.0 / P, None, ALU.mult))
                for t in range(T):
                    step.link(nc.vector.scalar_tensor_tensor(
                        chunk_t[:, :], c.iota_chunk[0:1, 0:g.chunks], first_c[0:1, t:t + 1], chunk_t[:, :],
                        ALU.is_ge, ALU.add))
                step.link(nc.vector.tensor_copy(g.tile_of[:, :], chunk_t[:, :]))
                step.link(nc.vector.tensor_tensor(
                    count[:, 0:C, :], count[:, 0:C, :], base.unsqueeze(1).broadcast_to([P, C, T]), ALU.add))

            @block.tensor
            def _(pe):
                pe.sem_inc(counted, 2)
                with pe.Fori(0, groups // 2, 1) as j:
                    for b in range(2):
                        pe.wait_ge(one_ready, 2 * j + b + 1)
                        pe.wait_ge(evacuated, 2 * j + b + 1)
                        for k in range(G):
                            last = nc.tensor.matmul(psC[:, b, k * T:(k + 1) * T], onelo[:, b, k, :],
                                                    onehi[:, b, k, :], start=True, stop=True)
                        last.then_inc(counted, 1)
                pe.wait_ge(totals, 1)
                nc.tensor.matmul(psL[:, 0, 0:T], c.ones[:, :], total[:, :], start=True, stop=True)
                nc.tensor.matmul(psL[:, 1, 0:T], c.above[:, :], total[:, :], start=True,
                                 stop=True).then_inc(summed, 1)

            @block.scalar
            def _(act):
                act.sem_inc(evacuated, 2)
                with act.Fori(0, groups // 2, 1) as j:
                    for b in range(2):
                        act.wait_ge(counted, 2 * j + b + 3)
                        nc.scalar.activation(
                            count_flat[:, bass.ds((2 * j + b) * (G * T) + T, G * T)],
                            psC[:, b, 0:G * T], ACT.Copy).then_inc(evacuated, 1)

        onehot = sem("onehot")
        turned = sem("turned")
        rows = sem("rows")
        copied = sem("copied")
        looked = sem("looked")
        chain = sem("chain")
        placed = sem("placed")
        passed = sem("passed")
        scattered = lasting(nc, c, f"{nm}_scattered", 2)
        with nc.Block() as block:
            @block.vector
            def _(v):
                v.sem_inc(placed, 2)

                def build(q, b):
                    col = bass.ds(q * QUAD, QUAD)
                    nc.vector.tensor_copy(quaddst[:, b, :], dstf[:, col])
                    nc.vector.tensor_tensor(
                        quadlo[:, b, :, :], c.iota[0:L, :].unsqueeze(1).broadcast_to([L, QUAD, P]),
                        lo[:, col].unsqueeze(2).broadcast_to([L, QUAD, P]), ALU.is_equal).then_inc(onehot, 1)

                def pair(j, first_pair):
                    for b in range(2):
                        v.wait_ge(turned, 2 * j + b + 1)
                        build(2 * j + b, b)
                    for b in range(2):
                        q = 2 * j + b
                        col = bass.ds(q * QUAD, QUAD)
                        nc.vector.tensor_tensor(
                            quadhi[:, b, :, :], c.iota[0:L, 0:T].unsqueeze(1).broadcast_to([L, QUAD, T]),
                            hi[:, col].unsqueeze(2).broadcast_to([L, QUAD, T]), ALU.is_equal).then_inc(chain, 1)
                        v.wait_ge(rows, q + 1)
                        for k in range(QUAD):
                            nc.vector.scalar_tensor_tensor(
                                junk[:, b, k, 0:L], psR[0:L, b, k * P:k * P + L], dstf[:, bass.ds(q * QUAD + k, 1)],
                                c.below[0:L, 0:L], ALU.is_equal, ALU.mult,
                                accum_out=rank[:, b, k:k + 1]).then_inc(chain, 1)
                        v.wait_ge(looked, q + 3)
                        v.wait_ge(chain, 8 * q + 5)
                        nc.vector.tensor_tensor(found[:, b, :, :],
                                                psL[0:L, b, 0:QUAD * T].rearrange("p (k t) -> p k t", k=QUAD),
                                                quadhi[:, b, :, :], ALU.mult).then_inc(chain, 1)
                        v.wait_ge(chain, 8 * q + 6)
                        nc.vector.tensor_reduce(first[:, b, :], found[:, b, :, :], AX.X, ALU.add).then_inc(chain, 1)
                        v.wait_ge(chain, 8 * q + 7)
                        if not first_pair:
                            v.wait_ge(scattered[b], 16 * QUAD * j)
                        nc.vector.tensor_copy(slot[:, b, :, :], rec[:, col, :]).then_inc(chain, 1)
                        nc.vector.tensor_tensor(place[:, b, :], first[:, b, :], rank[:, b, :],
                                                ALU.add).then_inc(placed, 1)

                pair(0, True)
                with v.Fori(1, quads // 2, 1) as j:
                    pair(j, False)

            @block.tensor
            def _(pe):
                pe.sem_inc(turned, 2)
                pe.sem_inc(looked, 2)
                with pe.Fori(0, quads // 2, 1) as j:
                    for b in range(2):
                        q = 2 * j + b
                        pe.wait_ge(onehot, q + 1)
                        pe.wait_ge(copied, q + 1)
                        for k in range(QUAD):
                            last = nc.tensor.transpose(psT[:, b, k * P:k * P + L], quadlo[:, b, k, :], c.identb[0:L, 0:L])
                        last.then_inc(turned, 1)
                        pe.wait_ge(placed, q + 1)
                        for k in range(QUAD):
                            last = nc.tensor.matmul(psR[:, b, k * P:k * P + L],
                                                    quaddst[:, b, k:k + 1].broadcast_to([L, P]), c.ident[0:L, 0:L], start=True, stop=True)
                        last.then_inc(rows, 1)
                    for b in range(2):
                        q = 2 * j + b
                        pe.wait_ge(copied, q + 3)
                        for k in range(QUAD):
                            last = nc.tensor.matmul(psL[0:L, b, k * T:(k + 1) * T], quadT[:, b, k, 0:L],
                                                    count_flat[:, bass.ds((q * QUAD + k) * T, T)],
                                                    start=True, stop=True)
                        last.then_inc(looked, 1)

            @block.scalar
            def _(act):
                act.sem_inc(copied, 2)
                with act.Fori(0, quads // 2, 1) as j:
                    for b in range(2):
                        act.wait_ge(turned, 2 * j + b + 3)
                        act.wait_ge(looked, 2 * j + b + 1)
                        nc.scalar.activation(quadT[:, b, :, 0:L],
                                             psT[:, b, 0:QUAD * P].rearrange("p (k l) -> p k l", k=QUAD)[:, :, 0:L],
                                             ACT.Copy).then_inc(copied, 1)

            @block.gpsimd
            def _(pool):
                with pool.Fori(0, quads // 2, 1) as j:
                    for b in range(2):
                        pool.wait_ge(placed, 2 * j + b + 3)
                        pool.sem_inc(passed, 1)
                        for k in range(QUAD):
                            nc.gpsimd.indirect_dma_start(
                                out=meta[:, :], out_offset=bass.IndirectOffsetOnAxis(ap=place[:, b, k:k + 1], axis=0),
                                in_=slot[:, b, k, :], in_offset=None).then_inc(scattered[b], 16)
                for b in range(2):
                    pool.wait_ge(scattered[b], 16 * QUAD * (quads // 2))


def load_sorted(nc, c, g, meta):
    CP, nm = g.cp, g.name
    with ExitStack() as s:
        raw = s.enter_context(nc.sbuf_tensor(f"{nm}_raw", [CP, 4, P, FIELDS], I32))
        edge = s.enter_context(nc.sbuf_tensor(f"{nm}_edge", [CP, 4, 2], I32))
        vals = s.enter_context(nc.sbuf_tensor(f"{nm}_vals", [CP, 4, 4, P], F32))
        key = s.enter_context(nc.sbuf_tensor(f"{nm}_key", [CP, 4, P + 2], F32))
        psB = s.enter_context(nc.psum_tensor(f"{nm}_psB", [P, 3, 512], F32))
        loaded = s.enter_context(nc.semaphore(f"{nm}_meta_loaded"))
        dve = s.enter_context(nc.semaphore(f"{nm}_meta_dve"))
        ready = s.enter_context(nc.semaphore(f"{nm}_meta_vals"))
        turned = s.enter_context(nc.semaphore(f"{nm}_meta_turned"))
        with nc.Block() as block:
            @block.sync
            def _(sp):
                rows = g.chunks * P
                sp.dma_start(raw[:, :, :, :].rearrange("p g l f -> p g (l f)"),
                             meta[1:1 + rows, :].rearrange("(g p l) f -> p g (l f)", g=4, l=P)).then_inc(loaded, 16)
                before = meta[0:rows, :].rearrange("(g p l) f -> p g l f", g=4, l=P)[:, :, 0, 2:3]
                after = meta[2:2 + rows, :].rearrange("(g p l) f -> p g l f", g=4, l=P)[:, :, P - 1, 2:3]
                sp.dma_start(edge[:, :, 0:1], before, allow_slow_non_contiguous=True).then_inc(loaded, 16)
                sp.dma_start(edge[:, :, 1:2], after, allow_slow_non_contiguous=True).then_inc(loaded, 16)

            @block.vector
            def _(v):
                step = Steps(v, dve)
                v.wait_ge(loaded, 48)
                for k, field in enumerate((0, 1, 3)):
                    nc.vector.tensor_copy(vals[:, k, :, :], raw[:, :, :, field]).then_inc(ready, 1)
                nc.vector.tensor_copy(key[:, :, 0:1], edge[:, :, 0:1])
                nc.vector.tensor_copy(key[:, :, P + 1:P + 2], edge[:, :, 1:2])
                step.link(nc.vector.tensor_copy(key[:, :, 1:P + 1], raw[:, :, :, 2]))
                for shift, out in ((0, g.reset_fwd), (2, g.reset_bwd)):
                    step.link(nc.vector.tensor_tensor(out[:, :, :], key[:, :, 1:P + 1], key[:, :, shift:shift + P],
                                                      ALU.is_equal))
                    step.link(nc.vector.tensor_scalar(out[:, :, :], out[:, :, :], -NEG, NEG, ALU.mult, ALU.add))
                step.link(nc.vector.tensor_scalar(g.is_last[:, :, :], g.reset_bwd[:, :, :], 0.0, None, ALU.is_lt))
                v.wait_ge(turned, 3)
                nc.vector.tensor_copy(g.src[:, :], psB[:, 0, 0:4 * CP])
                nc.vector.tensor_copy(g.lane[:, :], psB[:, 1, 0:4 * CP])
                if g.type is not None:
                    nc.vector.tensor_copy(g.type[:, :], psB[:, 2, 0:4 * CP])

            @block.tensor
            def _(pe):
                for k in range(3):
                    pe.wait_ge(ready, k + 1)
                    for q in range(4):
                        last = nc.tensor.transpose(psB[:, k, q * CP:(q + 1) * CP], vals[:, k, q, :],
                                                   c.ident[0:CP, 0:CP])
                    last.then_inc(turned, 1)


class Holder:
    pass


def open_graph(nc, ctx, g, typed):
    def sb(name, shape, dt):
        return ctx.enter_context(nc.sbuf_tensor(f"{g.name}_{name}", shape, dt))
    g.tile_of = sb("tile_of", [1, g.chunks], I32)
    g.src = sb("src_col", [P, g.chunks], I32)
    g.lane = sb("lane_col", [P, g.chunks], F32)
    g.type = sb("type_col", [P, g.chunks], F32) if typed else None
    g.reset_fwd = sb("reset_fwd", [g.cp, 4, P], F32)
    g.reset_bwd = sb("reset_bwd", [g.cp, 4, P], F32)
    g.is_last = sb("is_last", [g.cp, 4, P], F32)


def open_constants(nc, ctx, most_chunks):
    c = Holder()
    c.ctx = ctx
    def sb(name, shape, dt):
        return ctx.enter_context(nc.sbuf_tensor(name, shape, dt))
    c.iota = sb("iota", [P, P], F32)
    c.iota_chunk = sb("iota_chunk", [1, most_chunks], F32)
    c.ones = sb("ones", [P, P], F32)
    c.zeros = sb("zeros", [P, 512], F32)
    c.ident = sb("ident", [P, P], F32)
    c.identb = sb("identb", [P, P], BF16)
    c.below = sb("below", [P, P], F32)
    c.above = sb("above", [P, P], F32)
    return c


def quads_loop(eng, count, body):
    body(0, 0)
    body(1, 1)
    with eng.Fori(1, count // 2 - 1, 1) as j:
        body(2 * j, 0)
        body(2 * j + 1, 1)
    body(count - 2, 0)
    body(count - 1, 1)


def early(q):
    return isinstance(q, int) and q < 2


def tile_registers(eng, g, q, k_chunks):
    return [eng.value_load(g.tile_of[0:1, bass.ds(q * k_chunks + k, 1)], min_val=0, max_val=g.tiles - 1)
            for k in range(k_chunks)]


def gather_scores(nc, c, g, name, table, spill, node_vals, heads, width, store, K, relation=None):
    quads = g.chunks // K
    row = table.shape[1]
    NV = node_vals.shape[2]
    nodes_flat = node_vals[:, :, :].rearrange("p t n -> p (t n)")
    R = 0 if relation is None else relation.shape[0]
    spilled_cols = slice(0, width) if relation is None else slice(row - width, row)
    with ExitStack() as s:
        def sb(n, shape, dt):
            return s.enter_context(nc.sbuf_tensor(f"{name}_{n}", shape, dt))

        def sem(n):
            return s.enter_context(nc.semaphore(f"{name}_{n}"))

        slot = sb("slot", [P, 2, K], I32)
        rows = sb("rows", [P, 2, K, row], F32)
        onehot = sb("onehot", [P, 2, K, P], F32)
        onehotT = sb("onehotT", [P, 2, K, P], F32)
        psT = s.enter_context(nc.psum_tensor(f"{name}_psT", [P, 2, 512], F32))
        psE = s.enter_context(nc.psum_tensor(f"{name}_psE", [P, 2, 512], F32))
        if R:
            kind = sb("kind", [P, 2, K, R], F32)
            kindT = sb("kindT", [R, 2, K, P], F32)
            psR = s.enter_context(nc.psum_tensor(f"{name}_psR", [P, 2, 512], F32))
            prod = sb("prod", [P, 2, K, D], F32)
        ready = sem("ready")
        gathered = lasting(nc, c, f"{name}_gathered", 2)
        spilled = [sem(f"spilled{b}") for b in range(2)]
        turned = sem("turned")
        copied = sem("copied")
        spread = sem("spread")
        used = sem("used")
        passed = sem("passed")
        chain = sem("chain")
        with nc.Block() as block:
            @block.vector
            def _(v):
                def prepare(q, b):
                    col = bass.ds(q * K, K)
                    nc.vector.tensor_copy(slot[:, b, :], g.src[:, col])
                    if R:
                        nc.vector.tensor_tensor(
                            kind[:, b, :, :], c.iota[:, 0:R].unsqueeze(1).broadcast_to([P, K, R]),
                            g.type[:, col].unsqueeze(2).broadcast_to([P, K, R]), ALU.is_equal)
                    nc.vector.tensor_tensor(
                        onehot[:, b, :, :], c.iota[:, :].unsqueeze(1).broadcast_to([P, K, P]),
                        g.lane[:, col].unsqueeze(2).broadcast_to([P, K, P]), ALU.is_equal).then_inc(ready, 1)

                def use(q, b):
                    v.wait_ge(gathered[b], 8 * K * (q - b) + 16 * K)
                    v.wait_ge(spread, q + 1)
                    if R:
                        key = rows[:, b, :, 0:D].rearrange("p k (h d) -> p k h d", h=heads)
                        for k in range(K):
                            nc.vector.tensor_tensor(
                                prod[:, b, k, :].rearrange("p (h d) -> p h d", h=heads), key[:, k, :, :],
                                psR[:, b, k * R:(k + 1) * R].unsqueeze(1).broadcast_to([P, heads, R]),
                                ALU.add).then_inc(chain, 1)
                        v.wait_ge(chain, (K + 1) * q + K)
                        nc.vector.tensor_tensor(
                            prod[:, b, :, :], prod[:, b, :, :], psE[:, b, 0:K * D].rearrange("p (k n) -> p k n", k=K),
                            ALU.mult).then_inc(chain, 1)
                        v.wait_ge(chain, (K + 1) * q + K + 1)
                        nc.vector.tensor_reduce(
                            store[:, bass.ds(q * K, K), 0:heads],
                            prod[:, b, :, :].rearrange("p k (h d) -> p k h d", h=heads), AX.X,
                            ALU.add).then_inc(used, 1)
                    else:
                        vals = psE[:, b, 0:K * NV].rearrange("p (k n) -> p k n", k=K)
                        col = bass.ds(q * K, K)
                        nc.vector.tensor_tensor(store[:, col, 0:heads], rows[:, b, :, width:width + heads],
                                                vals[:, :, 0:heads], ALU.add)
                        nc.vector.tensor_copy(store[:, col, heads:2 * heads], vals[:, :, heads:2 * heads]).then_inc(used, 1)

                prepare(0, 0)
                prepare(1, 1)
                with v.Fori(0, quads // 2 - 1, 1) as j:
                    for b in range(2):
                        use(2 * j + b, b)
                        prepare(2 * j + 2 + b, b)
                for b in range(2):
                    use(quads - 2 + b, b)

            @block.gpsimd
            def _(pool):
                def body(q, b):
                    pool.wait_ge(ready, q + 1)
                    if not early(q):
                        pool.wait_ge(used, q - 1)
                        pool.wait_ge(spilled[b], 8 * (q - b))
                    pool.sem_inc(passed, 1)
                    for k in range(K):
                        nc.gpsimd.indirect_dma_start(
                            out=rows[:, b, k, :], out_offset=None, in_=table[:, :],
                            in_offset=bass.IndirectOffsetOnAxis(ap=slot[:, b, k:k + 1], axis=0)
                        ).then_inc(gathered[b], 16)
                quads_loop(pool, quads, body)

            @block.sync
            def _(sp):
                def body(q, b):
                    sp.wait_ge(gathered[b], 8 * K * (q - b) + 16 * K)
                    sp.dma_start(spill[bass.ds(q, 1), :, :].rearrange("a p n -> (a p) n"),
                                 rows[:, b, :, spilled_cols]).then_inc(spilled[b], 16)
                quads_loop(sp, quads, body)
                for b in range(2):
                    sp.wait_ge(spilled[b], 8 * quads)

            @block.tensor
            def _(pe):
                def turn(q, b):
                    pe.wait_ge(ready, q + 1)
                    if not early(q):
                        pe.wait_ge(copied, q - 1)
                    for k in range(K):
                        last = nc.tensor.transpose(psT[:, b, k * P:(k + 1) * P], onehot[:, b, k, :], c.ident[:, :])
                        if R:
                            last = nc.tensor.transpose(psT[0:R, b, (K + k) * P:(K + k + 1) * P], kind[:, b, k, :],
                                                       c.ident[:, :])
                    last.then_inc(turned, 1)

                def expand(q, b):
                    tiles = tile_registers(pe, g, q, K)
                    pe.wait_ge(copied, q + 1)
                    if not early(q):
                        pe.wait_ge(used, q - 1)
                    for k in range(K):
                        last = nc.tensor.matmul(psE[:, b, k * NV:(k + 1) * NV], onehotT[:, b, k, :],
                                                nodes_flat[:, bass.ds(tiles[k] * NV, NV)], start=True, stop=True)
                        if R:
                            last = nc.tensor.matmul(psR[:, b, k * R:(k + 1) * R], kindT[:, b, k, :], relation[:, :],
                                                    start=True, stop=True)
                    last.then_inc(spread, 1)

                turn(0, 0)
                turn(1, 1)
                expand(0, 0)
                turn(2, 0)
                expand(1, 1)
                turn(3, 1)
                with pe.Fori(1, quads // 2 - 1, 1) as j:
                    for b in range(2):
                        expand(2 * j + b, b)
                        turn(2 * j + 2 + b, b)
                for b in range(2):
                    expand(quads - 2 + b, b)

            @block.scalar
            def _(act):
                def body(q, b):
                    act.wait_ge(turned, q + 1)
                    if not early(q):
                        act.wait_ge(spread, q - 1)
                    if R:
                        nc.scalar.activation(kindT[:, b, :, :],
                                             psT[0:R, b, K * P:2 * K * P].rearrange("p (k l) -> p k l", k=K), ACT.Copy)
                    nc.scalar.activation(onehotT[:, b, :, :],
                                         psT[:, b, 0:K * P].rearrange("p (k l) -> p k l", k=K),
                                         ACT.Copy).then_inc(copied, 1)
                quads_loop(act, quads, body)


def edge_softmax(nc, c, g, name, heads, store, own, scale):
    CP, CH, H = g.cp, g.chunks, heads
    W = store.shape[2]
    assert W == (2 * H if own else H) + 1
    with ExitStack() as s:
        def sb(n, shape, dt=F32):
            return s.enter_context(nc.sbuf_tensor(f"{name}_{n}", shape, dt))

        def sem(n):
            return s.enter_context(nc.semaphore(f"{name}_{n}"))

        val = sb("val", [CP, H, 4, P])
        loop = sb("loop", [CP, H, 4, P]) if own else None
        fwd = sb("fwd", [CP, H, 4, P])
        bwd = sb("bwd", [CP, H, 4, P])
        reset = sb("reset", [CP, H, 4, P])
        link = sb("link", [CP, 2, 4])
        links = sb("links", [CP, 2, H, 4])
        ends = sb("ends", [H, 2, CH])
        linkT = sb("linkT", [H, 2, CH])
        state = sb("state", [H, 2, CH + 1])
        carry = sb("carry", [CP, 2, 4, H])
        kept = sb("kept", [CP, H, 4])
        into = sb("into", [CP, H, 4])
        ps = s.enter_context(nc.psum_tensor(f"{name}_ps", [P, 8, 512], F32))
        dve = sem("dve")
        scored = sem("scored")
        turned = sem("turned")
        copied = sem("copied")
        tails = sem("tails")
        tailsT = sem("tailsT")
        stated = sem("stated")
        carried = sem("carried")
        shifted = sem("shifted")
        weighted = sem("weighted")
        back = sem("back")
        stored = sem("stored")
        groups = [(0, h) for h in range(H)] + ([(1, h) for h in range(H)] if own else [])
        with nc.Block() as block:
            @block.vector
            def _(v):
                step = Steps(v, dve)
                if own:
                    flat = store[:, :, 0:H]
                    nc.vector.scalar_tensor_tensor(flat, flat, SLOPE, flat, ALU.mult, ALU.max).then_inc(scored, 1)
                else:
                    nc.vector.tensor_scalar(store[:, :, 0:H], store[:, :, 0:H], scale, None, ALU.mult).then_inc(scored, 1)
                nc.vector.tensor_reduce(link[:, 0, :], g.reset_fwd[:, :, :], AX.X, ALU.min)
                step.link(nc.vector.tensor_reduce(link[:, 1, :], g.reset_bwd[:, :, :], AX.X, ALU.min))
                for h in range(H):
                    nc.vector.tensor_copy(links[:, :, h, :], link[:, :, :])
                step.link(nc.vector.memset(state[:, :, :], NEG))
                v.wait_ge(copied, len(groups))
                val_f = val[:, :, :, :].rearrange("p h g l -> p (h g l)")
                reset_f = reset[:, :, :, :].rearrange("p h g l -> p (h g l)")
                fwd_f = fwd[:, :, :, :].rearrange("p h g l -> p (h g l)")
                bwd_f = bwd[:, :, :, :].rearrange("p h g l -> p (h g l)")

                def set_reset(source, edge):
                    for h in range(H):
                        last = nc.vector.tensor_copy(reset[:, h, :, :], source[:, :, :])
                        step.mark(last)
                    v.wait_ge(dve, step.n)
                    step.link(nc.vector.memset(reset[:, :, :, edge:edge + 1], NEG))

                def scan(out, backward):
                    a = (slice(None), slice(None, None, -1)) if backward else (slice(None), slice(None))
                    step.link(nc.vector.tensor_tensor_scan(out[a], reset_f[a], val_f[a], NEG, ALU.add, ALU.max))

                def with_carry(out, side, source, edge, backward):
                    step.link(nc.vector.tensor_tensor(
                        into[:, :, :], carry[:, side, :, :].rearrange("p g h -> p h g"),
                        source[:, :, edge].unsqueeze(1).broadcast_to([CP, H, 4]), ALU.add))
                    step.link(nc.vector.tensor_copy(kept[:, :, :], val[:, :, :, edge]))
                    step.link(nc.vector.tensor_tensor(val[:, :, :, edge], kept[:, :, :], into[:, :, :], ALU.max))
                    scan(out, backward)
                    step.link(nc.vector.tensor_copy(val[:, :, :, edge], kept[:, :, :]))

                set_reset(g.reset_bwd, P - 1)
                scan(bwd_f, True)
                set_reset(g.reset_fwd, 0)
                scan(fwd_f, False)
                v.sem_inc(tails, 1)
                v.wait_ge(tailsT, 1)
                for side in range(2):
                    nc.vector.tensor_copy(ends[:, side, :], ps[0:H, side, 0:CH])
                    step.link(nc.vector.tensor_copy(linkT[:, side, :], ps[0:H, 2 + side, 0:CH]))
                step.link(nc.vector.tensor_tensor_scan(state[:, 0, 1:], linkT[:, 0, :], ends[:, 0, :], NEG,
                                                       ALU.add, ALU.max))
                step.link(nc.vector.tensor_tensor_scan(state[:, 1, 0:CH][:, ::-1], linkT[:, 1, ::-1],
                                                       ends[:, 1, ::-1], NEG, ALU.add, ALU.max))
                v.sem_inc(stated, 1)
                v.wait_ge(carried, 1)
                for side in range(2):
                    step.link(nc.vector.tensor_copy(carry[:, side, :, :],
                                                    ps[0:CP, 4 + side, 0:4 * H].rearrange("p (g h) -> p g h", g=4)))
                with_carry(fwd_f, 0, g.reset_fwd, 0, False)
                set_reset(g.reset_bwd, P - 1)
                with_carry(bwd_f, 1, g.reset_bwd, P - 1, True)
                step.link(nc.vector.tensor_tensor(fwd_f, fwd_f, bwd_f, ALU.max))
                if own:
                    loop_f = loop[:, :, :, :].rearrange("p h g l -> p (h g l)")
                    step.link(nc.vector.tensor_tensor(fwd_f, fwd_f, loop_f, ALU.max))
                nc.vector.tensor_tensor(val_f, val_f, fwd_f, ALU.subtract).then_inc(shifted, 1)
                if own:
                    nc.vector.tensor_tensor(loop_f, loop_f, fwd_f, ALU.subtract).then_inc(shifted, 1)
                    v.wait_ge(weighted, 2)
                    nc.vector.tensor_tensor(
                        loop[:, :, :, :], loop[:, :, :, :],
                        g.is_last[:, :, :].unsqueeze(1).broadcast_to([CP, H, 4, P]), ALU.mult).then_inc(shifted, 1)
                for n in range(len(groups) + 1):
                    v.wait_ge(back, n + 1)
                    nc.vector.tensor_copy(store[:, :, n], ps[:, n % 8, 0:CH]).then_inc(stored, 1)

            @block.tensor
            def _(pe):
                pe.wait_ge(scored, 1)
                for n, (side, h) in enumerate(groups):
                    if n >= 8:
                        pe.wait_ge(copied, n - 7)
                    for q in range(4):
                        last = nc.tensor.transpose(ps[0:CP, n % 8, q * P:(q + 1) * P],
                                                   store[:, q * CP:(q + 1) * CP, side * H + h], c.ident[:, :])
                    last.then_inc(turned, 1)
                pe.wait_ge(tails, 1)
                pe.wait_ge(copied, len(groups))
                for q in range(4):
                    sl = slice(q * CP, (q + 1) * CP)
                    nc.tensor.transpose(ps[0:H, 0, sl], fwd[:, :, q, P - 1], c.ident[0:CP, 0:CP])
                    nc.tensor.transpose(ps[0:H, 1, sl], bwd[:, :, q, 0], c.ident[0:CP, 0:CP])
                    for side in range(2):
                        last = nc.tensor.transpose(ps[0:H, 2 + side, sl], links[:, side, :, q], c.ident[0:CP, 0:CP])
                last.then_inc(tailsT, 1)
                pe.wait_ge(stated, 1)
                for q in range(4):
                    for side in range(2):
                        last = nc.tensor.transpose(ps[0:CP, 4 + side, q * H:(q + 1) * H],
                                                   state[:, side, q * CP + side:(q + 1) * CP + side],
                                                   c.ident[0:H, 0:H])
                last.then_inc(carried, 1)
                for n in range(len(groups) + 1):
                    if n < len(groups):
                        side, h = groups[n]
                        source = (val, loop)[side][:, h, :, :]
                        if side == 0:
                            pe.wait_ge(weighted, 1)
                        else:
                            pe.wait_ge(shifted, 3)
                    else:
                        source = g.is_last[:, :, :]
                    if n >= 8:
                        pe.wait_ge(stored, n - 7)
                    for q in range(4):
                        last = nc.tensor.transpose(ps[:, n % 8, q * CP:(q + 1) * CP], source[:, q, :],
                                                   c.ident[0:CP, 0:CP])
                    last.then_inc(back, 1)

            @block.scalar
            def _(act):
                for n, (side, h) in enumerate(groups):
                    act.wait_ge(turned, n + 1)
                    nc.scalar.activation((val, loop)[side][:, h, :, :],
                                         ps[0:CP, n % 8, :].rearrange("p (g l) -> p g l", g=4),
                                         ACT.Copy).then_inc(copied, 1)
                act.wait_ge(shifted, 1)
                nc.scalar.activation(val[:, :, :, :], val[:, :, :, :], ACT.Exp).then_inc(weighted, 1)
                if own:
                    act.wait_ge(shifted, 2)
                    nc.scalar.activation(loop[:, :, :, :], loop[:, :, :, :], ACT.Exp).then_inc(weighted, 1)


def aggregate(nc, c, g, name, heads, width, spill, store, agg, K):
    quads = g.chunks // K
    W = store.shape[2]
    AW = width + W
    store_flat = store[:, :, :].rearrange("p c w -> p (c w)")
    agg_flat = agg[:, :, :].rearrange("p t w -> p (t w)")
    with ExitStack() as s:
        def sb(n, shape, dt=F32):
            return s.enter_context(nc.sbuf_tensor(f"{name}_{n}", shape, dt))

        def sem(n):
            return s.enter_context(nc.semaphore(f"{name}_{n}"))

        rows = sb("rows", [P, 2, K, width])
        part = sb("part", [P, 2, K, width])
        onehot = sb("onehot", [P, 2, K, P])
        ps = s.enter_context(nc.psum_tensor(f"{name}_psA", [P, 2, K, 512], F32))
        loaded = [sem(f"loaded{b}") for b in range(2)]
        weighed = sem("weighed")
        ready = sem("ready")
        summed = sem("summed")
        added = sem("added")
        zeroed = sem("zeroed")
        with nc.Block() as block:
            @block.sync
            def _(sp):
                def body(q, b):
                    if not early(q):
                        sp.wait_ge(weighed, q - 1)
                    sp.dma_start(rows[:, b, :, :].rearrange("p k n -> p (k n)"),
                                 spill[bass.ds(q, 1), :, :].rearrange("a p n -> (a p) n")).then_inc(loaded[b], 16)
                quads_loop(sp, quads, body)

            @block.gpsimd
            def _(pool):
                def body(q, b):
                    pool.wait_ge(loaded[b], 8 * (q - b) + 16)
                    if not early(q):
                        pool.wait_ge(summed, q - 1)
                    for k in range(K):
                        last = nc.gpsimd.tensor_tensor(
                            part[:, b, k, :].rearrange("p (h n) -> p h n", h=heads),
                            rows[:, b, k, :].rearrange("p (h n) -> p h n", h=heads),
                            store_flat[:, bass.ds((q * K + k) * W, heads)].unsqueeze(2)
                            .broadcast_to([P, heads, width // heads]), ALU.mult)
                    last.then_inc(weighed, 1)
                quads_loop(pool, quads, body)

            @block.tensor
            def _(pe):
                def body(q, b):
                    pe.wait_ge(ready, q + 1)
                    pe.wait_ge(weighed, q + 1)
                    if not early(q):
                        pe.wait_ge(added, K * (q - 1))
                    for k in range(K):
                        nc.tensor.matmul(ps[:, b, k, 0:width], onehot[:, b, k, :], part[:, b, k, :],
                                         start=True, stop=True)
                        last = nc.tensor.matmul(ps[:, b, k, width:AW], onehot[:, b, k, :],
                                                store_flat[:, bass.ds((q * K + k) * W, W)], start=True, stop=True)
                    last.then_inc(summed, 1)
                quads_loop(pe, quads, body)

            @block.vector
            def _(v):
                nc.vector.memset(agg[:, :, :], 0.0).then_inc(zeroed, 1)
                v.wait_ge(zeroed, 1)

                def prepare(q, b):
                    nc.vector.tensor_tensor(
                        onehot[:, b, :, :], c.iota[:, :].unsqueeze(1).broadcast_to([P, K, P]),
                        g.lane[:, bass.ds(q * K, K)].unsqueeze(2).broadcast_to([P, K, P]),
                        ALU.is_equal).then_inc(ready, 1)

                def add(q, b):
                    tiles = tile_registers(v, g, q, K)
                    v.wait_ge(summed, q + 1)
                    for k in range(K):
                        if not (isinstance(q, int) and q == 0 and k == 0):
                            v.wait_ge(added, q * K + k)
                        place = agg_flat[:, bass.ds(tiles[k] * AW, AW)]
                        nc.vector.tensor_tensor(place, place, ps[:, b, k, 0:AW], ALU.add).then_inc(added, 1)

                prepare(0, 0)
                prepare(1, 1)
                add(0, 0)
                prepare(2, 0)
                add(1, 1)
                prepare(3, 1)
                with v.Fori(1, quads // 2 - 1, 1) as j:
                    for b in range(2):
                        add(2 * j + b, b)
                        prepare(2 * j + 2 + b, b)
                add(quads - 2, 0)
                add(quads - 1, 1)


def wait_after(eng, sem, value):
    if not (isinstance(value, int) and value <= 0):
        eng.wait_ge(sem, value)


def load_rows(sp, dst, src, sem):
    sp.dma_start(dst[:, 0:NT - 1, :], src[0:(NT - 1) * P, :].rearrange("(t p) d -> p t d", p=P)).then_inc(sem, 16)
    sp.dma_start(dst[0:LAST, NT - 1, :], src[(NT - 1) * P:N, :]).then_inc(sem, 16)


def load_x(nc, x_d, xs):
    with ExitStack() as s:
        zeroed = s.enter_context(nc.semaphore("x_zeroed"))
        loaded = s.enter_context(nc.semaphore("x_loaded"))
        with nc.Block() as block:
            @block.vector
            def _(v):
                nc.vector.memset(xs[:, NT - 1, :], 0.0).then_inc(zeroed, 1)

            @block.sync
            def _(sp):
                sp.wait_ge(zeroed, 1)
                load_rows(sp, xs, x_d, loaded)
                sp.wait_ge(loaded, 32)


def store_x(nc, xs, out_d):
    with ExitStack() as s:
        stored = s.enter_context(nc.semaphore("out_stored"))
        with nc.Block() as block:
            @block.sync
            def _(sp):
                sp.dma_start(out_d[0:(NT - 1) * P, :].rearrange("(t p) d -> p t d", p=P),
                             xs[:, 0:NT - 1, :]).then_inc(stored, 16)
                sp.dma_start(out_d[(NT - 1) * P:N, :], xs[0:LAST, NT - 1, :]).then_inc(stored, 16)
                sp.wait_ge(stored, 32)


def inverse_root(nc, v, step, x, root, asked, rooted):
    v.sem_inc(asked, 1)
    v.wait_ge(rooted, 1)
    step.link(nc.vector.reciprocal(root, root))
    step.link(nc.vector.tensor_tensor(x, x, root, ALU.mult))
    step.link(nc.vector.tensor_tensor(x, x, root, ALU.mult))
    step.link(nc.vector.tensor_scalar(x, x, -0.5, 1.5, ALU.mult, ALU.add))
    step.link(nc.vector.tensor_tensor(root, root, x, ALU.mult))


def take_root(nc, act, x, root, asked, rooted):
    act.wait_ge(asked, 1)
    nc.scalar.activation(root, x, ACT.Sqrt).then_inc(rooted, 1)


def row_statistics(nc, v, step, x, stats, moments, rstd, asked, rooted):
    for t in range(NT):
        step.mark(nc.vector.bn_stats(stats[:, t, :], x[:, t, :]))
    v.wait_ge(step.sem, step.n)
    for t in range(NT):
        step.mark(nc.vector.bn_aggr(moments[:, t, :], stats[:, t, :]))
    v.wait_ge(step.sem, step.n)
    step.link(nc.vector.tensor_scalar(moments[:, :, 1], moments[:, :, 1], LN_EPS, None, ALU.add))
    inverse_root(nc, v, step, moments[:, :, 1], rstd[:, :], asked, rooted)


def turn_rows(nc, c, name, x, xT, norm, normed=None, shift=None):
    with ExitStack() as s:
        def sb(n, shape, dt=F32):
            return s.enter_context(nc.sbuf_tensor(f"{name}_{n}", shape, dt))

        def sem(n):
            return s.enter_context(nc.semaphore(f"{name}_{n}"))

        ps = s.enter_context(nc.psum_tensor(f"{name}_psX", [P, 8, 512], F32))
        dve, ready, turned, copied = sem("dve"), sem("ready"), sem("turned"), sem("copied")
        asked, rooted = sem("asked"), sem("rooted")
        src = x
        if norm:
            stats = sb("stats", [P, NT, 6])
            moments = sb("moments", [P, NT, 2])
            rstd = sb("rstd", [P, NT])
            src = normed if normed is not None else sb("normed", [P, NT, D])
        groups = [(t0, min(4, NT - t0)) for t0 in range(0, NT, 4)]
        with nc.Block() as block:
            @block.vector
            def _(v):
                step = Steps(v, dve)
                if norm:
                    row_statistics(nc, v, step, x, stats, moments, rstd, asked, rooted)
                    for t in range(NT):
                        nc.vector.tensor_scalar(src[:, t, :], x[:, t, :], moments[:, t, 0:1], rstd[:, t:t + 1],
                                                ALU.subtract, ALU.mult).then_inc(ready, 1)

            @block.tensor
            def _(pe):
                n = 0
                for t0, w in groups:
                    if norm:
                        pe.wait_ge(ready, t0 + w)
                    for k in range(KD):
                        wait_after(pe, copied, n - 7)
                        for i in range(w):
                            last = nc.tensor.transpose(ps[:, n % 8, i * P:(i + 1) * P],
                                                       src[:, t0 + i, k * P:(k + 1) * P], c.ident[:, :])
                        last.then_inc(turned, 1)
                        n += 1

            @block.scalar
            def _(act):
                if norm:
                    take_root(nc, act, moments[:, :, 1], rstd[:, :], asked, rooted)
                n = 0
                for t0, w in groups:
                    for k in range(KD):
                        act.wait_ge(turned, n + 1)
                        out = xT[:, k, t0 * P:(t0 + w) * P]
                        if shift is None:
                            nc.scalar.activation(out, ps[:, n % 8, 0:w * P], ACT.Copy).then_inc(copied, 1)
                        else:
                            nc.scalar.activation(out, ps[:, n % 8, 0:w * P], ACT.Identity,
                                                 bias=shift[:, k:k + 1]).then_inc(copied, 1)
                        n += 1


def project(nc, c, name, xT, weights, bias, out, add=None, table=None):
    M = weights.shape[2]
    with ExitStack() as s:
        def sem(n):
            return s.enter_context(nc.semaphore(f"{name}_{n}"))

        ps = s.enter_context(nc.psum_tensor(f"{name}_psP", [P, 8, 512], F32))
        made, taken, chain, sent = sem("made"), sem("taken"), sem("chain"), sem("sent")
        with nc.Block() as block:
            @block.tensor
            def _(pe):
                for t in range(NT):
                    wait_after(pe, taken, t - 7)
                    for k in range(KD):
                        last = nc.tensor.matmul(ps[:, t % 8, 0:M], xT[:, k, t * P:(t + 1) * P], weights[:, k, :],
                                                start=(k == 0), stop=(k == KD - 1))
                    last.then_inc(made, 1)

            @block.vector
            def _(v):
                step = Steps(v, chain)
                for t in range(NT):
                    v.wait_ge(made, t + 1)
                    got = ps[:, t % 8, 0:M]
                    if bias is None:
                        last = nc.vector.tensor_copy(out[:, t, :], got)
                    else:
                        last = nc.vector.tensor_tensor(out[:, t, :], got, bias[:, :], ALU.add)
                    if add is not None:
                        step.link(last)
                        last = nc.vector.tensor_tensor(out[:, t, :], out[:, t, :], add[:, t, :], ALU.add)
                    last.then_inc(taken, 1)

            if table is not None:
                @block.sync
                def _(sp):
                    w = table.shape[1]
                    sp.wait_ge(taken, NT)
                    sp.dma_start(table.rearrange("(t p) n -> p t n", p=P), out[:, :, 0:w]).then_inc(sent, 16)
                    sp.wait_ge(sent, 16)


def load_weights(nc, name, loads):
    with ExitStack() as s:
        loaded = s.enter_context(nc.semaphore(f"{name}_loaded"))
        with nc.Block() as block:
            @block.sync
            def _(sp):
                for dst, src in loads:
                    sp.dma_start(dst, src, allow_slow_non_contiguous=True).then_inc(loaded, 16)
                sp.wait_ge(loaded, 16 * len(loads))


def by_halves(w):
    return w.rearrange("(k p) n -> p k n", p=P)


def spread_row(v):
    n = v.shape[0]
    return v.rearrange("(a n) -> a n", a=1).broadcast_to([P, n])


def graph_attention(nc, c, g, name, xT, W, att_src, att_dst, bias, heads, scratch, out, load=None):
    HC = W.shape[1]
    H = heads
    C = HC // H
    with ExitStack() as s:
        def sb(n, shape, dt=F32):
            return s.enter_context(nc.sbuf_tensor(f"{name}_{n}", shape, dt))

        def sem(n):
            return s.enter_context(nc.semaphore(f"{name}_{n}"))

        rows = sb("noderows", [P, NT, HC + 2 * H])
        node_vals = sb("node_vals", [P, NT, 2 * H])
        store = sb("store", [P, g.chunks, 2 * H + 1])
        bias_row = sb("bias_row", [P, HC])
        table = scratch["table"][0:NP * (HC + H)].rearrange("(n w) -> n w", w=HC + H)
        spill = scratch["spill"][0:g.chunks * P * HC].rearrange("(q p n) -> q p n", p=P, n=QUAD * HC)
        with ExitStack() as w:
            weights = w.enter_context(nc.sbuf_tensor(f"{name}_weights", [P, KD, HC + 2 * H], F32))
            att = w.enter_context(nc.sbuf_tensor(f"{name}_att", [P, 2, HC], F32))
            prod = w.enter_context(nc.sbuf_tensor(f"{name}_prod", [P, 2 * KD, HC], F32))
            if callable(xT):
                fill_xT, xT = xT, w.enter_context(nc.sbuf_tensor(f"{name}_xT", [P, KD, NP], F32))
                fill_xT(xT)
            load_weights(nc, f"{name}_w", [
                (weights[:, :, 0:HC], by_halves(W)),
                (att[:, 0, :], spread_row(att_src.rearrange("h c -> (h c)"))),
                (att[:, 1, :], spread_row(att_dst.rearrange("h c -> (h c)"))),
                (bias_row[:, :], spread_row(bias))])
            fold = sem("fold")
            with nc.Block() as block:
                @block.vector
                def _(v):
                    step = Steps(v, fold)
                    for k in range(KD):
                        for a in range(2):
                            n = 2 * k + a
                            step.link(nc.vector.tensor_tensor(prod[:, n, :], weights[:, k, 0:HC], att[:, a, :], ALU.mult))
                            step.mark(nc.vector.tensor_reduce(
                                weights[:, k, HC + a * H:HC + (a + 1) * H],
                                prod[:, n, :].rearrange("p (h c) -> p h c", h=H), AX.X, ALU.add))
            project(nc, c, f"{name}_h", xT, weights, None, rows, table=table)
        own = sem("own")
        with nc.Block() as block:
            @block.vector
            def _(v):
                step = Steps(v, own)
                s_part, d_part = rows[:, :, HC:HC + H], rows[:, :, HC + H:HC + 2 * H]
                nc.vector.tensor_copy(node_vals[:, :, 0:H], d_part)
                step.link(nc.vector.tensor_tensor(node_vals[:, :, H:2 * H], s_part, d_part, ALU.add))
                step.link(nc.vector.scalar_tensor_tensor(node_vals[:, :, H:2 * H], node_vals[:, :, H:2 * H], SLOPE,
                                                         node_vals[:, :, H:2 * H], ALU.mult, ALU.max))
        gather_scores(nc, c, g, f"{name}_a", table, spill, node_vals, H, HC, store, QUAD)
        edge_softmax(nc, c, g, f"{name}_b", H, store, True, 1.0)
        agg = sb("agg", [P, NT, HC + 2 * H + 1])
        aggregate(nc, c, g, f"{name}_c", H, HC, spill, store, agg, QUAD)
        loops = sb("loops", [P, NT, H])
        recip = sb("recip", [P, NT, H])
        fin = sem("fin")
        with nc.Block() as block:
            @block.vector
            def _(v):
                step = Steps(v, fin)
                den = agg[:, :, HC:HC + H]
                own_w = agg[:, :, HC + H:HC + 2 * H]
                has = agg[:, :, HC + 2 * H:HC + 2 * H + 1].broadcast_to([P, NT, H])
                step.link(nc.vector.tensor_tensor(loops[:, :, :], own_w, has, ALU.subtract))
                step.link(nc.vector.tensor_scalar(loops[:, :, :], loops[:, :, :], 1.0, None, ALU.add))
                step.link(nc.vector.tensor_tensor(recip[:, :, :], den, loops[:, :, :], ALU.add))
                step.link(nc.vector.tensor_scalar(recip[:, :, :], recip[:, :, :], SOFT_EPS, None, ALU.add))
                step.link(nc.vector.reciprocal(recip[:, :, :], recip[:, :, :]))

                def per_head(a):
                    return a.rearrange("p t (h c) -> p t h c", h=H)

                h_rows = per_head(rows[:, :, 0:HC])
                step.link(nc.vector.tensor_tensor(h_rows, h_rows, loops[:, :, :].unsqueeze(3).broadcast_to([P, NT, H, C]),
                                                  ALU.mult))
                step.link(nc.vector.tensor_tensor(rows[:, :, 0:HC], rows[:, :, 0:HC], agg[:, :, 0:HC], ALU.add))
                step.link(nc.vector.tensor_tensor(h_rows, h_rows, recip[:, :, :].unsqueeze(3).broadcast_to([P, NT, H, C]),
                                                  ALU.mult))
                step.link(nc.vector.tensor_tensor(rows[:, :, 0:HC], rows[:, :, 0:HC],
                                                  bias_row[:, :].unsqueeze(1).broadcast_to([P, NT, HC]), ALU.add))
                out(step, rows[:, :, 0:HC])

            if load is not None:
                @block.sync
                def _(sp):
                    load(sp)


def relation_attention(nc, c, g, w, xs, scratch):
    H = 4
    C = D // H
    with ExitStack() as s:
        def sb(n, shape, dt=F32):
            return s.enter_context(nc.sbuf_tensor(f"r_{n}", shape, dt))

        def sem(n):
            return s.enter_context(nc.semaphore(f"r_{n}"))

        normed = sb("normed", [P, NT, D])
        relation = sb("relation", [w["L1_gnn_rel_w"].shape[0], C])
        store = sb("store", [P, g.chunks, H + 1])
        table = scratch["table"][0:NP * 2 * D].rearrange("(n w) -> n w", w=2 * D)
        spill2 = scratch["spill"][0:g.chunks * P * D].rearrange("(q p n) -> q p n", p=P, n=2 * D)
        shift = sb("shift", [P, KD])
        prep = sem("prep")
        with ExitStack() as q:
            query = q.enter_context(nc.sbuf_tensor("r_query", [P, NT, D], F32))
            with ExitStack() as t:
                xT = t.enter_context(nc.sbuf_tensor("r_xT", [P, KD, NP], F32))
                wq = t.enter_context(nc.sbuf_tensor("r_wq", [P, KD, D], F32))
                bq = t.enter_context(nc.sbuf_tensor("r_bq", [P, D], F32))
                wkv = t.enter_context(nc.sbuf_tensor("r_wkv", [P, KD, 2 * D], F32))
                bkv = t.enter_context(nc.sbuf_tensor("r_bkv", [P, 2 * D], F32))
                kv = t.enter_context(nc.sbuf_tensor("r_kv", [P, NT, 2 * D], F32))
                load_weights(nc, "r_w", [
                    (shift[:, :], w["L1_gnn_query_emb"].rearrange("(k p) -> p k", p=P)),
                    (relation[:, :], w["L1_gnn_rel_w"]),
                    (wq[:, :, :], by_halves(w["L1_gnn_Wq"])), (bq[:, :], spread_row(w["L1_gnn_bq"])),
                    (wkv[:, :, 0:D], by_halves(w["L1_gnn_Wk"])), (wkv[:, :, D:2 * D], by_halves(w["L1_gnn_Wv"])),
                    (bkv[:, 0:D], spread_row(w["L1_gnn_bk"])), (bkv[:, D:2 * D], spread_row(w["L1_gnn_bv"]))])
                with nc.Block() as block:
                    @block.vector
                    def _(v):
                        step = Steps(v, prep)
                        step.link(nc.vector.tensor_scalar(shift[:, :], shift[:, :], 0.1, None, ALU.mult))
                        step.link(nc.vector.tensor_scalar(relation[:, :], relation[:, :], 0.2, None, ALU.mult))
                turn_rows(nc, c, "r_n", xs, xT, True, normed=normed, shift=shift)
                project(nc, c, "r_q", xT, wq, bq, query)
                project(nc, c, "r_kv", xT, wkv, bkv, kv, table=table)
            gather_scores(nc, c, g, "r_a", table, spill2, query, H, D, store, 2, relation=relation)
        edge_softmax(nc, c, g, "r_b", H, store, False, 1.0 / C ** 0.5)
        msgs = sb("msgs", [P, NT, D])
        mT = sb("mT", [P, KD, NP])
        wo = sb("wo", [P, KD, D])
        rows3 = sb("rows3", [P, 3, D])
        load_weights(nc, "r_o", [(wo[:, :, :], by_halves(w["L1_gnn_Wo"])), (rows3[:, 0, :], spread_row(w["L1_gnn_bo"])),
                                 (rows3[:, 1, :], spread_row(w["L1_gnn_gamma"])),
                                 (rows3[:, 2, :], spread_row(w["L1_gnn_beta"])),
                                 (msgs[:, :, :], table.rearrange("(t p) n -> p t n", p=P)[:, :, D:2 * D])])
        with ExitStack() as a:
            agg = a.enter_context(nc.sbuf_tensor("r_agg", [P, NT, D + H + 1], F32))
            aggregate(nc, c, g, "r_c", H, D, spill2, store, agg, 2)
            lone = a.enter_context(nc.sbuf_tensor("r_lone", [P, NT, 1], F32))
            recip = a.enter_context(nc.sbuf_tensor("r_recip", [P, NT, H], F32))
            fin = sem("fin")
            with nc.Block() as block:
                @block.vector
                def _(v):
                    step = Steps(v, fin)
                    step.link(nc.vector.tensor_scalar(lone[:, :, :], agg[:, :, D + H:D + H + 1], -1.0, 1.0,
                                                      ALU.mult, ALU.add))
                    step.link(nc.vector.tensor_tensor(recip[:, :, :], agg[:, :, D:D + H],
                                                      lone[:, :, :].broadcast_to([P, NT, H]), ALU.add))
                    step.link(nc.vector.reciprocal(recip[:, :, :], recip[:, :, :]))
                    step.mark(nc.vector.tensor_tensor(msgs[:, :, :], msgs[:, :, :],
                                                      lone[:, :, :].broadcast_to([P, NT, D]), ALU.mult))
                    part = agg[:, :, 0:D].rearrange("p t (h c) -> p t h c", h=H)
                    step.link(nc.vector.tensor_tensor(part, part, recip[:, :, :].unsqueeze(3).broadcast_to([P, NT, H, C]),
                                                      ALU.mult))
                    step.link(nc.vector.tensor_tensor(msgs[:, :, :], msgs[:, :, :], agg[:, :, 0:D], ALU.add))
        turn_rows(nc, c, "r_m", msgs, mT, False)
        project(nc, c, "r_out", mT, wo, rows3[:, 0, :], msgs, add=normed)
        stats, moments, rstd = sb("stats", [P, NT, 6]), sb("moments", [P, NT, 2]), sb("rstd", [P, NT])
        last_norm, asked, rooted = sem("last_norm"), sem("asked"), sem("rooted")
        with nc.Block() as block:
            @block.vector
            def _(v):
                step = Steps(v, last_norm)
                row_statistics(nc, v, step, msgs, stats, moments, rstd, asked, rooted)
                for t in range(NT):
                    step.mark(nc.vector.tensor_scalar(msgs[:, t, :], msgs[:, t, :], moments[:, t, 0:1],
                                                      rstd[:, t:t + 1], ALU.subtract, ALU.mult))
                v.wait_ge(last_norm, step.n)
                for row, op in ((1, ALU.mult), (2, ALU.add)):
                    step.link(nc.vector.tensor_tensor(msgs[:, :, :], msgs[:, :, :],
                                                      rows3[:, row, :].unsqueeze(1).broadcast_to([P, NT, D]), op))
                step.link(nc.vector.tensor_tensor(xs[:, :, :], xs[:, :, :], msgs[:, :, :], ALU.add))

            @block.scalar
            def _(act):
                take_root(nc, act, moments[:, :, 1], rstd[:, :], asked, rooted)


def top_two_gates(nc, c, w, xT, g, scratch, gate):
    H, E = 4, 4
    with ExitStack() as s:
        def sb(n, shape, dt=F32):
            return s.enter_context(nc.sbuf_tensor(f"t_{n}", shape, dt))

        HE = H * E
        ln = sb("ln", [P, 2, HE])
        work = sb("work", [P, NT, HE])
        col = sb("col", [P, 12, NT])
        score = sb("score", [P, NT, E])
        picks = sb("picks", [P, 2, NT, E])
        equal = sb("equal", [P, NT, E])
        sq = sb("square", [P, NT, HE])
        load_weights(nc, "t_w", [(ln[:, 0, :], spread_row(w["L0_ffn_ln_gamma"])),
                                 (ln[:, 1, :], spread_row(w["L0_ffn_ln_beta"]))])

        def keep(step, got):
            step.link(nc.vector.tensor_copy(work[:, :, :], got))

        graph_attention(nc, c, g, "t", xT, w["L0_ffn_W_gat"], w["L0_ffn_att_src"], w["L0_ffn_att_dst"],
                        w["L0_ffn_b_gat"], H, scratch, keep)
        gates = s.enter_context(nc.semaphore("t_gates"))
        gap_ready = s.enter_context(nc.semaphore("t_gap_ready"))
        gap_exp = s.enter_context(nc.semaphore("t_gap_exp"))
        asked = s.enter_context(nc.semaphore("t_asked"))
        rooted = s.enter_context(nc.semaphore("t_rooted"))
        with nc.Block() as block:
            mean, var, rstd, top1, top2, seen, free, gap, p2, w1, w2, spare = (col[:, k, :] for k in range(12))

            @block.vector
            def _(v):
                step = Steps(v, gates)

                def wide(a, n):
                    return a.unsqueeze(2).broadcast_to([P, NT, n])

                step.link(nc.vector.tensor_reduce(mean, work[:, :, :], AX.X, ALU.add))
                step.link(nc.vector.tensor_scalar(mean, mean, 1.0 / HE, None, ALU.mult))
                step.link(nc.vector.tensor_tensor(work[:, :, :], work[:, :, :], wide(mean, HE), ALU.subtract))
                step.link(nc.vector.tensor_tensor(sq[:, :, :], work[:, :, :], work[:, :, :], ALU.mult))
                step.link(nc.vector.tensor_reduce(var, sq[:, :, :], AX.X, ALU.add))
                step.link(nc.vector.tensor_scalar(var, var, 1.0 / HE, LN_EPS, ALU.mult, ALU.add))
                inverse_root(nc, v, step, var, rstd, asked, rooted)
                step.link(nc.vector.tensor_tensor(work[:, :, :], work[:, :, :], wide(rstd, HE), ALU.mult))
                for k, op in ((0, ALU.mult), (1, ALU.add)):
                    step.link(nc.vector.tensor_tensor(work[:, :, :], work[:, :, :],
                                                      ln[:, k, :].unsqueeze(1).broadcast_to([P, NT, HE]), op))
                step.link(nc.vector.tensor_reduce(score[:, :, :], work[:, :, :].rearrange("p t (h e) -> p t e h", h=H),
                                                  AX.X, ALU.add))
                step.link(nc.vector.tensor_scalar(score[:, :, :], score[:, :, :], 1.0 / H, None, ALU.mult))
                for n, top in enumerate((top1, top2)):
                    step.link(nc.vector.tensor_reduce(top, score[:, :, :], AX.X, ALU.max))
                    step.link(nc.vector.tensor_tensor(equal[:, :, :], score[:, :, :], wide(top, E), ALU.is_equal))
                    step.link(nc.vector.memset(free, 1.0))
                    for e in range(E):
                        step.link(nc.vector.tensor_tensor(picks[:, n, :, e], equal[:, :, e], free, ALU.mult))
                        step.link(nc.vector.tensor_tensor(free, free, picks[:, n, :, e], ALU.subtract))
                    if n == 0:
                        step.link(nc.vector.scalar_tensor_tensor(score[:, :, :], picks[:, 0, :, :], NEG,
                                                                 score[:, :, :], ALU.mult, ALU.add))
                nc.vector.tensor_tensor(gap, top2, top1, ALU.subtract).then_inc(gap_ready, 1)
                v.wait_ge(gap_exp, 1)
                step.link(nc.vector.tensor_scalar(w1, p2, 1.0, None, ALU.add))
                step.link(nc.vector.reciprocal(w1, w1))
                step.link(nc.vector.tensor_tensor(w2, p2, w1, ALU.mult))
                step.link(nc.vector.tensor_tensor(picks[:, 0, :, :], picks[:, 0, :, :], wide(w1, E), ALU.mult))
                step.link(nc.vector.tensor_tensor(picks[:, 1, :, :], picks[:, 1, :, :], wide(w2, E), ALU.mult))
                step.link(nc.vector.tensor_tensor(gate[:, :, :], picks[:, 0, :, :], picks[:, 1, :, :], ALU.add))

            @block.scalar
            def _(act):
                take_root(nc, act, var, rstd, asked, rooted)
                act.wait_ge(gap_ready, 1)
                nc.scalar.activation(p2, gap, ACT.Exp).then_inc(gap_exp, 1)


def experts(nc, c, name, xT, xs, gate, stages, last_w, last_b):
    E = gate.shape[2]
    with ExitStack() as s:
        def sb(n, shape, dt=F32):
            return s.enter_context(nc.sbuf_tensor(f"{name}_{n}", shape, dt))

        def sem(n):
            return s.enter_context(nc.semaphore(f"{name}_{n}"))

        gateT = sb("gateT", [E, NP])
        psA = s.enter_context(nc.psum_tensor(f"{name}_psH", [P, 4, 512], F32))
        psB = s.enter_context(nc.psum_tensor(f"{name}_psY", [P, 2, 2, 512], F32))
        turned, copied, biased, taken = sem("turned"), sem("copied"), sem("biased"), sem("taken")
        with nc.Block() as block:
            @block.tensor
            def _(pe):
                for t in range(NT):
                    wait_after(pe, copied, t - 3)
                    nc.tensor.transpose(psA[0:E, t % 4, 0:P], gate[:, t, :], c.ident[:, :]).then_inc(turned, 1)
                for t in range(NT):
                    pe.wait_ge(copied, t + 1)
                    wait_after(pe, taken, t - 1)
                    nc.tensor.matmul(psB[:, t % 2, 0, 0:D], gateT[:, t * P:(t + 1) * P], last_b[:, :], start=True,
                                     stop=True).then_inc(biased, 1)

            @block.scalar
            def _(act):
                for t in range(NT):
                    act.wait_ge(turned, t + 1)
                    nc.scalar.activation(gateT[:, t * P:(t + 1) * P], psA[0:E, t % 4, 0:P], ACT.Copy).then_inc(copied, 1)

            @block.vector
            def _(v):
                for t in range(NT):
                    v.wait_ge(biased, t + 1)
                    nc.vector.tensor_tensor(xs[:, t, :], xs[:, t, :], psB[:, t % 2, 0, 0:D], ALU.add).then_inc(taken, 1)

        B = 4
        outs = [st[0].shape[3] // P for st in stages]
        PER = sum(outs)
        bufs = [sb(f"hidden{i}", [P, 2, m, B * P]) for i, m in enumerate(outs)]
        made, shaped, finished, added = sem("made"), sem("shaped"), sem("finished"), sem("added")
        xs_flat = xs[:, :, :].rearrange("p t d -> p (t d)")
        gate_flat = gate[:, :, :].rearrange("p t e -> p (t e)")
        whole = NT // B
        rest = NT - whole * B

        def bank(layer, m, e):
            return (e * PER + sum(outs[:layer]) + m) % 4

        assert (E * PER) % 4 == 0

        def blocks_loop(eng, body):
            body(0, B)
            with eng.Fori(1, whole, 1) as j:
                body(j, B)
            if rest:
                body(whole, rest)

        with nc.Block() as block:
            @block.tensor
            def _(pe):
                def hidden(blk, e, layer, tiles):
                    item = blk * E + e
                    weights = stages[layer][0]
                    inputs = weights.shape[2]
                    for m in range(outs[layer]):
                        n = item * PER + sum(outs[:layer]) + m
                        wait_after(pe, shaped, n - 3)
                        if layer and m == 0:
                            pe.wait_ge(shaped, item * PER + sum(outs[:layer]))
                        for k in range(inputs):
                            if layer == 0:
                                src = xT[:, k, bass.ds(blk * (B * P), tiles * P)]
                            else:
                                src = bufs[layer - 1][:, e % 2, k, 0:tiles * P]
                            last = nc.tensor.matmul(psA[:, bank(layer, m, e), 0:tiles * P],
                                                    weights[:, e, k, m * P:(m + 1) * P], src,
                                                    start=(k == 0), stop=(k == inputs - 1))
                        last.then_inc(made, 1)

                def final(blk, e, tiles):
                    item = blk * E + e
                    pe.wait_ge(shaped, (item + 1) * PER)
                    wait_after(pe, added, item - 1)
                    inputs = last_w.shape[2]
                    for t in range(tiles):
                        for k in range(inputs):
                            last = nc.tensor.matmul(psB[:, e % 2, t // 2, (t % 2) * D:(t % 2 + 1) * D],
                                                    bufs[-1][:, e % 2, k, t * P:(t + 1) * P], last_w[:, e, k, :],
                                                    start=(k == 0), stop=(k == inputs - 1))
                    last.then_inc(finished, 1)

                def body(blk, tiles):
                    for e in range(E):
                        for layer in range(len(stages)):
                            hidden(blk, e, layer, tiles)
                        final(blk, e, tiles)
                blocks_loop(pe, body)

            @block.scalar
            def _(act):
                def body(blk, tiles):
                    for e in range(E):
                        item = blk * E + e
                        for layer, (_, func, scale, bias) in enumerate(stages):
                            for m in range(outs[layer]):
                                n = item * PER + sum(outs[:layer]) + m
                                act.wait_ge(made, n + 1)
                                if m == 0:
                                    wait_after(act, finished, item - 1)
                                nc.scalar.activation(
                                    bufs[layer][:, e % 2, m, 0:tiles * P], psA[:, bank(layer, m, e), 0:tiles * P], func,
                                    bias=bias[:, e, m:m + 1],
                                    scale=1.0 if scale is None else scale[:, e, m:m + 1]).then_inc(shaped, 1)
                blocks_loop(act, body)

            @block.vector
            def _(v):
                def body(blk, tiles):
                    for e in range(E):
                        item = blk * E + e
                        v.wait_ge(finished, item + 1)
                        wait_after(v, added, item)
                        for t in range(tiles):
                            rows = xs_flat[:, bass.ds((blk * B + t) * D, D)]
                            last = nc.vector.scalar_tensor_tensor(
                                rows, psB[:, e % 2, t // 2, (t % 2) * D:(t % 2 + 1) * D],
                                gate_flat[:, bass.ds((blk * B + t) * E + e, 1)], rows, ALU.mult, ALU.add)
                        last.then_inc(added, 1)
                blocks_loop(v, body)


def feed_forward_top_two(nc, c, g2, w, xs, scratch):
    E, F = 4, 512
    with ExitStack() as s:
        def sb(n, shape, dt=F32):
            return s.enter_context(nc.sbuf_tensor(f"f_{n}", shape, dt))

        xT = sb("xT", [P, KD, NP])
        gate = sb("gate", [P, NT, E])
        turn_rows(nc, c, "f_n", xs, xT, True)
        top_two_gates(nc, c, w, xT, g2, scratch, gate)
        w1 = sb("w1", [P, E, KD, F])
        w2 = sb("w2", [P, E, F // P, D])
        b1 = sb("b1", [P, E, F // P])
        b2 = sb("b2", [E, D])
        load_weights(nc, "f_w", [
            (w1[:, e, :, :], by_halves(w["L0_ffn_W1"][e])) for e in range(E)] + [
            (w2[:, e, :, :], by_halves(w["L0_ffn_W2"][e])) for e in range(E)] + [
            (b1[:, :, :], w["L0_ffn_b1"].rearrange("e (m p) -> p e m", p=P)),
            (b2[:, :], w["L0_ffn_b2"])])
        experts(nc, c, "f_e", xT, xs, gate, [(w1, ACT.Gelu, None, b1)], w2, b2)


def feed_forward_all(nc, c, w, xs):
    E = 8
    eps = 0.001
    with ExitStack() as s:
        def sb(n, shape, dt=F32):
            return s.enter_context(nc.sbuf_tensor(f"l_{n}", shape, dt))

        def sem(n):
            return s.enter_context(nc.semaphore(f"l_{n}"))

        xT = sb("xT", [P, KD, NP])
        gate = sb("gate", [P, NT, E])
        wr = sb("wr", [P, KD, E])
        br = sb("br", [P, E])
        w1, w2, wo = (sb(n, [P, E, KD, D]) for n in ("w1", "w2", "wo"))
        bn = sb("bn", [P, 2, 5, E, KD])
        scale = sb("scale", [P, 2, E, KD])
        bias = sb("bias", [P, 2, E, KD])
        bo = sb("bo", [E, D])
        turn_rows(nc, c, "l_n", xs, xT, True)
        loads = [(wr[:, :, :], by_halves(w["L1_ffn_Wr"])), (br[:, :], spread_row(w["L1_ffn_br"])),
                 (bo[:, :], w["L1_ffn_bo"])]
        for e in range(E):
            loads += [(w1[:, e, :, :], by_halves(w["L1_ffn_W1"][e])), (w2[:, e, :, :], by_halves(w["L1_ffn_W2"][e])),
                      (wo[:, e, :, :], by_halves(w["L1_ffn_Wo"][e]))]
        for layer, names in enumerate((("b1", "g1", "be1", "m1", "v1"), ("b2", "g2", "be2", "m2", "v2"))):
            for k, n in enumerate(names):
                loads.append((bn[:, layer, k, :, :], w[f"L1_ffn_{n}"].rearrange("e (m p) -> p e m", p=P)))
        load_weights(nc, "l_w", loads)
        project(nc, c, "l_r", xT, wr, br, gate)
        top = sb("top", [P, NT])
        spread = sb("spread", [P, 2, E, KD])
        norm, shifted, exped, asked, rooted = (sem(n) for n in ("norm", "shifted", "exped", "asked", "rooted"))
        with nc.Block() as block:
            @block.vector
            def _(v):
                step = Steps(v, norm)

                def wide(a):
                    return a.unsqueeze(2).broadcast_to([P, NT, E])

                step.link(nc.vector.tensor_reduce(top[:, :], gate[:, :, :], AX.X, ALU.max))
                nc.vector.tensor_tensor(gate[:, :, :], gate[:, :, :], wide(top[:, :]), ALU.subtract).then_inc(shifted, 1)
                step.link(nc.vector.tensor_scalar(spread[:, :, :, :], bn[:, :, 4, :, :], eps, None, ALU.add))
                inverse_root(nc, v, step, spread[:, :, :, :], scale[:, :, :, :], asked, rooted)
                step.mark(nc.vector.tensor_tensor(bias[:, :, :, :], bn[:, :, 0, :, :], bn[:, :, 3, :, :], ALU.subtract))
                step.link(nc.vector.tensor_tensor(scale[:, :, :, :], scale[:, :, :, :], bn[:, :, 1, :, :], ALU.mult))
                step.link(nc.vector.tensor_tensor(bias[:, :, :, :], bias[:, :, :, :], scale[:, :, :, :], ALU.mult))
                step.link(nc.vector.tensor_tensor(bias[:, :, :, :], bias[:, :, :, :], bn[:, :, 2, :, :], ALU.add))
                v.wait_ge(exped, 1)
                step.link(nc.vector.tensor_reduce(top[:, :], gate[:, :, :], AX.X, ALU.add))
                step.link(nc.vector.reciprocal(top[:, :], top[:, :]))
                step.link(nc.vector.tensor_tensor(gate[:, :, :], gate[:, :, :], wide(top[:, :]), ALU.mult))

            @block.scalar
            def _(act):
                act.wait_ge(shifted, 1)
                nc.scalar.activation(gate[:, :, :], gate[:, :, :], ACT.Exp).then_inc(exped, 1)
                take_root(nc, act, spread[:, :, :, :], scale[:, :, :, :], asked, rooted)
        experts(nc, c, "l_e", xT, xs, gate,
                [(w1, ACT.Relu, scale[:, 0, :, :], bias[:, 0, :, :]), (w2, ACT.Relu, scale[:, 1, :, :], bias[:, 1, :, :])],
                wo, bo)


def two_convolutions(nc, c, g1, w, xs, scratch):
    def relu(step, got):
        step.link(nc.vector.tensor_scalar(xs[:, :, :], got, 0.0, None, ALU.max))

    graph_attention(nc, c, g1, "c1", lambda xT: turn_rows(nc, c, "c1_n", xs, xT, True), w["L0_gnn_W1"],
                    w["L0_gnn_att_src1"], w["L0_gnn_att_dst1"], w["L0_gnn_b1"], 8, scratch, relu)

    def add(step, got):
        step.eng.wait_ge(back, 32)
        step.link(nc.vector.tensor_tensor(xs[:, :, :], xs[:, :, :], got, ALU.add))

    with ExitStack() as s:
        back = s.enter_context(nc.semaphore("x_back"))
        graph_attention(nc, c, g1, "c2", lambda xT: turn_rows(nc, c, "c2_n", xs, xT, False), w["L0_gnn_W2"],
                        w["L0_gnn_att_src2"], w["L0_gnn_att_dst2"], w["L0_gnn_b2"], 1, scratch, add,
                        load=lambda sp: load_rows(sp, xs, w["x"], back))


def clear_semaphores(nc):
    ids = sorted({int(x) for x in nc.released_uncleared_semaphores})
    runs = []
    for i in ids:
        if runs and runs[-1].stop == i:
            runs[-1] = range(runs[-1].start, i + 1)
        else:
            runs.append(range(i, i + 1))
    for run in runs:
        nc.all_engine_barrier(sems_to_clear=run)


def gnn_ffn_program(nc, w, out):
    with ExitStack() as ctx:
        g1 = Graph("g1", w["dst"].shape[0], NT, 125, 20)
        g2 = Graph("g2", w["L0_ffn_edge_index"].shape[1], 2048 // P, P, 32)
        c = open_constants(nc, ctx, g1.chunks)
        open_graph(nc, ctx, g1, True)
        open_graph(nc, ctx, g2, False)
        scratch = {"table": nc.dram_tensor("table", (NP * 2 * D,), F32).ap(),
                   "spill": nc.dram_tensor("spill", (g1.chunks * P * D,), F32).ap()}
        make_constants(nc, c)
        for g, dst, src, kind in ((g1, w["dst"], w["src"], w["edge_type_64"]),
                                  (g2, w["L0_ffn_edge_index"][1], w["L0_ffn_edge_index"][0], None)):
            meta = nc.dram_tensor(f"{g.name}_meta", (g.chunks * P + 2, FIELDS), I32).ap()
            sort_edges(nc, c, g, dst, src, kind, meta)
            load_sorted(nc, c, g, meta)
        clear_semaphores(nc)
        xs = ctx.enter_context(nc.sbuf_tensor("xs", [P, NT, D], F32))
        load_x(nc, w["x"], xs)
        two_convolutions(nc, c, g1, w, xs, scratch)
        clear_semaphores(nc)
        feed_forward_top_two(nc, c, g2, w, xs, scratch)
        clear_semaphores(nc)
        relation_attention(nc, c, g1, w, xs, scratch)
        clear_semaphores(nc)
        feed_forward_all(nc, c, w, xs)
        clear_semaphores(nc)
        store_x(nc, xs, out)


def kernel(**inputs):
    import concourse.bacc as bacc
    from concourse.bass_utils import run_bass_kernel_spmd

    nc = bacc.Bacc("TRN2", target_bir_lowering=False, num_devices=1)
    arrays, w = {}, {}
    for name, value in inputs.items():
        a = np.ascontiguousarray(value)
        arrays[f"in_{name}"] = a
        w[name] = nc.dram_tensor(f"in_{name}", a.shape, mybir.dt.from_np(a.dtype), kind="ExternalInput").ap()
    out = nc.dram_tensor("out_x", inputs["x"].shape, F32, kind="ExternalOutput").ap()
    gnn_ffn_program(nc, w, out)
    r = run_bass_kernel_spmd(nc, [arrays], core_ids=[0])
    return r.results[0]["out_x"]
```

```python
import numpy as np
from contextlib import ExitStack

import concourse.bass as bass
from concourse import mybir

F32 = mybir.dt.float32
BF16 = mybir.dt.bfloat16
I32 = mybir.dt.int32
ALU = mybir.AluOpType
ACT = mybir.ActivationFunctionType
AX = mybir.AxisListType

P = 128
D = 256
KD = D // P
N = 3125
NT = (N + P - 1) // P
NP = NT * P
LAST = N - (NT - 1) * P
SLOPE = 0.2
LN_EPS = 1e-5
SOFT_EPS = 1e-16
NEG = -1e30
QUAD = 4
RING = 4
PARTS = 3
FIELDS = 4


class Graph:

    def __init__(self, name, edges, tiles, lanes, group):
        self.name = name
        self.tiles = tiles
        self.lanes = lanes
        self.cols = edges // lanes
        self.group = group
        self.chunks = -(-(edges // P + tiles) // (RING * QUAD)) * (RING * QUAD)
        self.cp = self.chunks // 4
        assert edges == lanes * self.cols and self.chunks == 4 * self.cp
        assert self.chunks % (RING * QUAD) == 0 and self.cp <= P
        assert self.cols % (2 * group) == 0 and self.cols % (2 * QUAD) == 0 and group * tiles <= 512


class Steps:

    def __init__(self, nc, eng, sem):
        self.nc, self.eng, self.sem, self.n = nc, eng, sem, 0

    def mark(self, ins):
        ins.then_inc(self.sem, 1)
        self.n += 1
        return self.n

    def link(self, ins):
        self.mark(ins)
        self.eng.wait_ge(self.sem, self.n)


def lasting(nc, c, name, count):
    return [c.ctx.enter_context(nc.semaphore(f"{name}{b}")) for b in range(count)]


def make_constants(nc, c):
    with ExitStack() as s:
        filled = s.enter_context(nc.semaphore("const_filled"))
        masked = s.enter_context(nc.semaphore("const_masked"))
        block = s.enter_context(nc.Block())

        @block.gpsimd
        def _(pool):
            step = Steps(nc, pool, filled)
            step.mark(nc.gpsimd.iota(c.iota[:, :], pattern=[[1, P]], base=0, channel_multiplier=0,
                                     allow_small_or_imprecise_dtypes=True))
            step.mark(nc.gpsimd.iota(c.iota_chunk[:, :], pattern=[[1, c.iota_chunk.shape[1]]], base=0,
                                     channel_multiplier=0, allow_small_or_imprecise_dtypes=True))
            step.mark(nc.gpsimd.memset(c.ones[:, :], 1.0))
            step.mark(nc.gpsimd.memset(c.zeros[:, :], 0.0))
            step.mark(nc.gpsimd.memset(c.ident[:, :], 0.0))
            step.mark(nc.gpsimd.memset(c.identb[:, :], 0.0))
            step.mark(nc.gpsimd.memset(c.below[:, :], 0.0))
            step.mark(nc.gpsimd.memset(c.above[:, :], 0.0))
            pool.wait_ge(filled, step.n)
            for t in (c.ident, c.identb):
                nc.gpsimd.affine_select(out=t[:, :], in_=t[:, :], compare_op=ALU.not_equal, fill=1.0, base=0,
                                        pattern=[[-1, P]], channel_multiplier=1).then_inc(masked, 1)
            nc.gpsimd.affine_select(out=c.below[:, :], in_=c.below[:, :], compare_op=ALU.is_ge, fill=1.0, base=0,
                                    pattern=[[1, P]], channel_multiplier=-1).then_inc(masked, 1)
            nc.gpsimd.affine_select(out=c.above[:, :], in_=c.above[:, :], compare_op=ALU.is_ge, fill=1.0, base=0,
                                    pattern=[[-1, P]], channel_multiplier=1).then_inc(masked, 1)
            pool.wait_ge(masked, 4)


def sort_edges(nc, c, g, dst_d, src_d, type_d, meta):
    L, C, T, G = g.lanes, g.cols, g.tiles, g.group
    groups = C // G
    quads = C // QUAD
    nm = g.name
    with ExitStack() as s:
        def sb(name, shape, dt):
            return s.enter_context(nc.sbuf_tensor(f"{nm}_{name}", shape, dt))

        def ps(name, shape, dt=F32):
            return s.enter_context(nc.psum_tensor(f"{nm}_{name}", shape, dt))

        def sem(name):
            return s.enter_context(nc.semaphore(f"{nm}_{name}"))

        rec = sb("rec", [L, C, FIELDS], I32)
        dst = sb("dst", [L, C], I32)
        src = sb("src", [L, C], I32)
        typ = sb("typ", [L, C], I32)
        part = sb("part", [L, C], I32)
        dstf = sb("dstf", [L, C], F32)
        lo = sb("lo", [L, C], F32)
        hi = sb("hi", [L, C], F32)
        fill = sb("fill", [P, g.cp // 4 * 4, FIELDS], I32)
        onelo = sb("onelo", [L, 2, G, P], BF16)
        onehi = sb("onehi", [L, 2, G, T], BF16)
        count = sb("count", [P, C + 1, T], F32)
        count_flat = count[:, :, :].rearrange("p c t -> p (c t)")
        total = sb("total", [P, T], F32)
        tiny = sb("tiny", [P, 4, T], F32)
        whole = sb("whole", [P, T], I32)
        quaddst = sb("quaddst", [L, 2, QUAD], F32)
        quadlo = sb("quadlo", [L, 2, QUAD, P], BF16)
        quadT = sb("quadT", [P, 2, QUAD, P], F32)
        quadhi = sb("quadhi", [L, 2, QUAD, T], F32)
        found = sb("found", [L, 2, QUAD, T], F32)
        first = sb("first", [L, 2, QUAD], F32)
        rank = sb("rank", [L, 2, QUAD], F32)
        junk = sb("junk", [L, 2, QUAD, P], F32)
        place = sb("place", [L, 2, QUAD], I32)
        slot = sb("slot", [L, 2, QUAD, FIELDS], I32)
        chunk_t = sb("chunk_t", [1, g.chunks], F32)
        psC = ps("psC", [P, 2, 512])
        psT = ps("psT", [P, 2, 1024], BF16)
        psR = ps("psR", [P, 2, QUAD * P])
        psL = ps("psL", [P, 2, 512])
        assert meta.shape[0] == g.chunks * P + 2

        loaded = sem("loaded")
        dve = sem("dve")
        filled = sem("filled")
        ready = sem("ready")
        one_ready = sem("one_ready")
        counted = sem("counted")
        evacuated = sem("evacuated")
        totals = sem("totals")
        summed = sem("summed")
        with nc.Block() as block:
            @block.sync
            def _(sp):
                sp.dma_start(dst[:, :], dst_d.rearrange("(l c) -> l c", l=L)).then_inc(loaded, 16)
                sp.dma_start(src[:, :], src_d.rearrange("(l c) -> l c", l=L)).then_inc(loaded, 16)
                if type_d is not None:
                    sp.dma_start(typ[:, :], type_d.rearrange("(l c) -> l c", l=L)).then_inc(loaded, 16)
                sp.wait_ge(ready, 1)
                rows = g.chunks * P // P
                for a in range(0, rows, fill.shape[1]):
                    b = min(a + fill.shape[1], rows)
                    sp.dma_start(meta[1:1 + g.chunks * P, :].rearrange("(p r) f -> p r f", p=P)[:, a:b, :],
                                 fill[:, 0:b - a, :]).then_inc(filled, 16)
                sp.dma_start(meta[0:1, :], fill[0:1, 0, :]).then_inc(filled, 16)
                sp.dma_start(meta[1 + g.chunks * P:2 + g.chunks * P, :], fill[0:1, 0, :]).then_inc(filled, 16)
                sp.wait_ge(filled, 16 * (2 + (rows + fill.shape[1] - 1) // fill.shape[1]))

            @block.vector
            def _(v):
                step = Steps(nc, v, dve)
                step.link(nc.vector.memset(fill[:, :, :], 0))
                step.link(nc.vector.memset(fill[:, :, 1:3], -1))
                v.sem_inc(ready, 1)
                if type_d is None:
                    step.link(nc.vector.memset(rec[:, :, 3], 0))
                v.wait_ge(loaded, 48 if type_d is not None else 32)
                nc.vector.tensor_copy(dstf[:, :], dst[:, :])
                nc.vector.tensor_copy(rec[:, :, 0], src[:, :])
                nc.vector.tensor_copy(rec[:, :, 2], dst[:, :])
                if type_d is not None:
                    nc.vector.tensor_copy(rec[:, :, 3], typ[:, :])
                step.link(nc.vector.tensor_scalar(part[:, :], dst[:, :], P - 1, None, ALU.bitwise_and))
                nc.vector.tensor_copy(rec[:, :, 1], part[:, :])
                step.link(nc.vector.tensor_copy(lo[:, :], part[:, :]))
                step.link(nc.vector.tensor_scalar(part[:, :], dst[:, :], P.bit_length() - 1, None, ALU.arith_shift_right))
                step.link(nc.vector.tensor_copy(hi[:, :], part[:, :]))
                with v.Fori(0, groups // 2, 1) as j:
                    for b in range(2):
                        v.wait_ge(counted, 2 * j + b + 1)
                        col = bass.ds((2 * j + b) * G, G)
                        nc.vector.tensor_tensor(
                            onelo[:, b, :, :], c.iota[0:L, :].unsqueeze(1).broadcast_to([L, G, P]),
                            lo[:, col].unsqueeze(2).broadcast_to([L, G, P]), ALU.is_equal)
                        nc.vector.tensor_tensor(
                            onehi[:, b, :, :], c.iota[0:L, 0:T].unsqueeze(1).broadcast_to([L, G, T]),
                            hi[:, col].unsqueeze(2).broadcast_to([L, G, T]), ALU.is_equal).then_inc(one_ready, 1)
                v.wait_ge(evacuated, groups + 2)
                step.link(nc.vector.memset(count[:, 0, :], 0.0))
                for t in range(T):
                    last = nc.vector.tensor_tensor_scan(count[:, 1:, t], count[:, 1:, t], c.zeros[:, 0:C], 0.0,
                                                        ALU.add, ALU.add)
                    step.mark(last)
                v.wait_ge(dve, step.n)
                step.link(nc.vector.tensor_copy(total[:, :], count[:, C, :]))
                v.sem_inc(totals, 1)
                n_t, after, first_c, base = (tiny[:, k, :] for k in range(4))
                v.wait_ge(summed, 1)
                step.link(nc.vector.tensor_scalar(whole[:, :], psL[:, 0, 0:T], float(P - 1), None, ALU.add))
                step.link(nc.vector.tensor_scalar(whole[:, :], whole[:, :], -P, None, ALU.bitwise_and))
                step.link(nc.vector.tensor_copy(n_t, whole[:, :]))
                step.link(nc.vector.tensor_tensor_scan(after, n_t, c.zeros[:, 0:T], 0.0, ALU.add, ALU.add))
                step.link(nc.vector.tensor_tensor(first_c, after, n_t, ALU.subtract))
                step.link(nc.vector.tensor_tensor(base, first_c, psL[:, 1, 0:T], ALU.add))
                step.link(nc.vector.tensor_scalar(base, base, 1.0, None, ALU.add))
                step.link(nc.vector.memset(chunk_t[:, :], -1.0))
                step.link(nc.vector.tensor_scalar(first_c, first_c, 1.0 / P, None, ALU.mult))
                for t in range(T):
                    step.link(nc.vector.scalar_tensor_tensor(
                        chunk_t[:, :], c.iota_chunk[0:1, 0:g.chunks], first_c[0:1, t:t + 1], chunk_t[:, :],
                        ALU.is_ge, ALU.add))
                step.link(nc.vector.tensor_copy(g.tile_of[:, :], chunk_t[:, :]))
                step.link(nc.vector.tensor_tensor(
                    count[:, 0:C, :], count[:, 0:C, :], base.unsqueeze(1).broadcast_to([P, C, T]), ALU.add))

            @block.tensor
            def _(pe):
                pe.sem_inc(counted, 2)
                with pe.Fori(0, groups // 2, 1) as j:
                    for b in range(2):
                        pe.wait_ge(one_ready, 2 * j + b + 1)
                        pe.wait_ge(evacuated, 2 * j + b + 1)
                        for k in range(G):
                            last = nc.tensor.matmul(psC[:, b, k * T:(k + 1) * T], onelo[:, b, k, :],
                                                    onehi[:, b, k, :], start=True, stop=True)
                        last.then_inc(counted, 1)
                pe.wait_ge(totals, 1)
                nc.tensor.matmul(psL[:, 0, 0:T], c.ones[:, :], total[:, :], start=True, stop=True)
                nc.tensor.matmul(psL[:, 1, 0:T], c.above[:, :], total[:, :], start=True,
                                 stop=True).then_inc(summed, 1)

            @block.scalar
            def _(act):
                act.sem_inc(evacuated, 2)
                with act.Fori(0, groups // 2, 1) as j:
                    for b in range(2):
                        act.wait_ge(counted, 2 * j + b + 3)
                        nc.scalar.activation(
                            count_flat[:, bass.ds((2 * j + b) * (G * T) + T, G * T)],
                            psC[:, b, 0:G * T], ACT.Copy).then_inc(evacuated, 1)

        onehot = sem("onehot")
        turned = sem("turned")
        rows = sem("rows")
        copied = sem("copied")
        looked = sem("looked")
        chain = sem("chain")
        placed = sem("placed")
        passed = sem("passed")
        scattered = lasting(nc, c, f"{nm}_scattered", 2)
        with nc.Block() as block:
            @block.vector
            def _(v):
                v.sem_inc(placed, 2)

                def build(q, b):
                    col = bass.ds(q * QUAD, QUAD)
                    nc.vector.tensor_copy(quaddst[:, b, :], dstf[:, col])
                    nc.vector.tensor_tensor(
                        quadlo[:, b, :, :], c.iota[0:L, :].unsqueeze(1).broadcast_to([L, QUAD, P]),
                        lo[:, col].unsqueeze(2).broadcast_to([L, QUAD, P]), ALU.is_equal).then_inc(onehot, 1)

                def pair(j, first_pair):
                    for b in range(2):
                        v.wait_ge(turned, 2 * j + b + 1)
                        build(2 * j + b, b)
                    for b in range(2):
                        q = 2 * j + b
                        col = bass.ds(q * QUAD, QUAD)
                        nc.vector.tensor_tensor(
                            quadhi[:, b, :, :], c.iota[0:L, 0:T].unsqueeze(1).broadcast_to([L, QUAD, T]),
                            hi[:, col].unsqueeze(2).broadcast_to([L, QUAD, T]), ALU.is_equal).then_inc(chain, 1)
                        v.wait_ge(rows, q + 1)
                        for k in range(QUAD):
                            nc.vector.scalar_tensor_tensor(
                                junk[:, b, k, 0:L], psR[0:L, b, k * P:k * P + L], dstf[:, bass.ds(q * QUAD + k, 1)],
                                c.below[0:L, 0:L], ALU.is_equal, ALU.mult,
                                accum_out=rank[:, b, k:k + 1]).then_inc(chain, 1)
                        v.wait_ge(looked, q + 3)
                        v.wait_ge(chain, 8 * q + 5)
                        nc.vector.tensor_tensor(found[:, b, :, :],
                                                psL[0:L, b, 0:QUAD * T].rearrange("p (k t) -> p k t", k=QUAD),
                                                quadhi[:, b, :, :], ALU.mult).then_inc(chain, 1)
                        v.wait_ge(chain, 8 * q + 6)
                        nc.vector.tensor_reduce(first[:, b, :], found[:, b, :, :], AX.X, ALU.add).then_inc(chain, 1)
                        v.wait_ge(chain, 8 * q + 7)
                        if not first_pair:
                            v.wait_ge(scattered[b], 16 * QUAD * j)
                        nc.vector.tensor_copy(slot[:, b, :, :], rec[:, col, :]).then_inc(chain, 1)
                        nc.vector.tensor_tensor(place[:, b, :], first[:, b, :], rank[:, b, :],
                                                ALU.add).then_inc(placed, 1)

                pair(0, True)
                with v.Fori(1, quads // 2, 1) as j:
                    pair(j, False)

            @block.tensor
            def _(pe):
                pe.sem_inc(turned, 2)
                pe.sem_inc(looked, 2)
                with pe.Fori(0, quads // 2, 1) as j:
                    for b in range(2):
                        q = 2 * j + b
                        pe.wait_ge(onehot, q + 1)
                        pe.wait_ge(copied, q + 1)
                        for k in range(QUAD):
                            last = nc.tensor.transpose(psT[:, b, k * P:k * P + L], quadlo[:, b, k, :], c.identb[0:L, 0:L])
                        last.then_inc(turned, 1)
                        pe.wait_ge(placed, q + 1)
                        for k in range(QUAD):
                            last = nc.tensor.matmul(psR[:, b, k * P:k * P + L],
                                                    quaddst[:, b, k:k + 1].broadcast_to([L, P]), c.ident[0:L, 0:L], start=True, stop=True)
                        last.then_inc(rows, 1)
                    for b in range(2):
                        q = 2 * j + b
                        pe.wait_ge(copied, q + 3)
                        for k in range(QUAD):
                            last = nc.tensor.matmul(psL[0:L, b, k * T:(k + 1) * T], quadT[:, b, k, 0:L],
                                                    count_flat[:, bass.ds((q * QUAD + k) * T, T)],
                                                    start=True, stop=True)
                        last.then_inc(looked, 1)

            @block.scalar
            def _(act):
                act.sem_inc(copied, 2)
                with act.Fori(0, quads // 2, 1) as j:
                    for b in range(2):
                        act.wait_ge(turned, 2 * j + b + 3)
                        act.wait_ge(looked, 2 * j + b + 1)
                        nc.scalar.activation(quadT[:, b, :, 0:L],
                                             psT[:, b, 0:QUAD * P].rearrange("p (k l) -> p k l", k=QUAD)[:, :, 0:L],
                                             ACT.Copy).then_inc(copied, 1)

            @block.gpsimd
            def _(pool):
                with pool.Fori(0, quads // 2, 1) as j:
                    for b in range(2):
                        pool.wait_ge(placed, 2 * j + b + 3)
                        pool.sem_inc(passed, 1)
                        for k in range(QUAD):
                            nc.gpsimd.indirect_dma_start(
                                out=meta[:, :], out_offset=bass.IndirectOffsetOnAxis(ap=place[:, b, k:k + 1], axis=0),
                                in_=slot[:, b, k, :], in_offset=None).then_inc(scattered[b], 16)
                for b in range(2):
                    pool.wait_ge(scattered[b], 16 * QUAD * (quads // 2))


def load_sorted(nc, c, g, meta):
    CP, nm = g.cp, g.name
    with ExitStack() as s:
        raw = s.enter_context(nc.sbuf_tensor(f"{nm}_raw", [CP, 4, P, FIELDS], I32))
        edge = s.enter_context(nc.sbuf_tensor(f"{nm}_edge", [CP, 4, 2], I32))
        vals = s.enter_context(nc.sbuf_tensor(f"{nm}_vals", [CP, 4, 4, P], F32))
        key = s.enter_context(nc.sbuf_tensor(f"{nm}_key", [CP, 4, P + 2], F32))
        psB = s.enter_context(nc.psum_tensor(f"{nm}_psB", [P, 3, 512], F32))
        loaded = s.enter_context(nc.semaphore(f"{nm}_meta_loaded"))
        dve = s.enter_context(nc.semaphore(f"{nm}_meta_dve"))
        ready = s.enter_context(nc.semaphore(f"{nm}_meta_vals"))
        turned = s.enter_context(nc.semaphore(f"{nm}_meta_turned"))
        with nc.Block() as block:
            @block.sync
            def _(sp):
                rows = g.chunks * P
                sp.dma_start(raw[:, :, :, :].rearrange("p g l f -> p g (l f)"),
                             meta[1:1 + rows, :].rearrange("(g p l) f -> p g (l f)", g=4, l=P)).then_inc(loaded, 16)
                before = meta[0:rows, :].rearrange("(g p l) f -> p g l f", g=4, l=P)[:, :, 0, 2:3]
                after = meta[2:2 + rows, :].rearrange("(g p l) f -> p g l f", g=4, l=P)[:, :, P - 1, 2:3]
                sp.dma_start(edge[:, :, 0:1], before, allow_slow_non_contiguous=True).then_inc(loaded, 16)
                sp.dma_start(edge[:, :, 1:2], after, allow_slow_non_contiguous=True).then_inc(loaded, 16)

            @block.vector
            def _(v):
                step = Steps(nc, v, dve)
                v.wait_ge(loaded, 48)
                for k, field in enumerate((0, 1, 3)):
                    nc.vector.tensor_copy(vals[:, k, :, :], raw[:, :, :, field]).then_inc(ready, 1)
                nc.vector.tensor_copy(key[:, :, 0:1], edge[:, :, 0:1])
                nc.vector.tensor_copy(key[:, :, P + 1:P + 2], edge[:, :, 1:2])
                step.link(nc.vector.tensor_copy(key[:, :, 1:P + 1], raw[:, :, :, 2]))
                for shift, out in ((0, g.reset_fwd), (2, g.reset_bwd)):
                    step.link(nc.vector.tensor_tensor(out[:, :, :], key[:, :, 1:P + 1], key[:, :, shift:shift + P],
                                                      ALU.is_equal))
                    step.link(nc.vector.tensor_scalar(out[:, :, :], out[:, :, :], -NEG, NEG, ALU.mult, ALU.add))
                step.link(nc.vector.tensor_scalar(g.is_last[:, :, :], g.reset_bwd[:, :, :], 0.0, None, ALU.is_lt))
                v.wait_ge(turned, 3)
                nc.vector.tensor_copy(g.src[:, :], psB[:, 0, 0:4 * CP])
                nc.vector.tensor_copy(g.lane[:, :], psB[:, 1, 0:4 * CP])
                if g.type is not None:
                    nc.vector.tensor_copy(g.type[:, :], psB[:, 2, 0:4 * CP])

            @block.tensor
            def _(pe):
                for k in range(3):
                    pe.wait_ge(ready, k + 1)
                    for q in range(4):
                        last = nc.tensor.transpose(psB[:, k, q * CP:(q + 1) * CP], vals[:, k, q, :],
                                                   c.ident[0:CP, 0:CP])
                    last.then_inc(turned, 1)


class Holder:
    pass


def open_graph(nc, ctx, g, typed):
    def sb(name, shape, dt):
        return ctx.enter_context(nc.sbuf_tensor(f"{g.name}_{name}", shape, dt))
    g.tile_of = sb("tile_of", [1, g.chunks], I32)
    g.src = sb("src_col", [P, g.chunks], I32)
    g.lane = sb("lane_col", [P, g.chunks], F32)
    g.type = sb("type_col", [P, g.chunks], F32) if typed else None
    g.reset_fwd = sb("reset_fwd", [g.cp, 4, P], F32)
    g.reset_bwd = sb("reset_bwd", [g.cp, 4, P], F32)
    g.is_last = sb("is_last", [g.cp, 4, P], F32)


def open_constants(nc, ctx, most_chunks):
    c = Holder()
    c.ctx = ctx
    def sb(name, shape, dt):
        return ctx.enter_context(nc.sbuf_tensor(name, shape, dt))
    c.iota = sb("iota", [P, P], F32)
    c.iota_chunk = sb("iota_chunk", [1, most_chunks], F32)
    c.ones = sb("ones", [P, P], F32)
    c.zeros = sb("zeros", [P, 512], F32)
    c.ident = sb("ident", [P, P], F32)
    c.identb = sb("identb", [P, P], BF16)
    c.below = sb("below", [P, P], F32)
    c.above = sb("above", [P, P], F32)
    return c


def ring_loop(eng, count, body, peel_last=False):
    rounds = count // RING
    for b in range(RING):
        body(b, b)
    with eng.Fori(1, rounds - 1 if peel_last else rounds, 1) as j:
        for b in range(RING):
            body(RING * j + b, b)
    if peel_last:
        for b in range(RING):
            body(RING * (rounds - 1) + b, b)


def wait_after(eng, sem, value):
    if not (isinstance(value, int) and value <= 0):
        eng.wait_ge(sem, value)


def round_of(q, b):
    return 16 // RING * (q - b)


def tile_registers(nc, engine, g, q):
    _, tiles = nc.values_load_multi_w_load_instructions(
        g.tile_of[0:1, bass.ds(q * QUAD, QUAD)], engines=(engine,), min_val=0, max_val=g.tiles - 1,
        skip_runtime_bounds_check_because="sort_edges counts tiles that start before a chunk, less one")
    return tiles


def gather_scores(nc, c, g, name, table, spill, node_parts, NV, heads, width, store, relation=None):
    K = QUAD
    quads = g.chunks // K
    row = table.shape[1]
    nodes_flat = node_parts[:, :, :, :].rearrange("p t a n -> p (t a n)")
    R, C = (0, 0) if relation is None else (relation.shape[0], relation.shape[2])
    spilled_cols = slice(0, width) if relation is None else slice(row - width, row)
    EB = -(-K * NV // 512)
    per_bank = K // EB
    with ExitStack() as s:
        def sb(n, shape, dt):
            return s.enter_context(nc.sbuf_tensor(f"{name}_{n}", shape, dt))

        def sem(n):
            return s.enter_context(nc.semaphore(f"{name}_{n}"))

        slot = sb("slot", [P, RING, K], I32)
        rows = sb("rows", [P, RING, K, row], F32)
        onehot = sb("onehot", [P, 2, K, P], BF16)
        onehotT = sb("onehotT", [P, 2, K, P], BF16)
        psT = s.enter_context(nc.psum_tensor(f"{name}_psT", [P, 2, 1024], BF16))
        psE = s.enter_context(nc.psum_tensor(f"{name}_psE", [P, 2, EB, 512], F32))
        if R:
            kind = sb("kind", [P, 2, K, R], BF16)
            kindT = sb("kindT", [R, 2, K, P], BF16)
            psR = s.enter_context(nc.psum_tensor(f"{name}_psR", [P, 2, 512], F32))
            prod = sb("prod", [P, 2, K, D], F32)
        listed = sem("listed")
        ready = sem("ready")
        gathered = lasting(nc, c, f"{name}_gathered", RING)
        spilled = [sem(f"spilled{b}") for b in range(RING)]
        turned = sem("turned")
        copied = sem("copied")
        spread = sem("spread")
        used = sem("used")
        passed = sem("passed")
        chain = sem("chain")
        with nc.Block() as block:
            @block.vector
            def _(v):
                def list_sources(q, b):
                    nc.vector.tensor_copy(slot[:, b, :], g.src[:, bass.ds(q * K, K)]).then_inc(listed, 1)

                def prepare(q, h):
                    col = bass.ds(q * K, K)
                    if R:
                        nc.vector.tensor_tensor(
                            kind[:, h, :, :], c.iota[:, 0:R].unsqueeze(1).broadcast_to([P, K, R]),
                            g.type[:, col].unsqueeze(2).broadcast_to([P, K, R]), ALU.is_equal)
                    nc.vector.tensor_tensor(
                        onehot[:, h, :, :], c.iota[:, :].unsqueeze(1).broadcast_to([P, K, P]),
                        g.lane[:, col].unsqueeze(2).broadcast_to([P, K, P]), ALU.is_equal).then_inc(ready, 1)

                def use(q, b):
                    h = b % 2
                    v.wait_ge(gathered[b], K * (round_of(q, b) + 16))
                    v.wait_ge(spread, q + 1)
                    if R:
                        key = rows[:, b, :, 0:D].rearrange("p k (h d) -> p k h d", h=heads)
                        for k in range(K):
                            nc.vector.tensor_tensor(
                                prod[:, h, k, :].rearrange("p (h d) -> p h d", h=heads), key[:, k, :, :],
                                psR[:, h, k * R:k * R + C].unsqueeze(1).broadcast_to([P, heads, C]),
                                ALU.add).then_inc(chain, 1)
                        for n in range(EB):
                            ks = slice(n * per_bank, (n + 1) * per_bank)
                            v.wait_ge(chain, (K + EB) * q + K + n)
                            nc.vector.tensor_tensor(
                                prod[:, h, ks, :], prod[:, h, ks, :],
                                psE[:, h, n, 0:per_bank * D].rearrange("p (k n) -> p k n", k=per_bank),
                                ALU.mult).then_inc(chain, 1)
                        v.wait_ge(chain, (K + EB) * (q + 1))
                        nc.vector.tensor_reduce(
                            store[:, bass.ds(q * K, K), 0:heads],
                            prod[:, h, :, :].rearrange("p k (h d) -> p k h d", h=heads), AX.X,
                            ALU.add).then_inc(used, 1)
                    else:
                        vals = psE[:, h, 0, 0:K * NV].rearrange("p (k n) -> p k n", k=K)
                        col = bass.ds(q * K, K)
                        nc.vector.tensor_tensor(store[:, col, 0:heads], rows[:, b, :, width:width + heads],
                                                vals[:, :, 0:heads], ALU.add)
                        nc.vector.tensor_copy(store[:, col, heads:2 * heads], vals[:, :, heads:2 * heads]).then_inc(used, 1)

                for b in range(RING):
                    list_sources(b, b)
                prepare(0, 0)
                prepare(1, 1)
                with v.Fori(0, quads // RING - 1, 1) as j:
                    for b in range(RING):
                        q = RING * j + b
                        use(q, b)
                        list_sources(q + RING, b)
                        prepare(q + 2, b % 2)
                for b in range(RING):
                    q = quads - RING + b
                    use(q, b)
                    if b < RING - 2:
                        prepare(q + 2, b % 2)

            @block.gpsimd
            def _(pool):
                def body(q, b):
                    pool.wait_ge(listed, q + 1)
                    wait_after(pool, used, q + 1 - RING)
                    wait_after(pool, spilled[b], round_of(q, b))
                    pool.sem_inc(passed, 1)
                    for k in range(K):
                        nc.gpsimd.indirect_dma_start(
                            out=rows[:, b, k, :], out_offset=None, in_=table[:, :],
                            in_offset=bass.IndirectOffsetOnAxis(ap=slot[:, b, k:k + 1], axis=0)
                        ).then_inc(gathered[b], 16)
                ring_loop(pool, quads, body)

            @block.sync
            def _(sp):
                def body(q, b):
                    sp.wait_ge(gathered[b], K * (round_of(q, b) + 16))
                    sp.dma_start(spill[bass.ds(q, 1), :, :].rearrange("a p n -> (a p) n"),
                                 rows[:, b, :, spilled_cols]).then_inc(spilled[b], 16)
                ring_loop(sp, quads, body)
                for b in range(RING):
                    sp.wait_ge(spilled[b], 16 * quads // RING)

            @block.tensor
            def _(pe):
                def turn(q, h):
                    pe.wait_ge(ready, q + 1)
                    wait_after(pe, copied, q - 1)
                    for k in range(K):
                        last = nc.tensor.transpose(psT[:, h, k * P:(k + 1) * P], onehot[:, h, k, :], c.identb[:, :])
                        if R:
                            last = nc.tensor.transpose(psT[0:R, h, (K + k) * P:(K + k + 1) * P], kind[:, h, k, :],
                                                       c.identb[:, :])
                    last.then_inc(turned, 1)

                def expand(q, h):
                    tiles = tile_registers(nc, mybir.EngineType.PE, g, q)
                    pe.wait_ge(copied, q + 1)
                    wait_after(pe, used, q - 1)
                    for k in range(K):
                        n, i = k // per_bank, k % per_bank
                        for part in range(PARTS):
                            last = nc.tensor.matmul(psE[:, h, n, i * NV:(i + 1) * NV], onehotT[:, h, k, :],
                                                    nodes_flat[:, bass.ds(tiles[k] * (PARTS * NV) + part * NV, NV)],
                                                    start=(part == 0), stop=(part == PARTS - 1))
                        for part in range(PARTS if R else 0):
                            last = nc.tensor.matmul(psR[:, h, k * R:k * R + C], kindT[:, h, k, :], relation[:, part, :],
                                                    start=(part == 0), stop=(part == PARTS - 1))
                    last.then_inc(spread, 1)

                turn(0, 0)
                turn(1, 1)

                def body(q, b):
                    expand(q, b % 2)
                    if not (isinstance(q, int) and q + 2 >= quads):
                        turn(q + 2, b % 2)
                ring_loop(pe, quads, body, peel_last=True)

            @block.scalar
            def _(act):
                def body(q, b):
                    h = b % 2
                    act.wait_ge(turned, q + 1)
                    wait_after(act, spread, q - 1)
                    if R:
                        nc.scalar.activation(kindT[:, h, :, :],
                                             psT[0:R, h, K * P:2 * K * P].rearrange("p (k l) -> p k l", k=K), ACT.Copy)
                    nc.scalar.activation(onehotT[:, h, :, :],
                                         psT[:, h, 0:K * P].rearrange("p (k l) -> p k l", k=K),
                                         ACT.Copy).then_inc(copied, 1)
                ring_loop(act, quads, body)


def split_parts(step, values, parts, rest):
    nc = step.nc
    for k in range(PARTS):
        left = values if k == 0 else rest
        step.link(nc.vector.tensor_copy(parts[k], left))
        if k < PARTS - 1:
            step.link(nc.vector.tensor_tensor(rest, left, parts[k], ALU.subtract))


def edge_softmax(nc, c, g, name, heads, store, own, scale):
    CP, CH, H = g.cp, g.chunks, heads
    W = store.shape[2]
    assert W == (2 * H if own else H) + 1
    with ExitStack() as s:
        def sb(n, shape, dt=F32):
            return s.enter_context(nc.sbuf_tensor(f"{name}_{n}", shape, dt))

        def sem(n):
            return s.enter_context(nc.semaphore(f"{name}_{n}"))

        val = sb("val", [CP, H, 4, P])
        loop = sb("loop", [CP, H, 4, P]) if own else None
        fwd = sb("fwd", [CP, H, 4, P])
        bwd = sb("bwd", [CP, H, 4, P])
        reset = sb("reset", [CP, H, 4, P])
        link = sb("link", [CP, 2, 4])
        links = sb("links", [CP, 2, H, 4])
        ends = sb("ends", [H, 2, CH])
        linkT = sb("linkT", [H, 2, CH])
        state = sb("state", [H, 2, CH + 1])
        carry = sb("carry", [CP, 2, 4, H])
        kept = sb("kept", [CP, H, 4])
        into = sb("into", [CP, H, 4])
        ps = s.enter_context(nc.psum_tensor(f"{name}_ps", [P, 8, 512], F32))
        dve = sem("dve")
        scored = sem("scored")
        turned = sem("turned")
        copied = sem("copied")
        tails = sem("tails")
        tailsT = sem("tailsT")
        stated = sem("stated")
        carried = sem("carried")
        shifted = sem("shifted")
        weighted = sem("weighted")
        back = sem("back")
        stored = sem("stored")
        groups = [(0, h) for h in range(H)] + ([(1, h) for h in range(H)] if own else [])
        with nc.Block() as block:
            @block.vector
            def _(v):
                step = Steps(nc, v, dve)
                if own:
                    flat = store[:, :, 0:H]
                    nc.vector.scalar_tensor_tensor(flat, flat, SLOPE, flat, ALU.mult, ALU.max).then_inc(scored, 1)
                else:
                    nc.vector.tensor_scalar(store[:, :, 0:H], store[:, :, 0:H], scale, None, ALU.mult).then_inc(scored, 1)
                nc.vector.tensor_reduce(link[:, 0, :], g.reset_fwd[:, :, :], AX.X, ALU.min)
                step.link(nc.vector.tensor_reduce(link[:, 1, :], g.reset_bwd[:, :, :], AX.X, ALU.min))
                for h in range(H):
                    nc.vector.tensor_copy(links[:, :, h, :], link[:, :, :])
                step.link(nc.vector.memset(state[:, :, :], NEG))
                v.wait_ge(copied, len(groups))
                val_f = val[:, :, :, :].rearrange("p h g l -> p (h g l)")
                reset_f = reset[:, :, :, :].rearrange("p h g l -> p (h g l)")
                fwd_f = fwd[:, :, :, :].rearrange("p h g l -> p (h g l)")
                bwd_f = bwd[:, :, :, :].rearrange("p h g l -> p (h g l)")

                def set_reset(source, edge):
                    for h in range(H):
                        last = nc.vector.tensor_copy(reset[:, h, :, :], source[:, :, :])
                        step.mark(last)
                    v.wait_ge(dve, step.n)
                    step.link(nc.vector.memset(reset[:, :, :, edge:edge + 1], NEG))

                def scan(out, backward):
                    a = (slice(None), slice(None, None, -1)) if backward else (slice(None), slice(None))
                    step.link(nc.vector.tensor_tensor_scan(out[a], reset_f[a], val_f[a], NEG, ALU.add, ALU.max))

                def with_carry(out, side, source, edge, backward):
                    step.link(nc.vector.tensor_tensor(
                        into[:, :, :], carry[:, side, :, :].rearrange("p g h -> p h g"),
                        source[:, :, edge].unsqueeze(1).broadcast_to([CP, H, 4]), ALU.add))
                    step.link(nc.vector.tensor_copy(kept[:, :, :], val[:, :, :, edge]))
                    step.link(nc.vector.tensor_tensor(val[:, :, :, edge], kept[:, :, :], into[:, :, :], ALU.max))
                    scan(out, backward)
                    step.link(nc.vector.tensor_copy(val[:, :, :, edge], kept[:, :, :]))

                set_reset(g.reset_bwd, P - 1)
                scan(bwd_f, True)
                set_reset(g.reset_fwd, 0)
                scan(fwd_f, False)
                v.sem_inc(tails, 1)
                v.wait_ge(tailsT, 1)
                for side in range(2):
                    nc.vector.tensor_copy(ends[:, side, :], ps[0:H, side, 0:CH])
                    step.link(nc.vector.tensor_copy(linkT[:, side, :], ps[0:H, 2 + side, 0:CH]))
                step.link(nc.vector.tensor_tensor_scan(state[:, 0, 1:], linkT[:, 0, :], ends[:, 0, :], NEG,
                                                       ALU.add, ALU.max))
                step.link(nc.vector.tensor_tensor_scan(state[:, 1, 0:CH][:, ::-1], linkT[:, 1, ::-1],
                                                       ends[:, 1, ::-1], NEG, ALU.add, ALU.max))
                v.sem_inc(stated, 1)
                v.wait_ge(carried, 1)
                for side in range(2):
                    step.link(nc.vector.tensor_copy(carry[:, side, :, :],
                                                    ps[0:CP, 4 + side, 0:4 * H].rearrange("p (g h) -> p g h", g=4)))
                with_carry(fwd_f, 0, g.reset_fwd, 0, False)
                set_reset(g.reset_bwd, P - 1)
                with_carry(bwd_f, 1, g.reset_bwd, P - 1, True)
                step.link(nc.vector.tensor_tensor(fwd_f, fwd_f, bwd_f, ALU.max))
                if own:
                    loop_f = loop[:, :, :, :].rearrange("p h g l -> p (h g l)")
                    step.link(nc.vector.tensor_tensor(fwd_f, fwd_f, loop_f, ALU.max))
                nc.vector.tensor_tensor(val_f, val_f, fwd_f, ALU.subtract).then_inc(shifted, 1)
                if own:
                    nc.vector.tensor_tensor(loop_f, loop_f, fwd_f, ALU.subtract).then_inc(shifted, 1)
                    v.wait_ge(weighted, 2)
                    nc.vector.tensor_tensor(
                        loop[:, :, :, :], loop[:, :, :, :],
                        g.is_last[:, :, :].unsqueeze(1).broadcast_to([CP, H, 4, P]), ALU.mult).then_inc(shifted, 1)
                for n in range(len(groups) + 1):
                    v.wait_ge(back, n + 1)
                    nc.vector.tensor_copy(store[:, :, n], ps[:, n % 8, 0:CH]).then_inc(stored, 1)

            @block.tensor
            def _(pe):
                pe.wait_ge(scored, 1)
                for n, (side, h) in enumerate(groups):
                    if n >= 8:
                        pe.wait_ge(copied, n - 7)
                    for q in range(4):
                        last = nc.tensor.transpose(ps[0:CP, n % 8, q * P:(q + 1) * P],
                                                   store[:, q * CP:(q + 1) * CP, side * H + h], c.ident[:, :])
                    last.then_inc(turned, 1)
                pe.wait_ge(tails, 1)
                pe.wait_ge(copied, len(groups))
                for q in range(4):
                    sl = slice(q * CP, (q + 1) * CP)
                    nc.tensor.transpose(ps[0:H, 0, sl], fwd[:, :, q, P - 1], c.ident[0:CP, 0:CP])
                    nc.tensor.transpose(ps[0:H, 1, sl], bwd[:, :, q, 0], c.ident[0:CP, 0:CP])
                    for side in range(2):
                        last = nc.tensor.transpose(ps[0:H, 2 + side, sl], links[:, side, :, q], c.ident[0:CP, 0:CP])
                last.then_inc(tailsT, 1)
                pe.wait_ge(stated, 1)
                for q in range(4):
                    for side in range(2):
                        last = nc.tensor.transpose(ps[0:CP, 4 + side, q * H:(q + 1) * H],
                                                   state[:, side, q * CP + side:(q + 1) * CP + side],
                                                   c.ident[0:H, 0:H])
                last.then_inc(carried, 1)
                for n in range(len(groups) + 1):
                    if n < len(groups):
                        side, h = groups[n]
                        source = (val, loop)[side][:, h, :, :]
                        if side == 0:
                            pe.wait_ge(weighted, 1)
                        else:
                            pe.wait_ge(shifted, 3)
                    else:
                        source = g.is_last[:, :, :]
                    if n >= 8:
                        pe.wait_ge(stored, n - 7)
                    for q in range(4):
                        last = nc.tensor.transpose(ps[:, n % 8, q * CP:(q + 1) * CP], source[:, q, :],
                                                   c.ident[0:CP, 0:CP])
                    last.then_inc(back, 1)

            @block.scalar
            def _(act):
                for n, (side, h) in enumerate(groups):
                    act.wait_ge(turned, n + 1)
                    nc.scalar.activation((val, loop)[side][:, h, :, :],
                                         ps[0:CP, n % 8, :].rearrange("p (g l) -> p g l", g=4),
                                         ACT.Copy).then_inc(copied, 1)
                act.wait_ge(shifted, 1)
                nc.scalar.activation(val[:, :, :, :], val[:, :, :, :], ACT.Exp).then_inc(weighted, 1)
                if own:
                    act.wait_ge(shifted, 2)
                    nc.scalar.activation(loop[:, :, :, :], loop[:, :, :, :], ACT.Exp).then_inc(weighted, 1)


def aggregate(nc, c, g, name, heads, width, spill, store, agg):
    K = QUAD
    quads = g.chunks // K
    W = store.shape[2]
    AW = width + W
    BANKS = 8
    store_flat = store[:, :, :].rearrange("p c w -> p (c w)")
    agg_flat = agg[:, :, :].rearrange("p t w -> p (t w)")
    with ExitStack() as s:
        def sb(n, shape, dt=F32):
            return s.enter_context(nc.sbuf_tensor(f"{name}_{n}", shape, dt))

        def sem(n):
            return s.enter_context(nc.semaphore(f"{name}_{n}"))

        rows = sb("rows", [P, RING, K, width])
        part = sb("part", [P, RING, K, AW])
        onehot = sb("onehot", [P, RING, K, P])
        ps = s.enter_context(nc.psum_tensor(f"{name}_psA", [P, BANKS, 512], F32))
        loaded = [sem(f"loaded{b}") for b in range(RING)]
        weighed = sem("weighed")
        extended = sem("extended")
        ready = sem("ready")
        summed = sem("summed")
        added = sem("added")
        zeroed = sem("zeroed")
        with nc.Block() as block:
            @block.sync
            def _(sp):
                def body(q, b):
                    wait_after(sp, weighed, q + 1 - RING)
                    sp.dma_start(rows[:, b, :, :].rearrange("p k n -> p (k n)"),
                                 spill[bass.ds(q, 1), :, :].rearrange("a p n -> (a p) n")).then_inc(loaded[b], 16)
                ring_loop(sp, quads, body)

            @block.gpsimd
            def _(pool):
                def body(q, b):
                    pool.wait_ge(loaded[b], round_of(q, b) + 16)
                    wait_after(pool, summed, K * (q + 1 - RING))
                    for k in range(K):
                        last = nc.gpsimd.tensor_tensor(
                            part[:, b, k, 0:width].rearrange("p (h n) -> p h n", h=heads),
                            rows[:, b, k, :].rearrange("p (h n) -> p h n", h=heads),
                            store_flat[:, bass.ds((q * K + k) * W, heads)].unsqueeze(2)
                            .broadcast_to([P, heads, width // heads]), ALU.mult)
                    last.then_inc(weighed, 1)
                ring_loop(pool, quads, body)

            @block.scalar
            def _(act):
                def body(q, b):
                    wait_after(act, summed, K * (q + 1 - RING))
                    nc.scalar.activation(part[:, b, :, width:AW], store[:, bass.ds(q * K, K), :],
                                         ACT.Copy).then_inc(extended, 1)
                ring_loop(act, quads, body)

            @block.tensor
            def _(pe):
                def body(q, b):
                    pe.wait_ge(weighed, q + 1)
                    pe.wait_ge(extended, q + 1)
                    for k in range(K):
                        pe.wait_ge(ready, K * q + k + 1)
                        wait_after(pe, added, K * q + k + 1 - BANKS)
                        nc.tensor.matmul(ps[:, (K * b + k) % BANKS, 0:AW], onehot[:, b, k, :], part[:, b, k, :],
                                         start=True, stop=True).then_inc(summed, 1)
                ring_loop(pe, quads, body)

            @block.vector
            def _(v):
                nc.vector.memset(agg[:, :, :], 0.0).then_inc(zeroed, 1)
                v.wait_ge(zeroed, 1)

                def prepare(chunk, b, k):
                    nc.vector.tensor_scalar(onehot[:, b, k, :], c.iota[:, :], g.lane[:, bass.ds(chunk, 1)], None,
                                            ALU.is_equal).then_inc(ready, 1)

                def body(q, b):
                    tiles = tile_registers(nc, mybir.EngineType.DVE, g, q)
                    for k in range(K):
                        v.wait_ge(summed, q * K + k + 1)
                        wait_after(v, added, q * K + k)
                        place = agg_flat[:, bass.ds(tiles[k] * AW, AW)]
                        nc.vector.tensor_tensor(place, place, ps[:, (K * b + k) % BANKS, 0:AW], ALU.add).then_inc(added, 1)
                        if not (isinstance(q, int) and q + RING - 1 >= quads):
                            prepare((q + RING - 1) * K + k, (b + RING - 1) % RING, k)

                for b in range(RING - 1):
                    for k in range(K):
                        prepare(b * K + k, b, k)
                ring_loop(v, quads, body, peel_last=True)


def load_rows(sp, dst, src, sem):
    sp.dma_start(dst[:, 0:NT - 1, :], src[0:(NT - 1) * P, :].rearrange("(t p) d -> p t d", p=P)).then_inc(sem, 16)
    sp.dma_start(dst[0:LAST, NT - 1, :], src[(NT - 1) * P:N, :]).then_inc(sem, 16)


def load_x(nc, x_d, xs):
    with ExitStack() as s:
        zeroed = s.enter_context(nc.semaphore("x_zeroed"))
        loaded = s.enter_context(nc.semaphore("x_loaded"))
        with nc.Block() as block:
            @block.vector
            def _(v):
                nc.vector.memset(xs[:, NT - 1, :], 0.0).then_inc(zeroed, 1)

            @block.sync
            def _(sp):
                sp.wait_ge(zeroed, 1)
                load_rows(sp, xs, x_d, loaded)
                sp.wait_ge(loaded, 32)


def store_x(nc, xs, out_d):
    with ExitStack() as s:
        stored = s.enter_context(nc.semaphore("out_stored"))
        with nc.Block() as block:
            @block.sync
            def _(sp):
                sp.dma_start(out_d[0:(NT - 1) * P, :].rearrange("(t p) d -> p t d", p=P),
                             xs[:, 0:NT - 1, :]).then_inc(stored, 16)
                sp.dma_start(out_d[(NT - 1) * P:N, :], xs[0:LAST, NT - 1, :]).then_inc(stored, 16)
                sp.wait_ge(stored, 32)


def inverse_root(nc, v, step, x, root, asked, rooted):
    v.sem_inc(asked, 1)
    v.wait_ge(rooted, 1)
    step.link(nc.vector.reciprocal(root, root))
    step.link(nc.vector.tensor_tensor(x, x, root, ALU.mult))
    step.link(nc.vector.tensor_tensor(x, x, root, ALU.mult))
    step.link(nc.vector.tensor_scalar(x, x, -0.5, 1.5, ALU.mult, ALU.add))
    step.link(nc.vector.tensor_tensor(root, root, x, ALU.mult))


def take_root(nc, act, x, root, asked, rooted):
    act.wait_ge(asked, 1)
    nc.scalar.activation(root, x, ACT.Sqrt).then_inc(rooted, 1)


def row_statistics(nc, v, step, x, stats, moments, rstd, asked, rooted):
    for t in range(NT):
        step.mark(nc.vector.bn_stats(stats[:, t, :], x[:, t, :]))
    v.wait_ge(step.sem, step.n)
    for t in range(NT):
        step.mark(nc.vector.bn_aggr(moments[:, t, :], stats[:, t, :]))
    v.wait_ge(step.sem, step.n)
    step.link(nc.vector.tensor_scalar(moments[:, :, 1], moments[:, :, 1], LN_EPS, None, ALU.add))
    inverse_root(nc, v, step, moments[:, :, 1], rstd[:, :], asked, rooted)


def turn_rows(nc, c, name, x, xT, norm, normed=None, shift=None):
    with ExitStack() as s:
        def sb(n, shape, dt=F32):
            return s.enter_context(nc.sbuf_tensor(f"{name}_{n}", shape, dt))

        def sem(n):
            return s.enter_context(nc.semaphore(f"{name}_{n}"))

        ps = s.enter_context(nc.psum_tensor(f"{name}_psX", [P, 8, 512], F32))
        dve, ready, turned, copied = sem("dve"), sem("ready"), sem("turned"), sem("copied")
        asked, rooted = sem("asked"), sem("rooted")
        src = x
        if norm:
            stats = sb("stats", [P, NT, 6])
            moments = sb("moments", [P, NT, 2])
            rstd = sb("rstd", [P, NT])
            src = normed if normed is not None else sb("normed", [P, NT, D])
        groups = [(t0, min(4, NT - t0)) for t0 in range(0, NT, 4)]
        with nc.Block() as block:
            @block.vector
            def _(v):
                step = Steps(nc, v, dve)
                if norm:
                    row_statistics(nc, v, step, x, stats, moments, rstd, asked, rooted)
                    for t in range(NT):
                        nc.vector.tensor_scalar(src[:, t, :], x[:, t, :], moments[:, t, 0:1], rstd[:, t:t + 1],
                                                ALU.subtract, ALU.mult).then_inc(ready, 1)

            @block.tensor
            def _(pe):
                n = 0
                for t0, w in groups:
                    if norm:
                        pe.wait_ge(ready, t0 + w)
                    for k in range(KD):
                        wait_after(pe, copied, n - 7)
                        for i in range(w):
                            last = nc.tensor.transpose(ps[:, n % 8, i * P:(i + 1) * P],
                                                       src[:, t0 + i, k * P:(k + 1) * P], c.ident[:, :])
                        last.then_inc(turned, 1)
                        n += 1

            @block.scalar
            def _(act):
                if norm:
                    take_root(nc, act, moments[:, :, 1], rstd[:, :], asked, rooted)
                n = 0
                for t0, w in groups:
                    for k in range(KD):
                        act.wait_ge(turned, n + 1)
                        out = xT[:, k, t0 * P:(t0 + w) * P]
                        if shift is None:
                            nc.scalar.activation(out, ps[:, n % 8, 0:w * P], ACT.Copy).then_inc(copied, 1)
                        else:
                            nc.scalar.activation(out, ps[:, n % 8, 0:w * P], ACT.Identity,
                                                 bias=shift[:, k:k + 1]).then_inc(copied, 1)
                        n += 1


def project(nc, c, name, xT, weights, bias, out, add=None, table=None):
    M = weights.shape[2]
    with ExitStack() as s:
        def sem(n):
            return s.enter_context(nc.semaphore(f"{name}_{n}"))

        ps = s.enter_context(nc.psum_tensor(f"{name}_psP", [P, 8, 512], F32))
        made, taken, chain, sent = sem("made"), sem("taken"), sem("chain"), sem("sent")
        with nc.Block() as block:
            @block.tensor
            def _(pe):
                for t in range(NT):
                    wait_after(pe, taken, t - 7)
                    for k in range(KD):
                        last = nc.tensor.matmul(ps[:, t % 8, 0:M], xT[:, k, t * P:(t + 1) * P], weights[:, k, :],
                                                start=(k == 0), stop=(k == KD - 1))
                    last.then_inc(made, 1)

            @block.vector
            def _(v):
                step = Steps(nc, v, chain)
                for t in range(NT):
                    v.wait_ge(made, t + 1)
                    got = ps[:, t % 8, 0:M]
                    if bias is None:
                        last = nc.vector.tensor_copy(out[:, t, :], got)
                    else:
                        last = nc.vector.tensor_tensor(out[:, t, :], got, bias[:, :], ALU.add)
                    if add is not None:
                        step.link(last)
                        last = nc.vector.tensor_tensor(out[:, t, :], out[:, t, :], add[:, t, :], ALU.add)
                    last.then_inc(taken, 1)

            if table is not None:
                @block.sync
                def _(sp):
                    w = table.shape[1]
                    sp.wait_ge(taken, NT)
                    sp.dma_start(table.rearrange("(t p) n -> p t n", p=P), out[:, :, 0:w]).then_inc(sent, 16)
                    sp.wait_ge(sent, 16)


def load_weights(nc, name, loads):
    with ExitStack() as s:
        loaded = s.enter_context(nc.semaphore(f"{name}_loaded"))
        with nc.Block() as block:
            @block.sync
            def _(sp):
                for dst, src in loads:
                    sp.dma_start(dst, src, allow_slow_non_contiguous=True).then_inc(loaded, 16)
                sp.wait_ge(loaded, 16 * len(loads))


def by_halves(w):
    return w.rearrange("(k p) n -> p k n", p=P)


def spread_row(v):
    n = v.shape[0]
    return v.rearrange("(a n) -> a n", a=1).broadcast_to([P, n])


def graph_attention(nc, c, g, name, xT, W, att_src, att_dst, bias, heads, scratch, out, load=None):
    HC = W.shape[1]
    H = heads
    C = HC // H
    with ExitStack() as s:
        def sb(n, shape, dt=F32):
            return s.enter_context(nc.sbuf_tensor(f"{name}_{n}", shape, dt))

        def sem(n):
            return s.enter_context(nc.semaphore(f"{name}_{n}"))

        rows = sb("noderows", [P, NT, HC + 2 * H])
        node_vals = sb("node_vals", [P, NT, 2 * H])
        node_parts = sb("node_parts", [P, NT, PARTS, 2 * H], BF16)
        store = sb("store", [P, g.chunks, 2 * H + 1])
        bias_row = sb("bias_row", [P, HC])
        table = scratch["table"][0:NP * (HC + H)].rearrange("(n w) -> n w", w=HC + H)
        spill = scratch["spill"][0:g.chunks * P * HC].rearrange("(q p n) -> q p n", p=P, n=QUAD * HC)
        with ExitStack() as w:
            weights = w.enter_context(nc.sbuf_tensor(f"{name}_weights", [P, KD, HC + 2 * H], F32))
            att = w.enter_context(nc.sbuf_tensor(f"{name}_att", [P, 2, HC], F32))
            prod = w.enter_context(nc.sbuf_tensor(f"{name}_prod", [P, 2 * KD, HC], F32))
            if callable(xT):
                fill_xT, xT = xT, w.enter_context(nc.sbuf_tensor(f"{name}_xT", [P, KD, NP], F32))
                fill_xT(xT)
            load_weights(nc, f"{name}_w", [
                (weights[:, :, 0:HC], by_halves(W)),
                (att[:, 0, :], spread_row(att_src.rearrange("h c -> (h c)"))),
                (att[:, 1, :], spread_row(att_dst.rearrange("h c -> (h c)"))),
                (bias_row[:, :], spread_row(bias))])
            fold = sem("fold")
            with nc.Block() as block:
                @block.vector
                def _(v):
                    step = Steps(nc, v, fold)
                    for k in range(KD):
                        for a in range(2):
                            n = 2 * k + a
                            step.link(nc.vector.tensor_tensor(prod[:, n, :], weights[:, k, 0:HC], att[:, a, :], ALU.mult))
                            step.mark(nc.vector.tensor_reduce(
                                weights[:, k, HC + a * H:HC + (a + 1) * H],
                                prod[:, n, :].rearrange("p (h c) -> p h c", h=H), AX.X, ALU.add))
            project(nc, c, f"{name}_h", xT, weights, None, rows, table=table)
        own = sem("own")
        with nc.Block() as block:
            @block.vector
            def _(v):
                step = Steps(nc, v, own)
                s_part, d_part = rows[:, :, HC:HC + H], rows[:, :, HC + H:HC + 2 * H]
                nc.vector.tensor_copy(node_vals[:, :, 0:H], d_part)
                step.link(nc.vector.tensor_tensor(node_vals[:, :, H:2 * H], s_part, d_part, ALU.add))
                step.link(nc.vector.scalar_tensor_tensor(node_vals[:, :, H:2 * H], node_vals[:, :, H:2 * H], SLOPE,
                                                         node_vals[:, :, H:2 * H], ALU.mult, ALU.max))
                split_parts(step, node_vals[:, :, :], [node_parts[:, :, k, :] for k in range(PARTS)],
                            node_vals[:, :, :])
        gather_scores(nc, c, g, f"{name}_a", table, spill, node_parts, 2 * H, H, HC, store)
        edge_softmax(nc, c, g, f"{name}_b", H, store, True, 1.0)
        agg = sb("agg", [P, NT, HC + 2 * H + 1])
        aggregate(nc, c, g, f"{name}_c", H, HC, spill, store, agg)
        loops = sb("loops", [P, NT, H])
        recip = sb("recip", [P, NT, H])
        fin = sem("fin")
        with nc.Block() as block:
            @block.vector
            def _(v):
                step = Steps(nc, v, fin)
                den = agg[:, :, HC:HC + H]
                own_w = agg[:, :, HC + H:HC + 2 * H]
                has = agg[:, :, HC + 2 * H:HC + 2 * H + 1].broadcast_to([P, NT, H])
                step.link(nc.vector.tensor_tensor(loops[:, :, :], own_w, has, ALU.subtract))
                step.link(nc.vector.tensor_scalar(loops[:, :, :], loops[:, :, :], 1.0, None, ALU.add))
                step.link(nc.vector.tensor_tensor(recip[:, :, :], den, loops[:, :, :], ALU.add))
                step.link(nc.vector.tensor_scalar(recip[:, :, :], recip[:, :, :], SOFT_EPS, None, ALU.add))
                step.link(nc.vector.reciprocal(recip[:, :, :], recip[:, :, :]))

                def per_head(a):
                    return a.rearrange("p t (h c) -> p t h c", h=H)

                h_rows = per_head(rows[:, :, 0:HC])
                step.link(nc.vector.tensor_tensor(h_rows, h_rows, loops[:, :, :].unsqueeze(3).broadcast_to([P, NT, H, C]),
                                                  ALU.mult))
                step.link(nc.vector.tensor_tensor(rows[:, :, 0:HC], rows[:, :, 0:HC], agg[:, :, 0:HC], ALU.add))
                step.link(nc.vector.tensor_tensor(h_rows, h_rows, recip[:, :, :].unsqueeze(3).broadcast_to([P, NT, H, C]),
                                                  ALU.mult))
                step.link(nc.vector.tensor_tensor(rows[:, :, 0:HC], rows[:, :, 0:HC],
                                                  bias_row[:, :].unsqueeze(1).broadcast_to([P, NT, HC]), ALU.add))
                out(step, rows[:, :, 0:HC])

            if load is not None:
                @block.sync
                def _(sp):
                    load(sp)


def relation_attention(nc, c, g, w, xs, scratch):
    H = 4
    C = D // H
    with ExitStack() as s:
        def sb(n, shape, dt=F32):
            return s.enter_context(nc.sbuf_tensor(f"r_{n}", shape, dt))

        def sem(n):
            return s.enter_context(nc.semaphore(f"r_{n}"))

        normed = sb("normed", [P, NT, D])
        relation = sb("relation", [w["L1_gnn_rel_w"].shape[0], C])
        relation_parts = sb("relation_parts", [w["L1_gnn_rel_w"].shape[0], PARTS, C], BF16)
        store = sb("store", [P, g.chunks, H + 1])
        table = scratch["table"][0:NP * 2 * D].rearrange("(n w) -> n w", w=2 * D)
        spill = scratch["spill"][0:g.chunks * P * D].rearrange("(q p n) -> q p n", p=P, n=QUAD * D)
        shift = sb("shift", [P, KD])
        prep = sem("prep")
        split = sem("split")
        with ExitStack() as q:
            query = q.enter_context(nc.sbuf_tensor("r_query", [P, NT, D], F32))
            with ExitStack() as t:
                xT = t.enter_context(nc.sbuf_tensor("r_xT", [P, KD, NP], F32))
                wq = t.enter_context(nc.sbuf_tensor("r_wq", [P, KD, D], F32))
                bq = t.enter_context(nc.sbuf_tensor("r_bq", [P, D], F32))
                wkv = t.enter_context(nc.sbuf_tensor("r_wkv", [P, KD, 2 * D], F32))
                bkv = t.enter_context(nc.sbuf_tensor("r_bkv", [P, 2 * D], F32))
                kv = t.enter_context(nc.sbuf_tensor("r_kv", [P, NT, 2 * D], F32))
                load_weights(nc, "r_w", [
                    (shift[:, :], w["L1_gnn_query_emb"].rearrange("(k p) -> p k", p=P)),
                    (relation[:, :], w["L1_gnn_rel_w"]),
                    (wq[:, :, :], by_halves(w["L1_gnn_Wq"])), (bq[:, :], spread_row(w["L1_gnn_bq"])),
                    (wkv[:, :, 0:D], by_halves(w["L1_gnn_Wk"])), (wkv[:, :, D:2 * D], by_halves(w["L1_gnn_Wv"])),
                    (bkv[:, 0:D], spread_row(w["L1_gnn_bk"])), (bkv[:, D:2 * D], spread_row(w["L1_gnn_bv"]))])
                with nc.Block() as block:
                    @block.vector
                    def _(v):
                        step = Steps(nc, v, prep)
                        step.link(nc.vector.tensor_scalar(shift[:, :], shift[:, :], 0.1, None, ALU.mult))
                        step.link(nc.vector.tensor_scalar(relation[:, :], relation[:, :], 0.2, None, ALU.mult))
                turn_rows(nc, c, "r_n", xs, xT, True, normed=normed, shift=shift)
                project(nc, c, "r_q", xT, wq, bq, query)
                project(nc, c, "r_kv", xT, wkv, bkv, kv, table=table)
            query_parts = q.enter_context(nc.sbuf_tensor("r_query_parts", [P, NT, PARTS, D], BF16))
            with nc.Block() as block:
                @block.vector
                def _(v):
                    step = Steps(nc, v, split)
                    split_parts(step, query[:, :, :], [query_parts[:, :, k, :] for k in range(PARTS)], query[:, :, :])
                    split_parts(step, relation[:, :], [relation_parts[:, k, :] for k in range(PARTS)], relation[:, :])
            gather_scores(nc, c, g, "r_a", table, spill, query_parts, D, H, D, store, relation=relation_parts)
        edge_softmax(nc, c, g, "r_b", H, store, False, 1.0 / C ** 0.5)
        msgs = sb("msgs", [P, NT, D])
        mT = sb("mT", [P, KD, NP])
        wo = sb("wo", [P, KD, D])
        rows3 = sb("rows3", [P, 3, D])
        load_weights(nc, "r_o", [(wo[:, :, :], by_halves(w["L1_gnn_Wo"])), (rows3[:, 0, :], spread_row(w["L1_gnn_bo"])),
                                 (rows3[:, 1, :], spread_row(w["L1_gnn_gamma"])),
                                 (rows3[:, 2, :], spread_row(w["L1_gnn_beta"])),
                                 (msgs[:, :, :], table.rearrange("(t p) n -> p t n", p=P)[:, :, D:2 * D])])
        with ExitStack() as a:
            agg = a.enter_context(nc.sbuf_tensor("r_agg", [P, NT, D + H + 1], F32))
            aggregate(nc, c, g, "r_c", H, D, spill, store, agg)
            lone = a.enter_context(nc.sbuf_tensor("r_lone", [P, NT, 1], F32))
            recip = a.enter_context(nc.sbuf_tensor("r_recip", [P, NT, H], F32))
            fin = sem("fin")
            with nc.Block() as block:
                @block.vector
                def _(v):
                    step = Steps(nc, v, fin)
                    step.link(nc.vector.tensor_scalar(lone[:, :, :], agg[:, :, D + H:D + H + 1], -1.0, 1.0,
                                                      ALU.mult, ALU.add))
                    step.link(nc.vector.tensor_tensor(recip[:, :, :], agg[:, :, D:D + H],
                                                      lone[:, :, :].broadcast_to([P, NT, H]), ALU.add))
                    step.link(nc.vector.reciprocal(recip[:, :, :], recip[:, :, :]))
                    step.mark(nc.vector.tensor_tensor(msgs[:, :, :], msgs[:, :, :],
                                                      lone[:, :, :].broadcast_to([P, NT, D]), ALU.mult))
                    part = agg[:, :, 0:D].rearrange("p t (h c) -> p t h c", h=H)
                    step.link(nc.vector.tensor_tensor(part, part, recip[:, :, :].unsqueeze(3).broadcast_to([P, NT, H, C]),
                                                      ALU.mult))
                    step.link(nc.vector.tensor_tensor(msgs[:, :, :], msgs[:, :, :], agg[:, :, 0:D], ALU.add))
        turn_rows(nc, c, "r_m", msgs, mT, False)
        project(nc, c, "r_out", mT, wo, rows3[:, 0, :], msgs, add=normed)
        stats, moments, rstd = sb("stats", [P, NT, 6]), sb("moments", [P, NT, 2]), sb("rstd", [P, NT])
        last_norm, asked, rooted = sem("last_norm"), sem("asked"), sem("rooted")
        with nc.Block() as block:
            @block.vector
            def _(v):
                step = Steps(nc, v, last_norm)
                row_statistics(nc, v, step, msgs, stats, moments, rstd, asked, rooted)
                for t in range(NT):
                    step.mark(nc.vector.tensor_scalar(msgs[:, t, :], msgs[:, t, :], moments[:, t, 0:1],
                                                      rstd[:, t:t + 1], ALU.subtract, ALU.mult))
                v.wait_ge(last_norm, step.n)
                for row, op in ((1, ALU.mult), (2, ALU.add)):
                    step.link(nc.vector.tensor_tensor(msgs[:, :, :], msgs[:, :, :],
                                                      rows3[:, row, :].unsqueeze(1).broadcast_to([P, NT, D]), op))
                step.link(nc.vector.tensor_tensor(xs[:, :, :], xs[:, :, :], msgs[:, :, :], ALU.add))

            @block.scalar
            def _(act):
                take_root(nc, act, moments[:, :, 1], rstd[:, :], asked, rooted)


def top_two_gates(nc, c, w, xT, g, scratch, gate):
    H, E = 4, 4
    with ExitStack() as s:
        def sb(n, shape, dt=F32):
            return s.enter_context(nc.sbuf_tensor(f"t_{n}", shape, dt))

        HE = H * E
        ln = sb("ln", [P, 2, HE])
        work = sb("work", [P, NT, HE])
        col = sb("col", [P, 12, NT])
        score = sb("score", [P, NT, E])
        picks = sb("picks", [P, 2, NT, E])
        equal = sb("equal", [P, NT, E])
        sq = sb("square", [P, NT, HE])
        load_weights(nc, "t_w", [(ln[:, 0, :], spread_row(w["L0_ffn_ln_gamma"])),
                                 (ln[:, 1, :], spread_row(w["L0_ffn_ln_beta"]))])

        def keep(step, got):
            step.link(nc.vector.tensor_copy(work[:, :, :], got))

        graph_attention(nc, c, g, "t", xT, w["L0_ffn_W_gat"], w["L0_ffn_att_src"], w["L0_ffn_att_dst"],
                        w["L0_ffn_b_gat"], H, scratch, keep)
        gates = s.enter_context(nc.semaphore("t_gates"))
        gap_ready = s.enter_context(nc.semaphore("t_gap_ready"))
        gap_exp = s.enter_context(nc.semaphore("t_gap_exp"))
        asked = s.enter_context(nc.semaphore("t_asked"))
        rooted = s.enter_context(nc.semaphore("t_rooted"))
        with nc.Block() as block:
            mean, var, rstd, top1, top2, seen, free, gap, p2, w1, w2, spare = (col[:, k, :] for k in range(12))

            @block.vector
            def _(v):
                step = Steps(nc, v, gates)

                def wide(a, n):
                    return a.unsqueeze(2).broadcast_to([P, NT, n])

                step.link(nc.vector.tensor_reduce(mean, work[:, :, :], AX.X, ALU.add))
                step.link(nc.vector.tensor_scalar(mean, mean, 1.0 / HE, None, ALU.mult))
                step.link(nc.vector.tensor_tensor(work[:, :, :], work[:, :, :], wide(mean, HE), ALU.subtract))
                step.link(nc.vector.tensor_tensor(sq[:, :, :], work[:, :, :], work[:, :, :], ALU.mult))
                step.link(nc.vector.tensor_reduce(var, sq[:, :, :], AX.X, ALU.add))
                step.link(nc.vector.tensor_scalar(var, var, 1.0 / HE, LN_EPS, ALU.mult, ALU.add))
                inverse_root(nc, v, step, var, rstd, asked, rooted)
                step.link(nc.vector.tensor_tensor(work[:, :, :], work[:, :, :], wide(rstd, HE), ALU.mult))
                for k, op in ((0, ALU.mult), (1, ALU.add)):
                    step.link(nc.vector.tensor_tensor(work[:, :, :], work[:, :, :],
                                                      ln[:, k, :].unsqueeze(1).broadcast_to([P, NT, HE]), op))
                step.link(nc.vector.tensor_reduce(score[:, :, :], work[:, :, :].rearrange("p t (h e) -> p t e h", h=H),
                                                  AX.X, ALU.add))
                step.link(nc.vector.tensor_scalar(score[:, :, :], score[:, :, :], 1.0 / H, None, ALU.mult))
                for n, top in enumerate((top1, top2)):
                    step.link(nc.vector.tensor_reduce(top, score[:, :, :], AX.X, ALU.max))
                    step.link(nc.vector.tensor_tensor(equal[:, :, :], score[:, :, :], wide(top, E), ALU.is_equal))
                    step.link(nc.vector.memset(free, 1.0))
                    for e in range(E):
                        step.link(nc.vector.tensor_tensor(picks[:, n, :, e], equal[:, :, e], free, ALU.mult))
                        step.link(nc.vector.tensor_tensor(free, free, picks[:, n, :, e], ALU.subtract))
                    if n == 0:
                        step.link(nc.vector.scalar_tensor_tensor(score[:, :, :], picks[:, 0, :, :], NEG,
                                                                 score[:, :, :], ALU.mult, ALU.add))
                nc.vector.tensor_tensor(gap, top2, top1, ALU.subtract).then_inc(gap_ready, 1)
                v.wait_ge(gap_exp, 1)
                step.link(nc.vector.tensor_scalar(w1, p2, 1.0, None, ALU.add))
                step.link(nc.vector.reciprocal(w1, w1))
                step.link(nc.vector.tensor_tensor(w2, p2, w1, ALU.mult))
                step.link(nc.vector.tensor_tensor(picks[:, 0, :, :], picks[:, 0, :, :], wide(w1, E), ALU.mult))
                step.link(nc.vector.tensor_tensor(picks[:, 1, :, :], picks[:, 1, :, :], wide(w2, E), ALU.mult))
                step.link(nc.vector.tensor_tensor(gate[:, :, :], picks[:, 0, :, :], picks[:, 1, :, :], ALU.add))

            @block.scalar
            def _(act):
                take_root(nc, act, var, rstd, asked, rooted)
                act.wait_ge(gap_ready, 1)
                nc.scalar.activation(p2, gap, ACT.Exp).then_inc(gap_exp, 1)


def experts(nc, c, name, xT, xs, gate, stages, last_w, last_b):
    E = gate.shape[2]
    with ExitStack() as s:
        def sb(n, shape, dt=F32):
            return s.enter_context(nc.sbuf_tensor(f"{name}_{n}", shape, dt))

        def sem(n):
            return s.enter_context(nc.semaphore(f"{name}_{n}"))

        gateT = sb("gateT", [E, NP])
        psA = s.enter_context(nc.psum_tensor(f"{name}_psH", [P, 4, 512], F32))
        psB = s.enter_context(nc.psum_tensor(f"{name}_psY", [P, 2, 2, 512], F32))
        turned, copied, biased, taken = sem("turned"), sem("copied"), sem("biased"), sem("taken")
        with nc.Block() as block:
            @block.tensor
            def _(pe):
                for t in range(NT):
                    wait_after(pe, copied, t - 3)
                    nc.tensor.transpose(psA[0:E, t % 4, 0:P], gate[:, t, :], c.ident[:, :]).then_inc(turned, 1)
                for t in range(NT):
                    pe.wait_ge(copied, t + 1)
                    wait_after(pe, taken, t - 1)
                    nc.tensor.matmul(psB[:, t % 2, 0, 0:D], gateT[:, t * P:(t + 1) * P], last_b[:, :], start=True,
                                     stop=True).then_inc(biased, 1)

            @block.scalar
            def _(act):
                for t in range(NT):
                    act.wait_ge(turned, t + 1)
                    nc.scalar.activation(gateT[:, t * P:(t + 1) * P], psA[0:E, t % 4, 0:P], ACT.Copy).then_inc(copied, 1)

            @block.vector
            def _(v):
                for t in range(NT):
                    v.wait_ge(biased, t + 1)
                    nc.vector.tensor_tensor(xs[:, t, :], xs[:, t, :], psB[:, t % 2, 0, 0:D], ALU.add).then_inc(taken, 1)

        B = 4
        outs = [st[0].shape[3] // P for st in stages]
        PER = sum(outs)
        bufs = [sb(f"hidden{i}", [P, 2, m, B * P]) for i, m in enumerate(outs)]
        made, shaped, finished, added = sem("made"), sem("shaped"), sem("finished"), sem("added")
        xs_flat = xs[:, :, :].rearrange("p t d -> p (t d)")
        gate_flat = gate[:, :, :].rearrange("p t e -> p (t e)")
        whole = NT // B
        rest = NT - whole * B

        def bank(layer, m, e):
            return (e * PER + sum(outs[:layer]) + m) % 4

        assert (E * PER) % 4 == 0

        def blocks_loop(eng, body):
            body(0, B)
            with eng.Fori(1, whole, 1) as j:
                body(j, B)
            if rest:
                body(whole, rest)

        with nc.Block() as block:
            @block.tensor
            def _(pe):
                def hidden(blk, e, layer, tiles):
                    item = blk * E + e
                    weights = stages[layer][0]
                    inputs = weights.shape[2]
                    for m in range(outs[layer]):
                        n = item * PER + sum(outs[:layer]) + m
                        wait_after(pe, shaped, n - 3)
                        if layer and m == 0:
                            pe.wait_ge(shaped, item * PER + sum(outs[:layer]))
                        for k in range(inputs):
                            if layer == 0:
                                src = xT[:, k, bass.ds(blk * (B * P), tiles * P)]
                            else:
                                src = bufs[layer - 1][:, e % 2, k, 0:tiles * P]
                            last = nc.tensor.matmul(psA[:, bank(layer, m, e), 0:tiles * P],
                                                    weights[:, e, k, m * P:(m + 1) * P], src,
                                                    start=(k == 0), stop=(k == inputs - 1))
                        last.then_inc(made, 1)

                def final(blk, e, tiles):
                    item = blk * E + e
                    pe.wait_ge(shaped, (item + 1) * PER)
                    wait_after(pe, added, item - 1)
                    inputs = last_w.shape[2]
                    for t in range(tiles):
                        for k in range(inputs):
                            last = nc.tensor.matmul(psB[:, e % 2, t // 2, (t % 2) * D:(t % 2 + 1) * D],
                                                    bufs[-1][:, e % 2, k, t * P:(t + 1) * P], last_w[:, e, k, :],
                                                    start=(k == 0), stop=(k == inputs - 1))
                    last.then_inc(finished, 1)

                def body(blk, tiles):
                    for e in range(E):
                        for layer in range(len(stages)):
                            hidden(blk, e, layer, tiles)
                        final(blk, e, tiles)
                blocks_loop(pe, body)

            @block.scalar
            def _(act):
                def body(blk, tiles):
                    for e in range(E):
                        item = blk * E + e
                        for layer, (_, func, scale, bias) in enumerate(stages):
                            for m in range(outs[layer]):
                                n = item * PER + sum(outs[:layer]) + m
                                act.wait_ge(made, n + 1)
                                if m == 0:
                                    wait_after(act, finished, item - 1)
                                nc.scalar.activation(
                                    bufs[layer][:, e % 2, m, 0:tiles * P], psA[:, bank(layer, m, e), 0:tiles * P], func,
                                    bias=bias[:, e, m:m + 1],
                                    scale=1.0 if scale is None else scale[:, e, m:m + 1]).then_inc(shaped, 1)
                blocks_loop(act, body)

            @block.vector
            def _(v):
                def body(blk, tiles):
                    for e in range(E):
                        item = blk * E + e
                        v.wait_ge(finished, item + 1)
                        wait_after(v, added, item)
                        for t in range(tiles):
                            rows = xs_flat[:, bass.ds((blk * B + t) * D, D)]
                            last = nc.vector.scalar_tensor_tensor(
                                rows, psB[:, e % 2, t // 2, (t % 2) * D:(t % 2 + 1) * D],
                                gate_flat[:, bass.ds((blk * B + t) * E + e, 1)], rows, ALU.mult, ALU.add)
                        last.then_inc(added, 1)
                blocks_loop(v, body)


def feed_forward_top_two(nc, c, g2, w, xs, scratch):
    E, F = 4, 512
    with ExitStack() as s:
        def sb(n, shape, dt=F32):
            return s.enter_context(nc.sbuf_tensor(f"f_{n}", shape, dt))

        xT = sb("xT", [P, KD, NP])
        gate = sb("gate", [P, NT, E])
        turn_rows(nc, c, "f_n", xs, xT, True)
        top_two_gates(nc, c, w, xT, g2, scratch, gate)
        w1 = sb("w1", [P, E, KD, F])
        w2 = sb("w2", [P, E, F // P, D])
        b1 = sb("b1", [P, E, F // P])
        b2 = sb("b2", [E, D])
        load_weights(nc, "f_w", [
            (w1[:, e, :, :], by_halves(w["L0_ffn_W1"][e])) for e in range(E)] + [
            (w2[:, e, :, :], by_halves(w["L0_ffn_W2"][e])) for e in range(E)] + [
            (b1[:, :, :], w["L0_ffn_b1"].rearrange("e (m p) -> p e m", p=P)),
            (b2[:, :], w["L0_ffn_b2"])])
        experts(nc, c, "f_e", xT, xs, gate, [(w1, ACT.Gelu, None, b1)], w2, b2)


def feed_forward_all(nc, c, w, xs):
    E = 8
    eps = 0.001
    with ExitStack() as s:
        def sb(n, shape, dt=F32):
            return s.enter_context(nc.sbuf_tensor(f"l_{n}", shape, dt))

        def sem(n):
            return s.enter_context(nc.semaphore(f"l_{n}"))

        xT = sb("xT", [P, KD, NP])
        gate = sb("gate", [P, NT, E])
        wr = sb("wr", [P, KD, E])
        br = sb("br", [P, E])
        w1, w2, wo = (sb(n, [P, E, KD, D]) for n in ("w1", "w2", "wo"))
        bn = sb("bn", [P, 2, 5, E, KD])
        scale = sb("scale", [P, 2, E, KD])
        bias = sb("bias", [P, 2, E, KD])
        bo = sb("bo", [E, D])
        turn_rows(nc, c, "l_n", xs, xT, True)
        loads = [(wr[:, :, :], by_halves(w["L1_ffn_Wr"])), (br[:, :], spread_row(w["L1_ffn_br"])),
                 (bo[:, :], w["L1_ffn_bo"])]
        for e in range(E):
            loads += [(w1[:, e, :, :], by_halves(w["L1_ffn_W1"][e])), (w2[:, e, :, :], by_halves(w["L1_ffn_W2"][e])),
                      (wo[:, e, :, :], by_halves(w["L1_ffn_Wo"][e]))]
        for layer, names in enumerate((("b1", "g1", "be1", "m1", "v1"), ("b2", "g2", "be2", "m2", "v2"))):
            for k, n in enumerate(names):
                loads.append((bn[:, layer, k, :, :], w[f"L1_ffn_{n}"].rearrange("e (m p) -> p e m", p=P)))
        load_weights(nc, "l_w", loads)
        project(nc, c, "l_r", xT, wr, br, gate)
        top = sb("top", [P, NT])
        spread = sb("spread", [P, 2, E, KD])
        norm, shifted, exped, asked, rooted = (sem(n) for n in ("norm", "shifted", "exped", "asked", "rooted"))
        with nc.Block() as block:
            @block.vector
            def _(v):
                step = Steps(nc, v, norm)

                def wide(a):
                    return a.unsqueeze(2).broadcast_to([P, NT, E])

                step.link(nc.vector.tensor_reduce(top[:, :], gate[:, :, :], AX.X, ALU.max))
                nc.vector.tensor_tensor(gate[:, :, :], gate[:, :, :], wide(top[:, :]), ALU.subtract).then_inc(shifted, 1)
                step.link(nc.vector.tensor_scalar(spread[:, :, :, :], bn[:, :, 4, :, :], eps, None, ALU.add))
                inverse_root(nc, v, step, spread[:, :, :, :], scale[:, :, :, :], asked, rooted)
                step.mark(nc.vector.tensor_tensor(bias[:, :, :, :], bn[:, :, 0, :, :], bn[:, :, 3, :, :], ALU.subtract))
                step.link(nc.vector.tensor_tensor(scale[:, :, :, :], scale[:, :, :, :], bn[:, :, 1, :, :], ALU.mult))
                step.link(nc.vector.tensor_tensor(bias[:, :, :, :], bias[:, :, :, :], scale[:, :, :, :], ALU.mult))
                step.link(nc.vector.tensor_tensor(bias[:, :, :, :], bias[:, :, :, :], bn[:, :, 2, :, :], ALU.add))
                v.wait_ge(exped, 1)
                step.link(nc.vector.tensor_reduce(top[:, :], gate[:, :, :], AX.X, ALU.add))
                step.link(nc.vector.reciprocal(top[:, :], top[:, :]))
                step.link(nc.vector.tensor_tensor(gate[:, :, :], gate[:, :, :], wide(top[:, :]), ALU.mult))

            @block.scalar
            def _(act):
                act.wait_ge(shifted, 1)
                nc.scalar.activation(gate[:, :, :], gate[:, :, :], ACT.Exp).then_inc(exped, 1)
                take_root(nc, act, spread[:, :, :, :], scale[:, :, :, :], asked, rooted)
        experts(nc, c, "l_e", xT, xs, gate,
                [(w1, ACT.Relu, scale[:, 0, :, :], bias[:, 0, :, :]), (w2, ACT.Relu, scale[:, 1, :, :], bias[:, 1, :, :])],
                wo, bo)


def two_convolutions(nc, c, g1, w, xs, scratch):
    def relu(step, got):
        step.link(nc.vector.tensor_scalar(xs[:, :, :], got, 0.0, None, ALU.max))

    graph_attention(nc, c, g1, "c1", lambda xT: turn_rows(nc, c, "c1_n", xs, xT, True), w["L0_gnn_W1"],
                    w["L0_gnn_att_src1"], w["L0_gnn_att_dst1"], w["L0_gnn_b1"], 8, scratch, relu)

    def add(step, got):
        step.eng.wait_ge(back, 32)
        step.link(nc.vector.tensor_tensor(xs[:, :, :], xs[:, :, :], got, ALU.add))

    with ExitStack() as s:
        back = s.enter_context(nc.semaphore("x_back"))
        graph_attention(nc, c, g1, "c2", lambda xT: turn_rows(nc, c, "c2_n", xs, xT, False), w["L0_gnn_W2"],
                        w["L0_gnn_att_src2"], w["L0_gnn_att_dst2"], w["L0_gnn_b2"], 1, scratch, add,
                        load=lambda sp: load_rows(sp, xs, w["x"], back))


def clear_semaphores(nc):
    ids = sorted({int(x) for x in nc.released_uncleared_semaphores})
    runs = []
    for i in ids:
        if runs and runs[-1].stop == i:
            runs[-1] = range(runs[-1].start, i + 1)
        else:
            runs.append(range(i, i + 1))
    for run in runs:
        nc.all_engine_barrier(sems_to_clear=run)


def gnn_ffn_program(nc, w, out):
    with ExitStack() as ctx:
        g1 = Graph("g1", w["dst"].shape[0], NT, 125, 20)
        g2 = Graph("g2", w["L0_ffn_edge_index"].shape[1], 2048 // P, P, 32)
        c = open_constants(nc, ctx, g1.chunks)
        open_graph(nc, ctx, g1, True)
        open_graph(nc, ctx, g2, False)
        scratch = {"table": nc.dram_tensor("table", (NP * 2 * D,), F32).ap(),
                   "spill": nc.dram_tensor("spill", (g1.chunks * P * D,), F32).ap()}
        make_constants(nc, c)
        for g, dst, src, kind in ((g1, w["dst"], w["src"], w["edge_type_64"]),
                                  (g2, w["L0_ffn_edge_index"][1], w["L0_ffn_edge_index"][0], None)):
            meta = nc.dram_tensor(f"{g.name}_meta", (g.chunks * P + 2, FIELDS), I32).ap()
            sort_edges(nc, c, g, dst, src, kind, meta)
            load_sorted(nc, c, g, meta)
        clear_semaphores(nc)
        xs = ctx.enter_context(nc.sbuf_tensor("xs", [P, NT, D], F32))
        load_x(nc, w["x"], xs)
        two_convolutions(nc, c, g1, w, xs, scratch)
        clear_semaphores(nc)
        feed_forward_top_two(nc, c, g2, w, xs, scratch)
        clear_semaphores(nc)
        relation_attention(nc, c, g1, w, xs, scratch)
        clear_semaphores(nc)
        feed_forward_all(nc, c, w, xs)
        clear_semaphores(nc)
        store_x(nc, xs, out)


def kernel(**inputs):
    import concourse.bacc as bacc
    from concourse.bass_utils import run_bass_kernel_spmd

    nc = bacc.Bacc("TRN2", target_bir_lowering=False, num_devices=1)
    arrays, w = {}, {}
    for name, value in inputs.items():
        a = np.ascontiguousarray(value)
        arrays[f"in_{name}"] = a
        w[name] = nc.dram_tensor(f"in_{name}", a.shape, mybir.dt.from_np(a.dtype), kind="ExternalInput").ap()
    out = nc.dram_tensor("out_x", inputs["x"].shape, F32, kind="ExternalOutput").ap()
    gnn_ffn_program(nc, w, out)
    r = run_bass_kernel_spmd(nc, [arrays], core_ids=[0])
    return r.results[0]["out_x"]
```

```python
import numpy as np
from contextlib import ExitStack

import concourse.bass as bass
from concourse import mybir

F32 = mybir.dt.float32
BF16 = mybir.dt.bfloat16
I32 = mybir.dt.int32
ALU = mybir.AluOpType
ACT = mybir.ActivationFunctionType
AX = mybir.AxisListType

P = 128
D = 256
KD = D // P
N = 3125
NT = (N + P - 1) // P
NP = NT * P
LAST = N - (NT - 1) * P
SLOPE = 0.2
LN_EPS = 1e-5
SOFT_EPS = 1e-16
NEG = -1e30
QUAD = 4
RING = 4
PARTS = 3
FIELDS = 4


class Graph:

    def __init__(self, name, edges, tiles, lanes, group):
        self.name = name
        self.tiles = tiles
        self.lanes = lanes
        self.cols = edges // lanes
        self.group = group
        self.chunks = -(-(edges // P + tiles) // (RING * QUAD)) * (RING * QUAD)
        self.cp = self.chunks // 4
        assert edges == lanes * self.cols and self.chunks == 4 * self.cp
        assert self.chunks % (RING * QUAD) == 0 and self.cp <= P
        assert self.cols % (2 * group) == 0 and self.cols % (RING * QUAD) == 0 and group * tiles <= 512


class Steps:

    def __init__(self, nc, eng, sem):
        self.nc, self.eng, self.sem, self.n = nc, eng, sem, 0

    def mark(self, ins):
        ins.then_inc(self.sem, 1)
        self.n += 1
        return self.n

    def link(self, ins):
        self.mark(ins)
        self.eng.wait_ge(self.sem, self.n)


def wait_after(eng, sem, value):
    if not (isinstance(value, int) and value <= 0):
        eng.wait_ge(sem, value)


def round_of(q, b):
    return 16 // RING * (q - b)


def lasting(nc, c, name, count):
    return [c.ctx.enter_context(nc.semaphore(f"{name}{b}")) for b in range(count)]


def make_constants(nc, c):
    with ExitStack() as s:
        filled = s.enter_context(nc.semaphore("const_filled"))
        masked = s.enter_context(nc.semaphore("const_masked"))
        block = s.enter_context(nc.Block())

        @block.gpsimd
        def _(pool):
            step = Steps(nc, pool, filled)
            step.mark(nc.gpsimd.iota(c.iota[:, :], pattern=[[1, P]], base=0, channel_multiplier=0,
                                     allow_small_or_imprecise_dtypes=True))
            step.mark(nc.gpsimd.iota(c.iota_chunk[:, :], pattern=[[1, c.iota_chunk.shape[1]]], base=0,
                                     channel_multiplier=0, allow_small_or_imprecise_dtypes=True))
            step.mark(nc.gpsimd.iota(c.number[:, :], pattern=[[0, 1]], base=0, channel_multiplier=1,
                                     allow_small_or_imprecise_dtypes=True))
            step.mark(nc.gpsimd.memset(c.ones[:, :], 1.0))
            step.mark(nc.gpsimd.memset(c.zeros[:, :], 0.0))
            step.mark(nc.gpsimd.memset(c.ident[:, :], 0.0))
            step.mark(nc.gpsimd.memset(c.identb[:, :], 0.0))
            step.mark(nc.gpsimd.memset(c.below[:, :], 0.0))
            step.mark(nc.gpsimd.memset(c.above[:, :], 0.0))
            pool.wait_ge(filled, step.n)
            for t in (c.ident, c.identb):
                nc.gpsimd.affine_select(out=t[:, :], in_=t[:, :], compare_op=ALU.not_equal, fill=1.0, base=0,
                                        pattern=[[-1, P]], channel_multiplier=1).then_inc(masked, 1)
            nc.gpsimd.affine_select(out=c.below[:, :], in_=c.below[:, :], compare_op=ALU.is_ge, fill=1.0, base=0,
                                    pattern=[[1, P]], channel_multiplier=-1).then_inc(masked, 1)
            nc.gpsimd.affine_select(out=c.above[:, :], in_=c.above[:, :], compare_op=ALU.is_ge, fill=1.0, base=0,
                                    pattern=[[-1, P]], channel_multiplier=1).then_inc(masked, 1)
            pool.wait_ge(masked, 4)


def shift_windows(nc, step, near, far, offset, has_bit, columns):
    width, bit = 2 * P, P // 2
    CP = offset.shape[0]
    while bit:
        width -= bit
        step.mark(nc.vector.tensor_scalar(has_bit[:, :], offset[:, :], bit, None, ALU.bitwise_and))
        step.link(nc.vector.tensor_copy(far[:, :, 0:width], near[:, :, 0:width]))
        step.link(nc.vector.copy_predicated(far[:, :, 0:width], has_bit[:, :].unsqueeze(2).broadcast_to([CP, 4, width]),
                                            near[:, :, bit:bit + width]))
        near, far = far, near
        bit //= 2
    assert width >= columns
    return near


def sort_edges(nc, c, g, dst_d, src_d, type_d, meta, packed_d=None):
    L, C, T, G = g.lanes, g.cols, g.tiles, g.group
    groups = C // G
    quads = C // QUAD
    nm = g.name
    with ExitStack() as s:
        def sb(name, shape, dt):
            return s.enter_context(nc.sbuf_tensor(f"{nm}_{name}", shape, dt))

        def ps(name, shape, dt=F32):
            return s.enter_context(nc.psum_tensor(f"{nm}_{name}", shape, dt))

        def sem(name):
            return s.enter_context(nc.semaphore(f"{nm}_{name}"))

        rec = sb("rec", [L, C, FIELDS], I32)
        dst = sb("dst", [L, C], I32)
        src = sb("src", [L, C], I32)
        typ = sb("typ", [L, C], I32)
        part = sb("part", [L, C], I32)
        dstf = sb("dstf", [L, C], F32)
        lo = sb("lo", [L, C], F32)
        hi = sb("hi", [L, C], F32)
        fill = sb("fill", [P, g.cp // 4 * 4, FIELDS], I32)
        onelo = sb("onelo", [L, 2, G, P], BF16)
        onehi = sb("onehi", [L, 2, G, T], BF16)
        count = sb("count", [P, C + 1, T], F32)
        count_flat = count[:, :, :].rearrange("p c t -> p (c t)")
        total = sb("total", [P, T], F32)
        tiny = sb("tiny", [P, 4, T], F32)
        whole = sb("whole", [P, T], I32)
        quaddst = sb("quaddst", [L, 2, QUAD], F32)
        quadlo = sb("quadlo", [L, 2, QUAD, P], BF16)
        quadT = sb("quadT", [P, 2, QUAD, P], F32)
        quadhi = sb("quadhi", [L, 2, QUAD, T], F32)
        found = sb("found", [L, 2, QUAD, T], F32)
        first = sb("first", [L, 2, QUAD], F32)
        rank = sb("rank", [L, 2, QUAD], F32)
        junk = sb("junk", [L, 2, QUAD, P], F32)
        place = sb("place", [L, RING, QUAD], I32)
        slot = sb("slot", [L, RING, QUAD, FIELDS], I32)
        firsts = sb("firsts", [P, 4, T], F32)
        in_lane = sb("in_lane", [L, T], F32)
        ones_row = sb("ones_row", [L, C], F32)
        by_tile = sb("by_tile", [T, 4], F32)
        started = sb("started", [T, g.chunks], F32)
        out_of_order = sb("out_of_order", [P, 1], F32)
        unsorted = sb("unsorted", [1, 1], I32)
        short_way = packed_d is not None
        if short_way:
            CP = g.cp
            lane_bits, source_bits = P.bit_length() - 1, (N - 1).bit_length()
            next_dst = sb("next_dst", [L, C], I32)
            packed = sb("packed", [L, C], I32)
            spare = sb("spare", [L, C], I32)
            span = sb("span", [CP, 4, 3], F32)
            chunk_no = sb("chunk_no", [CP, 4], F32)
            first_edge = sb("first_edge", [CP, 4], I32)
            offset = sb("offset", [CP, 4], I32)
            has_bit = sb("has_bit", [CP, 4], I32)
            run = sb("run", [CP, 2, 4], I32)
            window = sb("window", [CP, 4, 2 * P], I32)
            moved = sb("moved", [CP, 4, 2 * P], I32)
            field = sb("field", [CP, 3, 4, P], I32)
            fieldf = sb("fieldf", [CP, 4, 4, P], F32)
            valid = sb("valid", [CP, 4, P], F32)
            records = sb("records", [CP, 4, P, FIELDS], I32)
            packed_rows = packed_d.shape[0]
        psC = ps("psC", [P, 2, 512])
        psT = ps("psT", [P, 2, 1024], BF16)
        psR = ps("psR", [P, 2, QUAD * P])
        psL = ps("psL", [P, 2, 512])
        assert meta.shape[0] == g.chunks * P + 2

        loaded = sem("loaded")
        dve = sem("dve")
        filled = sem("filled")
        ready = sem("ready")
        one_ready = sem("one_ready")
        counted = sem("counted")
        evacuated = sem("evacuated")
        totals = sem("totals")
        summed = sem("summed")
        successors_set = sem("successors_set")
        firsts_ready = sem("firsts_ready")
        columns_turned = sem("columns_turned")
        started_ready = sem("started_ready")
        tables_made = sem("tables_made")
        with nc.Block() as block:
            @block.sync
            def _(sp):
                sp.dma_start(dst[:, :], dst_d.rearrange("(l c) -> l c", l=L)).then_inc(loaded, 16)
                sp.dma_start(src[:, :], src_d.rearrange("(l c) -> l c", l=L)).then_inc(loaded, 16)
                if type_d is not None:
                    sp.dma_start(typ[:, :], type_d.rearrange("(l c) -> l c", l=L)).then_inc(loaded, 16)
                if short_way:
                    sp.wait_ge(successors_set, 1)
                    E = L * C
                    sp.dma_start(next_dst[0:L - 1, :],
                                 dst_d[1:E - C + 1].rearrange("(l c) -> l c", l=L - 1)).then_inc(loaded, 16)
                    sp.dma_start(next_dst[L - 1:L, 0:C - 1],
                                 dst_d[E - C + 1:E].rearrange("(l c) -> l c", l=1)).then_inc(loaded, 16)
                sp.wait_ge(ready, 1)
                rows = g.chunks * P // P
                for a in range(0, rows, fill.shape[1]):
                    b = min(a + fill.shape[1], rows)
                    sp.dma_start(meta[1:1 + g.chunks * P, :].rearrange("(p r) f -> p r f", p=P)[:, a:b, :],
                                 fill[:, 0:b - a, :]).then_inc(filled, 16)
                sp.dma_start(meta[0:1, :], fill[0:1, 0, :]).then_inc(filled, 16)
                sp.dma_start(meta[1 + g.chunks * P:2 + g.chunks * P, :], fill[0:1, 0, :]).then_inc(filled, 16)
                sp.wait_ge(filled, 16 * (2 + (rows + fill.shape[1] - 1) // fill.shape[1]))

            @block.vector
            def _(v):
                step = Steps(nc, v, dve)
                nc.vector.memset(ones_row[:, :], 1.0)
                nc.vector.memset(in_lane[:, :], 0.0)
                if short_way:
                    nc.vector.memset(next_dst[:, :], 1 << 20).then_inc(successors_set, 1)
                step.link(nc.vector.memset(fill[:, :, :], 0))
                step.link(nc.vector.memset(fill[:, :, 1:3], -1))
                v.sem_inc(ready, 1)
                if type_d is None:
                    step.link(nc.vector.memset(rec[:, :, 3], 0))
                v.wait_ge(loaded, 16 * (2 + (type_d is not None) + 2 * short_way))
                nc.vector.tensor_copy(dstf[:, :], dst[:, :])
                nc.vector.tensor_copy(rec[:, :, 0], src[:, :])
                nc.vector.tensor_copy(rec[:, :, 2], dst[:, :])
                if type_d is not None:
                    nc.vector.tensor_copy(rec[:, :, 3], typ[:, :])
                step.link(nc.vector.tensor_scalar(part[:, :], dst[:, :], P - 1, None, ALU.bitwise_and))
                nc.vector.tensor_copy(rec[:, :, 1], part[:, :])
                step.link(nc.vector.tensor_copy(lo[:, :], part[:, :]))
                step.link(nc.vector.tensor_scalar(part[:, :], dst[:, :], P.bit_length() - 1, None, ALU.arith_shift_right))
                step.link(nc.vector.tensor_copy(hi[:, :], part[:, :]))
                if short_way:
                    step.link(nc.vector.tensor_tensor(spare[:, :], dst[:, :], next_dst[:, :], ALU.is_gt))
                    step.link(nc.vector.tensor_reduce(out_of_order[0:L, :], spare[:, :], AX.X, ALU.max))
                    step.link(nc.vector.tensor_scalar(packed[:, :], rec[:, :, 1], source_bits, None,
                                                      ALU.logical_shift_left))
                    step.link(nc.vector.tensor_tensor(packed[:, :], packed[:, :], src[:, :], ALU.bitwise_or))
                    step.link(nc.vector.tensor_scalar(spare[:, :], typ[:, :], source_bits + lane_bits, None,
                                                      ALU.logical_shift_left))
                    step.link(nc.vector.tensor_tensor(packed[:, :], packed[:, :], spare[:, :], ALU.bitwise_or))
                for t in range(1, T):
                    step.mark(nc.vector.scalar_tensor_tensor(
                        count_flat[0:L, t * C:(t + 1) * C], hi[:, :], float(t), ones_row[:, :], ALU.is_lt, ALU.mult,
                        accum_out=in_lane[:, t:t + 1]))
                v.wait_ge(dve, step.n)
                v.sem_inc(totals, 1)
                n_t, after, first_c = (tiny[:, k, :] for k in range(3))
                edges, before, shift_c, shift_by = (firsts[:, k, :] for k in range(4))
                v.wait_ge(summed, 1)
                step.link(nc.vector.tensor_copy(before, psL[:, 0, 0:T]))
                step.link(nc.vector.tensor_tensor(edges[:, 0:T - 1], before[:, 1:T], before[:, 0:T - 1], ALU.subtract))
                step.link(nc.vector.tensor_scalar(edges[:, T - 1:T], before[:, T - 1:T], -1.0, float(L * C), ALU.mult,
                                                  ALU.add))
                step.link(nc.vector.tensor_scalar(whole[:, :], edges, float(P - 1), None, ALU.add))
                step.link(nc.vector.tensor_scalar(whole[:, :], whole[:, :], -P, None, ALU.bitwise_and))
                step.link(nc.vector.tensor_copy(n_t, whole[:, :]))
                step.link(nc.vector.tensor_tensor_scan(after, n_t, c.zeros[:, 0:T], 0.0, ALU.add, ALU.add))
                step.link(nc.vector.tensor_tensor(first_c, after, n_t, ALU.subtract))
                step.link(nc.vector.tensor_tensor(before, before, first_c, ALU.subtract))
                step.link(nc.vector.tensor_copy(shift_by, before))
                step.link(nc.vector.tensor_tensor(shift_by[:, 1:T], before[:, 1:T], before[:, 0:T - 1], ALU.subtract))
                step.link(nc.vector.tensor_scalar(shift_c, first_c, 1.0 / P, None, ALU.mult))
                v.sem_inc(firsts_ready, 1)
                v.wait_ge(columns_turned, 1)
                step.link(nc.vector.memset(by_tile[:, :], 1.0))
                for k, row in ((0, 2), (1, 0), (3, 1)):
                    step.link(nc.vector.tensor_copy(by_tile[:, k:k + 1], psR[0:T, 0, row * P:row * P + 1]))
                step.link(nc.vector.tensor_scalar(started[:, :], c.iota_chunk[0:T, 0:g.chunks], by_tile[:, 3:4], None,
                                                  ALU.is_ge))
                v.sem_inc(started_ready, 1)
                v.wait_ge(tables_made, 1)
                step.link(nc.vector.tensor_scalar(g.tile_of[:, :], psC[0:1, 0, 0:g.chunks], -1.0, None, ALU.add))
                if short_way:
                    step.link(nc.vector.tensor_copy(unsorted[:, :], psL[0:1, 0, 2 * T:2 * T + 1]))
                    step.link(nc.vector.tensor_copy(span[:, :, :], psR[0:CP, 1, 0:12].rearrange("p (g k) -> p g k", g=4)))

            @block.tensor
            def _(pe):
                pe.wait_ge(totals, 1)
                if short_way:
                    nc.tensor.matmul(psL[:, 0, 2 * T:2 * T + 1], c.ones[0:L, :], out_of_order[0:L, :], start=True, stop=True)
                nc.tensor.matmul(psL[:, 0, 0:T], c.ones[0:L, :], in_lane[:, :], start=True, stop=True).then_inc(summed, 1)
                pe.wait_ge(firsts_ready, 1)
                for row, source in enumerate((0, 2, 3)):
                    last = nc.tensor.transpose(psR[0:T, 0, row * P:(row + 1) * P], firsts[:, source, :], c.ident[:, :])
                last.then_inc(columns_turned, 1)
                pe.wait_ge(started_ready, 1)
                if short_way:
                    for q in range(4):
                        nc.tensor.matmul(psR[0:CP, 1, 3 * q:3 * q + 3], started[:, q * CP:(q + 1) * CP],
                                         by_tile[:, 0:3], start=True, stop=True)
                nc.tensor.matmul(psC[0:1, 0, 0:g.chunks], c.ones[0:T, 0:1], started[:, :], start=True,
                                 stop=True).then_inc(tables_made, 1)

        column_totals, scanned, stacked = sem("column_totals"), sem("scanned"), sem("stacked")
        based = sem("based")
        onehot = sem("onehot")
        turned = sem("turned")
        rows = sem("rows")
        copied = sem("copied")
        looked = sem("looked")
        chain = sem("chain")
        placed = sem("placed")
        passed = sem("passed")
        skipped = sem("skipped")
        scattered = lasting(nc, c, f"{nm}_scattered", RING)
        if short_way:
            listed_out, kept = sem("listed_out"), sem("kept")
            runs_ready, recorded, cut = sem("runs_ready"), sem("recorded"), sem("cut")
            windows, = lasting(nc, c, f"{nm}_windows", 1)

            def vector_windows(v):
                step = Steps(nc, v, cut)
                quarters = [CP, 4, P]

                def wide(a):
                    return a.unsqueeze(2).broadcast_to(quarters)

                for q in range(4):
                    step.mark(nc.vector.tensor_scalar(chunk_no[:, q:q + 1], c.number[0:CP, :], float(q * CP), None, ALU.add))
                v.wait_ge(cut, step.n)
                step.link(nc.vector.scalar_tensor_tensor(span[:, :, 0], chunk_no[:, :], float(P), span[:, :, 0],
                                                         ALU.mult, ALU.add))
                step.link(nc.vector.tensor_tensor(span[:, :, 1], span[:, :, 1], span[:, :, 0], ALU.subtract))
                step.link(nc.vector.tensor_scalar(span[:, :, 0], span[:, :, 0], float(L * C), None, ALU.min))
                step.link(nc.vector.tensor_copy(first_edge[:, :], span[:, :, 0]))
                step.link(nc.vector.tensor_scalar(offset[:, :], first_edge[:, :], P - 1, None, ALU.bitwise_and))
                step.link(nc.vector.tensor_scalar(run[:, 0, :], first_edge[:, :], lane_bits, None, ALU.arith_shift_right))
                nc.vector.tensor_scalar(run[:, 1, :], run[:, 0, :], 1, None, ALU.add).then_inc(runs_ready, 1)
                v.wait_ge(windows, 16 * 8)
                got = shift_windows(nc, step, window, moved, offset, has_bit, P)[:, :, 0:P]
                for k, (low, bits) in enumerate(((0, source_bits), (source_bits, lane_bits))):
                    step.link(nc.vector.tensor_scalar(field[:, k, :, :], got, low, None, ALU.logical_shift_right))
                    step.link(nc.vector.tensor_scalar(field[:, k, :, :], field[:, k, :, :], (1 << bits) - 1, None,
                                                      ALU.bitwise_and))
                step.link(nc.vector.tensor_scalar(field[:, 2, :, :], got, source_bits + lane_bits, None,
                                                  ALU.logical_shift_right))
                step.link(nc.vector.tensor_tensor(valid[:, :, :], c.iota[0:CP, :].unsqueeze(1).broadcast_to(quarters),
                                                  wide(span[:, :, 1]), ALU.is_lt))
                step.link(nc.vector.tensor_scalar(span[:, :, 2], span[:, :, 2], -1.0, float(P), ALU.add, ALU.mult))
                step.link(nc.vector.tensor_scalar(fieldf[:, 1, :, :], field[:, 1, :, :], 1.0, None, ALU.add))
                step.link(nc.vector.tensor_tensor(fieldf[:, 2, :, :], fieldf[:, 1, :, :], wide(span[:, :, 2]), ALU.add))
                step.mark(nc.vector.tensor_tensor(records[:, :, :, 0], field[:, 0, :, :], valid[:, :, :], ALU.mult))
                step.mark(nc.vector.tensor_tensor(records[:, :, :, 3], field[:, 2, :, :], valid[:, :, :], ALU.mult))
                for k in (1, 2):
                    step.link(nc.vector.tensor_tensor(fieldf[:, k, :, :], fieldf[:, k, :, :], valid[:, :, :], ALU.mult))
                    step.link(nc.vector.tensor_scalar(records[:, :, :, k], fieldf[:, k, :, :], -1.0, None, ALU.add))
                v.sem_inc(recorded, 1)

            def sync_windows(sp):
                E = L * C
                sp.dma_start(packed_d.rearrange("r l -> (r l)")[0:E].rearrange("(l c) -> l c", l=L),
                             packed[:, :]).then_inc(listed_out, 16)
                sp.dma_start(packed_d.rearrange("r l -> (r l)")[E:packed_rows * P].rearrange("(l c) -> l c", l=1),
                             packed[0:1, 0:packed_rows * P - E]).then_inc(listed_out, 16)
                sp.wait_ge(recorded, 1)
                sp.dma_start(meta[1:1 + g.chunks * P, :].rearrange("(g p l) f -> p g (l f)", g=4, l=P),
                             records[:, :, :, :].rearrange("p g l f -> p g (l f)")).then_inc(kept, 16)
                sp.wait_ge(kept, 16)

            def pool_windows(pool):
                pool.wait_ge(listed_out, 32)
                pool.wait_ge(runs_ready, 1)
                pool.sem_inc(passed, 1)
                for q in range(4):
                    for half in range(2):
                        nc.gpsimd.indirect_dma_start(
                            out=window[:, q, half * P:(half + 1) * P], out_offset=None, in_=packed_d[:, :],
                            in_offset=bass.IndirectOffsetOnAxis(ap=run[:, half, q:q + 1], axis=0)).then_inc(windows, 16)
                pool.wait_ge(windows, 16 * 8)

        windows_of = {"vector": vector_windows, "gpsimd": pool_windows} if short_way else {"vector": None, "gpsimd": None}

        def either(eng, kind, sorted_way, general_way):
            if not short_way:
                return general_way(eng)
            _, values = nc.values_load_multi_w_load_instructions(
                unsorted[0:1, 0:1], engines=(kind,), min_val=0, max_val=L,
                skip_runtime_bounds_check_because="it counts lanes of the list")
            with eng.If(values[0] < 1):
                if sorted_way is not None:
                    sorted_way(eng)
                else:
                    eng.sem_inc(skipped, 1)
            with eng.Else():
                general_way(eng)
        with nc.Block() as block:
            def vector_general(v):
                step = Steps(nc, v, scanned)
                with v.Fori(0, groups // 2, 1) as j:
                    for b in range(2):
                        v.wait_ge(counted, 2 * j + b + 1)
                        col = bass.ds((2 * j + b) * G, G)
                        nc.vector.tensor_tensor(
                            onelo[:, b, :, :], c.iota[0:L, :].unsqueeze(1).broadcast_to([L, G, P]),
                            lo[:, col].unsqueeze(2).broadcast_to([L, G, P]), ALU.is_equal)
                        nc.vector.tensor_tensor(
                            onehi[:, b, :, :], c.iota[0:L, 0:T].unsqueeze(1).broadcast_to([L, G, T]),
                            hi[:, col].unsqueeze(2).broadcast_to([L, G, T]), ALU.is_equal).then_inc(one_ready, 1)
                v.wait_ge(evacuated, groups + 2)
                step.link(nc.vector.memset(count[:, 0, :], 0.0))
                for t in range(T):
                    last = nc.vector.tensor_tensor_scan(count[:, 1:, t], count[:, 1:, t], c.zeros[:, 0:C], 0.0,
                                                        ALU.add, ALU.add)
                    step.mark(last)
                v.wait_ge(scanned, step.n)
                step.link(nc.vector.tensor_copy(total[:, :], count[:, C, :]))
                v.sem_inc(column_totals, 1)
                v.wait_ge(stacked, 1)
                base = tiny[:, 3, :]
                step.link(nc.vector.tensor_tensor(base, tiny[:, 2, :], psL[:, 1, 0:T], ALU.add))
                step.link(nc.vector.tensor_scalar(base, base, 1.0, None, ALU.add))
                nc.vector.tensor_tensor(
                    count[:, 0:C, :], count[:, 0:C, :], base.unsqueeze(1).broadcast_to([P, C, T]),
                    ALU.add).then_inc(based, 1)
                v.sem_inc(placed, 2)

                def build(q, b):
                    col = bass.ds(q * QUAD, QUAD)
                    nc.vector.tensor_copy(quaddst[:, b, :], dstf[:, col])
                    nc.vector.tensor_tensor(
                        quadlo[:, b, :, :], c.iota[0:L, :].unsqueeze(1).broadcast_to([L, QUAD, P]),
                        lo[:, col].unsqueeze(2).broadcast_to([L, QUAD, P]), ALU.is_equal).then_inc(onehot, 1)

                def pair(q0, b0, first_round):
                    for b in range(2):
                        v.wait_ge(turned, q0 + b + 1)
                        build(q0 + b, b)
                    for b in range(2):
                        q, r = q0 + b, b0 + b
                        col = bass.ds(q * QUAD, QUAD)
                        nc.vector.tensor_tensor(
                            quadhi[:, b, :, :], c.iota[0:L, 0:T].unsqueeze(1).broadcast_to([L, QUAD, T]),
                            hi[:, col].unsqueeze(2).broadcast_to([L, QUAD, T]), ALU.is_equal).then_inc(chain, 1)
                        if not first_round:
                            v.wait_ge(scattered[r], QUAD * round_of(q, r))
                        nc.vector.tensor_copy(slot[:, r, :, :], rec[:, col, :]).then_inc(chain, 1)
                        v.wait_ge(rows, q + 1)
                        for k in range(QUAD):
                            nc.vector.scalar_tensor_tensor(
                                junk[:, b, k, 0:L], psR[0:L, b, k * P:k * P + L], dstf[:, bass.ds(q * QUAD + k, 1)],
                                c.below[0:L, 0:L], ALU.is_equal, ALU.mult,
                                accum_out=rank[:, b, k:k + 1]).then_inc(chain, 1)
                    for b in range(2):
                        v.wait_ge(looked, q0 + b + 3)
                        v.wait_ge(chain, 8 * q0 + 12 + 2 * b)
                        nc.vector.tensor_tensor(found[:, b, :, :],
                                                psL[0:L, b, 0:QUAD * T].rearrange("p (k t) -> p k t", k=QUAD),
                                                quadhi[:, b, :, :], ALU.mult).then_inc(chain, 1)
                        v.wait_ge(chain, 8 * q0 + 13 + 2 * b)
                        nc.vector.tensor_reduce(first[:, b, :], found[:, b, :, :], AX.X, ALU.add).then_inc(chain, 1)
                        v.wait_ge(chain, 8 * q0 + 14 + 2 * b)
                        nc.vector.tensor_tensor(place[:, b0 + b, :], first[:, b, :], rank[:, b, :],
                                                ALU.add).then_inc(placed, 1)

                for b in range(0, RING, 2):
                    pair(b, b, True)
                with v.Fori(1, quads // RING, 1) as j:
                    for b in range(0, RING, 2):
                        pair(RING * j + b, b, False)

            def tensor_general(pe):
                pe.sem_inc(counted, 2)
                with pe.Fori(0, groups // 2, 1) as j:
                    for b in range(2):
                        pe.wait_ge(one_ready, 2 * j + b + 1)
                        pe.wait_ge(evacuated, 2 * j + b + 1)
                        for k in range(G):
                            last = nc.tensor.matmul(psC[:, b, k * T:(k + 1) * T], onelo[:, b, k, :],
                                                    onehi[:, b, k, :], start=True, stop=True)
                        last.then_inc(counted, 1)
                pe.wait_ge(column_totals, 1)
                nc.tensor.matmul(psL[:, 1, 0:T], c.above[:, :], total[:, :], start=True, stop=True).then_inc(stacked, 1)
                pe.wait_ge(based, 1)
                pe.sem_inc(turned, 2)
                pe.sem_inc(looked, 2)
                with pe.Fori(0, quads // 2, 1) as j:
                    for b in range(2):
                        q = 2 * j + b
                        pe.wait_ge(onehot, q + 1)
                        pe.wait_ge(copied, q + 1)
                        for k in range(QUAD):
                            last = nc.tensor.transpose(psT[:, b, k * P:k * P + L], quadlo[:, b, k, :], c.identb[0:L, 0:L])
                        last.then_inc(turned, 1)
                        pe.wait_ge(placed, q + 1)
                        for k in range(QUAD):
                            last = nc.tensor.matmul(psR[:, b, k * P:k * P + L],
                                                    quaddst[:, b, k:k + 1].broadcast_to([L, P]), c.ident[0:L, 0:L], start=True, stop=True)
                        last.then_inc(rows, 1)
                    for b in range(2):
                        q = 2 * j + b
                        pe.wait_ge(copied, q + 3)
                        for k in range(QUAD):
                            last = nc.tensor.matmul(psL[0:L, b, k * T:(k + 1) * T], quadT[:, b, k, 0:L],
                                                    count_flat[:, bass.ds((q * QUAD + k) * T, T)],
                                                    start=True, stop=True)
                        last.then_inc(looked, 1)

            def scalar_general(act):
                act.sem_inc(evacuated, 2)
                with act.Fori(0, groups // 2, 1) as j:
                    for b in range(2):
                        act.wait_ge(counted, 2 * j + b + 3)
                        nc.scalar.activation(
                            count_flat[:, bass.ds((2 * j + b) * (G * T) + T, G * T)],
                            psC[:, b, 0:G * T], ACT.Copy).then_inc(evacuated, 1)
                act.sem_inc(copied, 2)
                with act.Fori(0, quads // 2, 1) as j:
                    for b in range(2):
                        act.wait_ge(turned, 2 * j + b + 3)
                        act.wait_ge(looked, 2 * j + b + 1)
                        nc.scalar.activation(quadT[:, b, :, 0:L],
                                             psT[:, b, 0:QUAD * P].rearrange("p (k l) -> p k l", k=QUAD)[:, :, 0:L],
                                             ACT.Copy).then_inc(copied, 1)

            def gpsimd_general(pool):
                with pool.Fori(0, quads // RING, 1) as j:
                    for b in range(RING):
                        pool.wait_ge(placed, RING * j + b + 3)
                        pool.sem_inc(passed, 1)
                        for k in range(QUAD):
                            nc.gpsimd.indirect_dma_start(
                                out=meta[:, :], out_offset=bass.IndirectOffsetOnAxis(ap=place[:, b, k:k + 1], axis=0),
                                in_=slot[:, b, k, :], in_offset=None).then_inc(scattered[b], 16)
                for b in range(RING):
                    pool.wait_ge(scattered[b], 16 * QUAD * (quads // RING))

            @block.vector
            def _(v):
                either(v, mybir.EngineType.DVE, windows_of["vector"], vector_general)

            @block.tensor
            def _(pe):
                either(pe, mybir.EngineType.PE, None, tensor_general)

            @block.scalar
            def _(act):
                either(act, mybir.EngineType.Activation, None, scalar_general)

            @block.gpsimd
            def _(pool):
                either(pool, mybir.EngineType.Pool, windows_of["gpsimd"], gpsimd_general)

            if short_way:
                @block.sync
                def _(sp):
                    either(sp, mybir.EngineType.SP, sync_windows, lambda sp: sp.sem_inc(skipped, 1))


def load_sorted(nc, c, g, meta):
    CP, nm = g.cp, g.name
    with ExitStack() as s:
        raw = s.enter_context(nc.sbuf_tensor(f"{nm}_raw", [CP, 4, P, FIELDS], I32))
        edge = s.enter_context(nc.sbuf_tensor(f"{nm}_edge", [CP, 4, 2], I32))
        vals = s.enter_context(nc.sbuf_tensor(f"{nm}_vals", [CP, 4, 4, P], F32))
        key = s.enter_context(nc.sbuf_tensor(f"{nm}_key", [CP, 4, P + 2], F32))
        psB = s.enter_context(nc.psum_tensor(f"{nm}_psB", [P, 3, 512], F32))
        loaded = s.enter_context(nc.semaphore(f"{nm}_meta_loaded"))
        dve = s.enter_context(nc.semaphore(f"{nm}_meta_dve"))
        ready = s.enter_context(nc.semaphore(f"{nm}_meta_vals"))
        turned = s.enter_context(nc.semaphore(f"{nm}_meta_turned"))
        with nc.Block() as block:
            @block.sync
            def _(sp):
                rows = g.chunks * P
                sp.dma_start(raw[:, :, :, :].rearrange("p g l f -> p g (l f)"),
                             meta[1:1 + rows, :].rearrange("(g p l) f -> p g (l f)", g=4, l=P)).then_inc(loaded, 16)
                before = meta[0:rows, :].rearrange("(g p l) f -> p g l f", g=4, l=P)[:, :, 0, 2:3]
                after = meta[2:2 + rows, :].rearrange("(g p l) f -> p g l f", g=4, l=P)[:, :, P - 1, 2:3]
                sp.dma_start(edge[:, :, 0:1], before, allow_slow_non_contiguous=True).then_inc(loaded, 16)
                sp.dma_start(edge[:, :, 1:2], after, allow_slow_non_contiguous=True).then_inc(loaded, 16)

            @block.vector
            def _(v):
                step = Steps(nc, v, dve)
                v.wait_ge(loaded, 48)
                for k, field in enumerate((0, 1, 3)):
                    nc.vector.tensor_copy(vals[:, k, :, :], raw[:, :, :, field]).then_inc(ready, 1)
                nc.vector.tensor_copy(key[:, :, 0:1], edge[:, :, 0:1])
                nc.vector.tensor_copy(key[:, :, P + 1:P + 2], edge[:, :, 1:2])
                step.link(nc.vector.tensor_copy(key[:, :, 1:P + 1], raw[:, :, :, 2]))
                for shift, out in ((0, g.reset_fwd), (2, g.reset_bwd)):
                    step.link(nc.vector.tensor_tensor(out[:, :, :], key[:, :, 1:P + 1], key[:, :, shift:shift + P],
                                                      ALU.is_equal))
                    step.link(nc.vector.tensor_scalar(out[:, :, :], out[:, :, :], -NEG, NEG, ALU.mult, ALU.add))
                step.link(nc.vector.tensor_scalar(g.is_last[:, :, :], g.reset_bwd[:, :, :], 0.0, None, ALU.is_lt))
                v.wait_ge(turned, 3)
                nc.vector.tensor_copy(g.src[:, :], psB[:, 0, 0:4 * CP])
                nc.vector.tensor_copy(g.lane[:, :], psB[:, 1, 0:4 * CP])
                if g.type is not None:
                    nc.vector.tensor_copy(g.type[:, :], psB[:, 2, 0:4 * CP])

            @block.tensor
            def _(pe):
                for k in range(3):
                    pe.wait_ge(ready, k + 1)
                    for q in range(4):
                        last = nc.tensor.transpose(psB[:, k, q * CP:(q + 1) * CP], vals[:, k, q, :],
                                                   c.ident[0:CP, 0:CP])
                    last.then_inc(turned, 1)


class Holder:
    pass


def open_graph(nc, ctx, g, typed):
    def sb(name, shape, dt):
        return ctx.enter_context(nc.sbuf_tensor(f"{g.name}_{name}", shape, dt))
    g.tile_of = sb("tile_of", [1, g.chunks], I32)
    g.src = sb("src_col", [P, g.chunks], I32)
    g.lane = sb("lane_col", [P, g.chunks], F32)
    g.type = sb("type_col", [P, g.chunks], F32) if typed else None
    g.reset_fwd = sb("reset_fwd", [g.cp, 4, P], F32)
    g.reset_bwd = sb("reset_bwd", [g.cp, 4, P], F32)
    g.is_last = sb("is_last", [g.cp, 4, P], F32)


def open_constants(nc, ctx):
    c = Holder()
    c.ctx = ctx
    def sb(name, shape, dt):
        return ctx.enter_context(nc.sbuf_tensor(name, shape, dt))
    c.iota = sb("iota", [P, P], F32)
    c.number = sb("number", [P, 1], F32)
    c.ones = sb("ones", [P, P], F32)
    c.zeros = sb("zeros", [P, 512], F32)
    c.ident = sb("ident", [P, P], F32)
    c.identb = sb("identb", [P, P], BF16)
    return c


def open_sort_constants(nc, ctx, c, most_chunks):
    def sb(name, shape, dt):
        return ctx.enter_context(nc.sbuf_tensor(name, shape, dt))
    c.iota_chunk = sb("iota_chunk", [32, most_chunks], F32)
    c.below = sb("below", [P, P], F32)
    c.above = sb("above", [P, P], F32)


def ring_loop(eng, count, body, peel_last=False):
    rounds = count // RING
    for b in range(RING):
        body(b, b)
    with eng.Fori(1, rounds - 1 if peel_last else rounds, 1) as j:
        for b in range(RING):
            body(RING * j + b, b)
    if peel_last:
        for b in range(RING):
            body(RING * (rounds - 1) + b, b)


def beside_loop(eng, count, body, beside):
    per = RING * beside.experts
    blocks = beside.blocks

    def block_of(blk):
        for r in range(per):
            body(per * blk + r, r % RING, (blk, r // RING, r % RING))

    assert RING == 4 and blocks * per <= count
    block_of(0)
    with eng.Fori(1, blocks, 1) as j:
        block_of(j)
    for q in range(per * blocks, count):
        body(q, q % RING, None)


class ExpertsBeside:

    def __init__(self, xT, w1, b1, w2, y):
        self.xT, self.w1, self.b1, self.w2, self.y = xT, w1, b1, w2, y
        self.experts, self.blocks = w1.shape[1], y.shape[1] // 4
        assert w1.shape[3] == 4 * P and y.shape[1] % 4 == 0

    def open(self, nc, s, name):
        self.nc = nc
        self.hidden = s.enter_context(nc.sbuf_tensor(f"{name}_hidden", [P, 4, 4 * P], F32))
        self.psH = s.enter_context(nc.psum_tensor(f"{name}_psH", [P, 2, 512], F32))
        self.psY = s.enter_context(nc.psum_tensor(f"{name}_psY", [P, 2, 512], F32))
        self.made, self.shaped, self.finished, self.yielded = (
            s.enter_context(nc.semaphore(f"{name}_{n}")) for n in ("made", "shaped", "finished", "yielded"))

    def tensor(self, pe, blk, e, share):
        item = blk * self.experts + e
        if share < 2:
            for m in (2 * share, 2 * share + 1):
                wait_after(pe, self.shaped, 4 * item + m - 1)
                for k in range(KD):
                    last = self.nc.tensor.matmul(self.psH[:, m % 2, :], self.w1[:, e, k, m * P:(m + 1) * P],
                                                 self.xT[:, k, bass.ds(blk * (4 * P), 4 * P)], start=(k == 0),
                                                 stop=(k == KD - 1))
                last.then_inc(self.made, 1)
        else:
            half = share - 2
            pe.wait_ge(self.shaped, 4 * item + 4)
            wait_after(pe, self.yielded, 2 * item + half - 1)
            for t in range(2):
                for k in range(4):
                    last = self.nc.tensor.matmul(self.psY[:, half, t * D:(t + 1) * D],
                                                 self.hidden[:, k, (2 * half + t) * P:(2 * half + t + 1) * P],
                                                 self.w2[:, e, k, :], start=(k == 0), stop=(k == 3))
            last.then_inc(self.finished, 1)

    def scalar(self, act, blk, e, share):
        item = blk * self.experts + e
        for m in (2 * share, 2 * share + 1):
            act.wait_ge(self.made, 4 * item + m + 1)
            self.nc.scalar.activation(self.hidden[:, m, :], self.psH[:, m % 2, :], ACT.Gelu,
                                      bias=self.b1[:, e, m:m + 1]).then_inc(self.shaped, 1)

    def vector(self, v, blk, e, half):
        item = blk * self.experts + e
        v.wait_ge(self.finished, 2 * item + half + 1)
        self.nc.vector.tensor_copy(self.y[:, bass.ds(blk * 4 + 2 * half, 2), e, :],
                                   self.psY[:, half, :].rearrange("p (t d) -> p t d", t=2)).then_inc(self.yielded, 1)


class TileRegisters:

    def __init__(self, nc, engine, g):
        self.nc, self.engine, self.g = nc, engine, g

    def of(self, q, b):
        if b % 2 == 0:
            _, self.pair = self.nc.values_load_multi_w_load_instructions(
                self.g.tile_of[0:1, bass.ds(q * QUAD, 2 * QUAD)], engines=(self.engine,), min_val=0,
                max_val=self.g.tiles - 1,
                skip_runtime_bounds_check_because="sort_edges counts tiles that start before a chunk, less one")
        return self.pair[b % 2 * QUAD:(b % 2 + 1) * QUAD]


def gather_scores(nc, c, g, name, table, spill, node_parts, NV, heads, width, store, relation=None,
                  kept=None, beside=None):
    K = QUAD
    quads = g.chunks // K
    row = table.shape[1]
    nodes_flat = node_parts[:, :, :, :].rearrange("p t a n -> p (t a n)")
    R, C = (0, 0) if relation is None else (relation.shape[0], relation.shape[2])
    spilled_cols = slice(0, width) if relation is None else slice(row - width, row)
    EB = -(-K * NV // 512)
    per_bank = K // EB
    with ExitStack() as s:
        def sb(n, shape, dt):
            return s.enter_context(nc.sbuf_tensor(f"{name}_{n}", shape, dt))

        def sem(n):
            return s.enter_context(nc.semaphore(f"{name}_{n}"))

        slot = sb("slot", [P, RING, K], I32)
        rows = sb("rows", [P, RING, K, row], F32)
        onehot = sb("onehot", [P, 2, K, P], BF16)
        onehotT = sb("onehotT", [P, 2, K, P], BF16)
        psT = s.enter_context(nc.psum_tensor(f"{name}_psT", [P, 2, 1024], BF16))
        psE = s.enter_context(nc.psum_tensor(f"{name}_psE", [P, 2, EB, 512], F32))
        if R:
            kind = sb("kind", [P, 2, K, R], BF16)
            away = sb("away", [P, K, P + R], F32)
            kindT = sb("kindT", [R, 2, K, P], BF16)
            psR = s.enter_context(nc.psum_tensor(f"{name}_psR", [P, 2, 512], F32))
            prod = sb("prod", [P, 2, K, D], F32)
        saved = sem("saved")
        listed = sem("listed")
        ready = sem("ready")
        gathered = lasting(nc, c, f"{name}_gathered", RING)
        spilled = [sem(f"spilled{b}") for b in range(RING)]
        turned = sem("turned")
        copied = sem("copied")
        spread = sem("spread")
        used = sem("used")
        passed = sem("passed")
        chain = sem("chain")
        measured = sem("measured")
        if beside is not None:
            beside.open(nc, s, f"{name}_beside")
        with nc.Block() as block:
            @block.vector
            def _(v):
                def list_sources(q, b):
                    nc.vector.tensor_copy(slot[:, b, :], g.src[:, bass.ds(q * K, K)]).then_inc(listed, 1)

                def mark_lanes(q, h):
                    wait_after(v, turned, q - 1)
                    nc.vector.tensor_tensor(
                        onehot[:, h, :, :], c.iota[:, :].unsqueeze(1).broadcast_to([P, K, P]),
                        g.lane[:, bass.ds(q * K, K)].unsqueeze(2).broadcast_to([P, K, P]),
                        ALU.is_equal).then_inc(ready, 1)

                def step(q, b, marks, lists):
                    h = b % 2
                    if marks and not R:
                        mark_lanes(q + 2, h)
                    v.wait_ge(gathered[b], K * (round_of(q, b) + 16))
                    v.wait_ge(spread, q + 1)
                    if R:
                        def per_head(a, n):
                            return a[:, n * per_bank:(n + 1) * per_bank, 0:D].rearrange("p k (h d) -> p k h d", h=heads)

                        steps = 2 * EB
                        for n in range(EB):
                            kinds = psR[:, h, n * per_bank * R:(n + 1) * per_bank * R].rearrange("p (k c) -> p k c", k=per_bank)
                            nc.vector.tensor_tensor(
                                per_head(prod[:, h, :, :], n), per_head(rows[:, b, :, :], n),
                                kinds[:, :, 0:C].unsqueeze(2).broadcast_to([P, per_bank, heads, C]),
                                ALU.add).then_inc(chain, 1)
                        for n in range(EB):
                            ks = slice(n * per_bank, (n + 1) * per_bank)
                            v.wait_ge(chain, steps * q + n + 1)
                            nc.vector.tensor_tensor(
                                prod[:, h, ks, :], prod[:, h, ks, :],
                                psE[:, h, n, 0:per_bank * D].rearrange("p (k n) -> p k n", k=per_bank),
                                ALU.mult).then_inc(chain, 1)
                        if lists:
                            list_sources(q + RING, b)
                        for n in range(EB):
                            v.wait_ge(chain, steps * q + EB + n + 1)
                            last = nc.vector.tensor_reduce(
                                store[:, bass.ds(q * K + n * per_bank, per_bank), 0:heads],
                                prod[:, h, n * per_bank:(n + 1) * per_bank, :].rearrange("p k (h d) -> p k h d", h=heads),
                                AX.X, ALU.add)
                        last.then_inc(used, 1)
                    else:
                        vals = psE[:, h, 0, 0:K * NV].rearrange("p (k n) -> p k n", k=K)
                        col = bass.ds(q * K, K)
                        nc.vector.tensor_tensor(store[:, col, 0:heads], rows[:, b, :, width:width + heads],
                                                vals[:, :, 0:heads], ALU.add)
                        nc.vector.tensor_copy(store[:, col, heads:2 * heads], vals[:, :, heads:2 * heads]).then_inc(used, 1)
                        if lists:
                            list_sources(q + RING, b)

                for b in range(RING):
                    list_sources(b, b)
                for h in range(0 if R else 2):
                    mark_lanes(h, h)
                if beside is None:
                    with v.Fori(0, quads // RING - 1, 1) as j:
                        for b in range(RING):
                            step(RING * j + b, b, True, True)
                    for b in range(RING):
                        step(quads - RING + b, b, b < RING - 2, False)
                else:
                    def body(q, b, share):
                        static = isinstance(q, int)
                        step(q, b, not (static and q + 2 >= quads), not (static and q + RING >= quads))
                        if share is not None and b == RING - 1:
                            for half in range(2):
                                beside.vector(v, share[0], share[1], half)
                    beside_loop(v, quads, body, beside)

            @block.gpsimd
            def _(pool):
                def body(q, b):
                    pool.wait_ge(listed, q + 1)
                    wait_after(pool, used, q + 1 - RING)
                    if kept is None:
                        wait_after(pool, spilled[b], round_of(q, b))
                    else:
                        wait_after(pool, saved, q + 1 - RING)
                    pool.sem_inc(passed, 1)
                    for k in range(K):
                        nc.gpsimd.indirect_dma_start(
                            out=rows[:, b, k, :], out_offset=None, in_=table[:, :],
                            in_offset=bass.IndirectOffsetOnAxis(ap=slot[:, b, k:k + 1], axis=0)
                        ).then_inc(gathered[b], 16)
                ring_loop(pool, quads, body)

            def spill_rows(sp):
                def body(q, b):
                    sp.wait_ge(gathered[b], K * (round_of(q, b) + 16))
                    sp.dma_start(spill[bass.ds(q, 1), :, :].rearrange("a p n -> (a p) n"),
                                 rows[:, b, :, spilled_cols]).then_inc(spilled[b], 16)
                ring_loop(sp, quads, body)
                for b in range(RING):
                    sp.wait_ge(spilled[b], 16 * quads // RING)

            if kept is None:
                block.sync(spill_rows)

            @block.tensor
            def _(pe):
                def turn(q, h):
                    pe.wait_ge(ready, q + 1)
                    wait_after(pe, copied, q - 1)
                    for k in range(K):
                        last = nc.tensor.transpose(psT[:, h, k * P:(k + 1) * P], onehot[:, h, k, :], c.identb[:, :])
                        if R:
                            last = nc.tensor.transpose(psT[0:R, h, (K + k) * P:(K + k + 1) * P], kind[:, h, k, :],
                                                       c.identb[:, :])
                    last.then_inc(turned, 1)

                registers = TileRegisters(nc, mybir.EngineType.PE, g)

                def expand(q, h):
                    tiles = registers.of(q, h)
                    pe.wait_ge(copied, q + 1)
                    wait_after(pe, used, q - 1)
                    for k in range(K):
                        n, i = k // per_bank, k % per_bank
                        for part in range(PARTS):
                            last = nc.tensor.matmul(psE[:, h, n, i * NV:(i + 1) * NV], onehotT[:, h, k, :],
                                                    nodes_flat[:, bass.ds(tiles[k] * (PARTS * NV) + part * NV, NV)],
                                                    start=(part == 0), stop=(part == PARTS - 1))
                        for part in range(PARTS if R else 0):
                            last = nc.tensor.matmul(psR[:, h, k * R:k * R + C], kindT[:, h, k, :], relation[:, part, :],
                                                    start=(part == 0), stop=(part == PARTS - 1))
                    last.then_inc(spread, 1)

                turn(0, 0)
                turn(1, 1)

                def body(q, b):
                    expand(q, b % 2)
                    if not (isinstance(q, int) and q + 2 >= quads):
                        turn(q + 2, b % 2)

                def body_beside(q, b, share):
                    body(q, b)
                    if share is not None:
                        beside.tensor(pe, *share)
                if beside is None:
                    ring_loop(pe, quads, body, peel_last=True)
                else:
                    beside_loop(pe, quads, body_beside, beside)

            @block.scalar
            def _(act):
                def marks(q, h):
                    wait_after(act, ready, q)
                    for k in range(K):
                        col = bass.ds(q * K + k, 1)
                        nc.scalar.activation(away[:, k, 0:P], c.iota[:, :], ACT.Abs, bias=g.lane[:, col], scale=-1.0)
                        nc.scalar.activation(away[:, k, P:P + R], c.iota[:, 0:R], ACT.Abs, bias=g.type[:, col],
                                             scale=-1.0).then_inc(measured, 1)
                    act.wait_ge(measured, K * (q + 1))
                    nc.scalar.activation(kind[:, h, :, :], away[:, :, P:P + R], ACT.Relu, bias=1.0, scale=-1.0)
                    nc.scalar.activation(onehot[:, h, :, :], away[:, :, 0:P], ACT.Relu, bias=1.0,
                                         scale=-1.0).then_inc(ready, 1)

                def body(q, b):
                    h = b % 2
                    act.wait_ge(turned, q + 1)
                    wait_after(act, spread, q - 1)
                    if R:
                        nc.scalar.activation(kindT[:, h, :, :],
                                             psT[0:R, h, K * P:2 * K * P].rearrange("p (k l) -> p k l", k=K), ACT.Copy)
                    nc.scalar.activation(onehotT[:, h, :, :],
                                         psT[:, h, 0:K * P].rearrange("p (k l) -> p k l", k=K),
                                         ACT.Copy).then_inc(copied, 1)
                    if kept is not None:
                        act.wait_ge(gathered[b], K * (round_of(q, b) + 16))
                        nc.scalar.activation(kept[:, bass.ds(q * K, K), 0:width], rows[:, b, :, 0:width],
                                             ACT.Copy).then_inc(saved, 1)
                    if R and not (isinstance(q, int) and q + 2 >= quads):
                        marks(q + 2, h)
                if R:
                    marks(0, 0)
                    marks(1, 1)

                def body_beside(q, b, share):
                    body(q, b)
                    if share is not None and b in (1, 2):
                        beside.scalar(act, share[0], share[1], b - 1)
                if beside is None:
                    ring_loop(act, quads, body, peel_last=bool(R))
                else:
                    beside_loop(act, quads, body_beside, beside)


def split_parts(step, values, parts, rest):
    nc = step.nc
    for k in range(PARTS):
        left = values if k == 0 else rest
        step.link(nc.vector.tensor_copy(parts[k], left))
        if k < PARTS - 1:
            step.link(nc.vector.tensor_tensor(rest, left, parts[k], ALU.subtract))


def edge_softmax(nc, c, g, name, heads, store, own, scale, room=None):
    CP, CH, H = g.cp, g.chunks, heads
    W = store.shape[2]
    assert W == (2 * H if own else H) + 1
    with ExitStack() as s:
        def sb(n, shape, dt=F32):
            return s.enter_context(nc.sbuf_tensor(f"{name}_{n}", shape, dt))

        def sem(n):
            return s.enter_context(nc.semaphore(f"{name}_{n}"))

        val = sb("val", [CP, H, 4, P])
        if room is None:
            loop = sb("loop", [CP, H, 4, P]) if own else None
            fwd = sb("fwd", [CP, H, 4, P])
            bwd = sb("bwd", [CP, H, 4, P])
            reset = sb("reset", [CP, H, 4, P])
        else:
            size = H * 4 * P
            fwd, bwd, reset, loop = (
                lent[0:CP, :, :, :].rearrange("p a b c -> p (a b c)")[:, k * size:(k + 1) * size]
                .rearrange("p (h g l) -> p h g l", h=H, g=4) for lent in room for k in range(2))
        link = sb("link", [CP, 2, 4])
        links = sb("links", [CP, 2, H, 4])
        ends = sb("ends", [H, 2, CH])
        linkT = sb("linkT", [H, 2, CH])
        state = sb("state", [H, 2, CH + 1])
        carry = sb("carry", [CP, 2, 4, H])
        kept = sb("kept", [CP, H, 4])
        into = sb("into", [CP, H, 4])
        ps = s.enter_context(nc.psum_tensor(f"{name}_ps", [P, 8, 512], F32))
        dve = sem("dve")
        scored = sem("scored")
        turned = sem("turned")
        copied = sem("copied")
        tails = sem("tails")
        tailsT = sem("tailsT")
        stated = sem("stated")
        carried = sem("carried")
        shifted = sem("shifted")
        weighted = sem("weighted")
        back = sem("back")
        stored = sem("stored")
        groups = [(0, h) for h in range(H)] + ([(1, h) for h in range(H)] if own else [])
        with nc.Block() as block:
            @block.vector
            def _(v):
                step = Steps(nc, v, dve)
                if own:
                    flat = store[:, :, 0:H]
                    nc.vector.scalar_tensor_tensor(flat, flat, SLOPE, flat, ALU.mult, ALU.max).then_inc(scored, 1)
                else:
                    nc.vector.tensor_scalar(store[:, :, 0:H], store[:, :, 0:H], scale, None, ALU.mult).then_inc(scored, 1)
                nc.vector.tensor_reduce(link[:, 0, :], g.reset_fwd[:, :, :], AX.X, ALU.min)
                step.link(nc.vector.tensor_reduce(link[:, 1, :], g.reset_bwd[:, :, :], AX.X, ALU.min))
                for h in range(H):
                    nc.vector.tensor_copy(links[:, :, h, :], link[:, :, :])
                step.link(nc.vector.memset(state[:, :, :], NEG))
                v.wait_ge(copied, len(groups))
                val_f = val[:, :, :, :].rearrange("p h g l -> p (h g l)")
                reset_f = reset[:, :, :, :].rearrange("p h g l -> p (h g l)")
                fwd_f = fwd[:, :, :, :].rearrange("p h g l -> p (h g l)")
                bwd_f = bwd[:, :, :, :].rearrange("p h g l -> p (h g l)")

                def set_reset(source, edge):
                    for h in range(H):
                        last = nc.vector.tensor_copy(reset[:, h, :, :], source[:, :, :])
                        step.mark(last)
                    v.wait_ge(dve, step.n)
                    step.link(nc.vector.memset(reset[:, :, :, edge:edge + 1], NEG))

                def scan(out, backward):
                    a = (slice(None), slice(None, None, -1)) if backward else (slice(None), slice(None))
                    step.link(nc.vector.tensor_tensor_scan(out[a], reset_f[a], val_f[a], NEG, ALU.add, ALU.max))

                def with_carry(out, side, source, edge, backward):
                    step.link(nc.vector.tensor_tensor(
                        into[:, :, :], carry[:, side, :, :].rearrange("p g h -> p h g"),
                        source[:, :, edge].unsqueeze(1).broadcast_to([CP, H, 4]), ALU.add))
                    step.link(nc.vector.tensor_copy(kept[:, :, :], val[:, :, :, edge]))
                    step.link(nc.vector.tensor_tensor(val[:, :, :, edge], kept[:, :, :], into[:, :, :], ALU.max))
                    scan(out, backward)
                    step.link(nc.vector.tensor_copy(val[:, :, :, edge], kept[:, :, :]))

                set_reset(g.reset_bwd, P - 1)
                scan(bwd_f, True)
                set_reset(g.reset_fwd, 0)
                scan(fwd_f, False)
                v.sem_inc(tails, 1)
                v.wait_ge(tailsT, 1)
                for side in range(2):
                    nc.vector.tensor_copy(ends[:, side, :], ps[0:H, side, 0:CH])
                    step.link(nc.vector.tensor_copy(linkT[:, side, :], ps[0:H, 2 + side, 0:CH]))
                step.link(nc.vector.tensor_tensor_scan(state[:, 0, 1:], linkT[:, 0, :], ends[:, 0, :], NEG,
                                                       ALU.add, ALU.max))
                step.link(nc.vector.tensor_tensor_scan(state[:, 1, 0:CH][:, ::-1], linkT[:, 1, ::-1],
                                                       ends[:, 1, ::-1], NEG, ALU.add, ALU.max))
                v.sem_inc(stated, 1)
                v.wait_ge(carried, 1)
                for side in range(2):
                    step.link(nc.vector.tensor_copy(carry[:, side, :, :],
                                                    ps[0:CP, 4 + side, 0:4 * H].rearrange("p (g h) -> p g h", g=4)))
                with_carry(fwd_f, 0, g.reset_fwd, 0, False)
                set_reset(g.reset_bwd, P - 1)
                with_carry(bwd_f, 1, g.reset_bwd, P - 1, True)
                step.link(nc.vector.tensor_tensor(fwd_f, fwd_f, bwd_f, ALU.max))
                if own:
                    loop_f = loop[:, :, :, :].rearrange("p h g l -> p (h g l)")
                    step.link(nc.vector.tensor_tensor(fwd_f, fwd_f, loop_f, ALU.max))
                nc.vector.tensor_tensor(val_f, val_f, fwd_f, ALU.subtract).then_inc(shifted, 1)
                if own:
                    nc.vector.tensor_tensor(loop_f, loop_f, fwd_f, ALU.subtract).then_inc(shifted, 1)
                    v.wait_ge(weighted, 2)
                    nc.vector.tensor_tensor(
                        loop[:, :, :, :], loop[:, :, :, :],
                        g.is_last[:, :, :].unsqueeze(1).broadcast_to([CP, H, 4, P]), ALU.mult).then_inc(shifted, 1)
                for n in range(len(groups) + 1):
                    v.wait_ge(back, n + 1)
                    nc.vector.tensor_copy(store[:, :, n], ps[:, n % 8, 0:CH]).then_inc(stored, 1)

            @block.tensor
            def _(pe):
                pe.wait_ge(scored, 1)
                for n, (side, h) in enumerate(groups):
                    if n >= 8:
                        pe.wait_ge(copied, n - 7)
                    for q in range(4):
                        last = nc.tensor.transpose(ps[0:CP, n % 8, q * P:(q + 1) * P],
                                                   store[:, q * CP:(q + 1) * CP, side * H + h], c.ident[:, :])
                    last.then_inc(turned, 1)
                pe.wait_ge(tails, 1)
                pe.wait_ge(copied, len(groups))
                for q in range(4):
                    sl = slice(q * CP, (q + 1) * CP)
                    nc.tensor.transpose(ps[0:H, 0, sl], fwd[:, :, q, P - 1], c.ident[0:CP, 0:CP])
                    nc.tensor.transpose(ps[0:H, 1, sl], bwd[:, :, q, 0], c.ident[0:CP, 0:CP])
                    for side in range(2):
                        last = nc.tensor.transpose(ps[0:H, 2 + side, sl], links[:, side, :, q], c.ident[0:CP, 0:CP])
                last.then_inc(tailsT, 1)
                pe.wait_ge(stated, 1)
                for q in range(4):
                    for side in range(2):
                        last = nc.tensor.transpose(ps[0:CP, 4 + side, q * H:(q + 1) * H],
                                                   state[:, side, q * CP + side:(q + 1) * CP + side],
                                                   c.ident[0:H, 0:H])
                last.then_inc(carried, 1)
                for n in range(len(groups) + 1):
                    if n < len(groups):
                        side, h = groups[n]
                        source = (val, loop)[side][:, h, :, :]
                        if side == 0:
                            pe.wait_ge(weighted, 1)
                        else:
                            pe.wait_ge(shifted, 3)
                    else:
                        source = g.is_last[:, :, :]
                    if n >= 8:
                        pe.wait_ge(stored, n - 7)
                    for q in range(4):
                        last = nc.tensor.transpose(ps[:, n % 8, q * CP:(q + 1) * CP], source[:, q, :],
                                                   c.ident[0:CP, 0:CP])
                    last.then_inc(back, 1)

            @block.scalar
            def _(act):
                for n, (side, h) in enumerate(groups):
                    act.wait_ge(turned, n + 1)
                    nc.scalar.activation((val, loop)[side][:, h, :, :],
                                         ps[0:CP, n % 8, :].rearrange("p (g l) -> p g l", g=4),
                                         ACT.Copy).then_inc(copied, 1)
                act.wait_ge(shifted, 1)
                nc.scalar.activation(val[:, :, :, :], val[:, :, :, :], ACT.Exp).then_inc(weighted, 1)
                if own:
                    act.wait_ge(shifted, 2)
                    nc.scalar.activation(loop[:, :, :, :], loop[:, :, :, :], ACT.Exp).then_inc(weighted, 1)


def aggregate(nc, c, g, name, heads, width, spill, store, agg, kept=None, loads=()):
    K = QUAD
    quads = g.chunks // K
    W = store.shape[2]
    AW = width + W
    BANKS = 8
    store_flat = store[:, :, :].rearrange("p c w -> p (c w)") if kept is None else None
    SUMS = agg.shape[1]
    agg_flat = agg[:, :, :, :].rearrange("p s t w -> p (s t w)")
    with ExitStack() as s:
        def sb(n, shape, dt=F32):
            return s.enter_context(nc.sbuf_tensor(f"{name}_{n}", shape, dt))

        def sem(n):
            return s.enter_context(nc.semaphore(f"{name}_{n}"))

        rows = sb("rows", [P, RING, K, AW]) if kept is None else None
        onehot = sb("onehot", [P, RING, K, P])
        ps = s.enter_context(nc.psum_tensor(f"{name}_psA", [P, BANKS, 512], F32))
        loaded = [sem(f"loaded{b}") for b in range(RING)]
        weighed = sem("weighed")
        extended = sem("extended")
        ready = sem("ready")
        summed = sem("summed")
        added = sem("added")
        zeroed = sem("zeroed")
        fetched = sem("fetched")
        with nc.Block() as block:
            def reload_rows(sp):
                def body(q, b):
                    wait_after(sp, summed, K * (q + 1 - RING))
                    sp.dma_start(rows[:, b, :, 0:width],
                                 spill[bass.ds(q, 1), :, :].rearrange("a p (k n) -> (a p) k n", k=K)
                                 ).then_inc(loaded[b], 16)
                ring_loop(sp, quads, body)

            def weigh_rows(pool):
                def body(q, b):
                    pool.wait_ge(loaded[b], round_of(q, b) + 16)
                    for k in range(K - 1):
                        per_head = rows[:, b, k, 0:width].rearrange("p (h n) -> p h n", h=heads)
                        last = nc.gpsimd.tensor_tensor(
                            per_head, per_head,
                            store_flat[:, bass.ds((q * K + k) * W, heads)].unsqueeze(2)
                            .broadcast_to([P, heads, width // heads]), ALU.mult)
                    last.then_inc(weighed, 1)
                ring_loop(pool, quads, body)

            def extend_rows(act):
                def body(q, b):
                    wait_after(act, summed, K * (q + 1 - RING))
                    nc.scalar.activation(rows[:, b, :, width:AW], store[:, bass.ds(q * K, K), :], ACT.Copy)
                    act.wait_ge(loaded[b], round_of(q, b) + 16)
                    for h in range(heads):
                        part = rows[:, b, K - 1, h * width // heads:(h + 1) * width // heads]
                        last = nc.scalar.activation(part, part, ACT.Copy,
                                                    scale=store_flat[:, bass.ds((q * K + K - 1) * W + h, 1)])
                    last.then_inc(extended, 1)
                ring_loop(act, quads, body)

            if kept is None:
                block.sync(reload_rows)
                block.gpsimd(weigh_rows)
                block.scalar(extend_rows)
            else:
                @block.sync
                def _(sp):
                    for dst, source in loads:
                        sp.dma_start(dst, source).then_inc(fetched, 16)
                    if loads:
                        sp.wait_ge(fetched, 16 * len(loads))

                @block.scalar
                def _(act):
                    def body(q, b):
                        wait_after(act, summed, K * (q + 1 - RING))
                        for k in range(K):
                            nc.scalar.activation(onehot[:, b, k, :], c.iota[:, :], ACT.Abs,
                                                 bias=g.lane[:, bass.ds(q * K + k, 1)], scale=-1.0).then_inc(extended, 1)
                        act.wait_ge(extended, K * (q + 1))
                        nc.scalar.activation(onehot[:, b, :, :], onehot[:, b, :, :], ACT.Relu, bias=1.0,
                                             scale=-1.0).then_inc(ready, 1)
                    ring_loop(act, quads, body)

                @block.gpsimd
                def _(pool):
                    per_head = kept[:, :, 0:width].rearrange("p c (h n) -> p c h n", h=heads)
                    nc.gpsimd.tensor_tensor(per_head, per_head, store[:, :, 0:heads].unsqueeze(3)
                                            .broadcast_to([P, g.chunks, heads, width // heads]),
                                            ALU.mult).then_inc(weighed, 1)

            @block.tensor
            def _(pe):
                if kept is not None:
                    pe.wait_ge(weighed, 1)
                    kept_flat = kept[:, :, :].rearrange("p c w -> p (c w)")

                def body(q, b):
                    if kept is None:
                        pe.wait_ge(weighed, q + 1)
                        pe.wait_ge(extended, q + 1)
                    pe.wait_ge(ready, q + 1)
                    for k in range(K):
                        wait_after(pe, added, K * q + k + 1 - BANKS)
                        weighted = rows[:, b, k, :] if kept is None else kept_flat[:, bass.ds((q * K + k) * AW, AW)]
                        nc.tensor.matmul(ps[:, (K * b + k) % BANKS, 0:AW], onehot[:, b, k, :], weighted,
                                         start=True, stop=True).then_inc(summed, 1)
                ring_loop(pe, quads, body)

            @block.vector
            def _(v):
                for n in range(SUMS):
                    nc.vector.memset(agg[:, n, :, :], 0.0).then_inc(zeroed, 1)

                def prepare(q, b):
                    nc.vector.tensor_tensor(
                        onehot[:, b, :, :], c.iota[:, :].unsqueeze(1).broadcast_to([P, K, P]),
                        g.lane[:, bass.ds(q * K, K)].unsqueeze(2).broadcast_to([P, K, P]),
                        ALU.is_equal).then_inc(ready, 1)

                registers = TileRegisters(nc, mybir.EngineType.DVE, g)

                def body(q, b):
                    tiles = registers.of(q, b)
                    for k in range(K):
                        v.wait_ge(summed, q * K + k + 1)
                        wait_after(v, added, q * K + k + 1 - SUMS)
                        place = agg_flat[:, bass.ds(tiles[k] * AW + k % SUMS * (NT * AW), AW)]
                        nc.vector.tensor_tensor(place, place, ps[:, (K * b + k) % BANKS, 0:AW], ALU.add).then_inc(added, 1)
                    if kept is None and not (isinstance(q, int) and q + RING - 1 >= quads):
                        prepare(q + RING - 1, (b + RING - 1) % RING)

                for b in range(RING - 1 if kept is None else 0):
                    prepare(b, b)
                v.wait_ge(zeroed, SUMS)
                ring_loop(v, quads, body, peel_last=True)
                for n in range(1, SUMS):
                    v.wait_ge(added, quads * K + n - 1)
                    nc.vector.tensor_tensor(agg[:, 0, :, :], agg[:, 0, :, :], agg[:, n, :, :], ALU.add).then_inc(added, 1)


def load_rows(sp, dst, src, sem):
    sp.dma_start(dst[:, 0:NT - 1, :], src[0:(NT - 1) * P, :].rearrange("(t p) d -> p t d", p=P)).then_inc(sem, 16)
    sp.dma_start(dst[0:LAST, NT - 1, :], src[(NT - 1) * P:N, :]).then_inc(sem, 16)


def load_x(nc, x_d, xs):
    with ExitStack() as s:
        zeroed = s.enter_context(nc.semaphore("x_zeroed"))
        loaded = s.enter_context(nc.semaphore("x_loaded"))
        with nc.Block() as block:
            @block.vector
            def _(v):
                nc.vector.memset(xs[:, NT - 1, :], 0.0).then_inc(zeroed, 1)

            @block.sync
            def _(sp):
                sp.wait_ge(zeroed, 1)
                load_rows(sp, xs, x_d, loaded)
                sp.wait_ge(loaded, 32)


def store_x(nc, xs, out_d):
    with ExitStack() as s:
        stored = s.enter_context(nc.semaphore("out_stored"))
        with nc.Block() as block:
            @block.sync
            def _(sp):
                sp.dma_start(out_d[0:(NT - 1) * P, :].rearrange("(t p) d -> p t d", p=P),
                             xs[:, 0:NT - 1, :]).then_inc(stored, 16)
                sp.dma_start(out_d[(NT - 1) * P:N, :], xs[0:LAST, NT - 1, :]).then_inc(stored, 16)
                sp.wait_ge(stored, 32)


def inverse_root(nc, v, step, x, root, asked, rooted):
    v.sem_inc(asked, 1)
    v.wait_ge(rooted, 1)
    step.link(nc.vector.reciprocal(root, root))
    step.link(nc.vector.tensor_tensor(x, x, root, ALU.mult))
    step.link(nc.vector.tensor_tensor(x, x, root, ALU.mult))
    step.link(nc.vector.tensor_scalar(x, x, -0.5, 1.5, ALU.mult, ALU.add))
    step.link(nc.vector.tensor_tensor(root, root, x, ALU.mult))


def take_root(nc, act, x, root, asked, rooted):
    act.wait_ge(asked, 1)
    nc.scalar.activation(root, x, ACT.Sqrt).then_inc(rooted, 1)


def row_statistics(nc, v, step, x, stats, moments, rstd, asked, rooted):
    for t in range(NT):
        step.mark(nc.vector.bn_stats(stats[:, t, :], x[:, t, :]))
    v.wait_ge(step.sem, step.n)
    for t in range(NT):
        step.mark(nc.vector.bn_aggr(moments[:, t, :], stats[:, t, :]))
    v.wait_ge(step.sem, step.n)
    step.link(nc.vector.tensor_scalar(moments[:, :, 1], moments[:, :, 1], LN_EPS, None, ALU.add))
    inverse_root(nc, v, step, moments[:, :, 1], rstd[:, :], asked, rooted)


def turn_and_project(nc, c, name, x, xT, norm, normed=None, shift=None, loads=(), fold=None, projections=(),
                     later_loads=()):
    with ExitStack() as s:
        def sb(n, shape, dt=F32):
            return s.enter_context(nc.sbuf_tensor(f"{name}_{n}", shape, dt))

        def sem(n):
            return s.enter_context(nc.semaphore(f"{name}_{n}"))

        psX = s.enter_context(nc.psum_tensor(f"{name}_psX", [P, 4, 512], F32))
        psP = s.enter_context(nc.psum_tensor(f"{name}_psP", [P, 4, 512], F32))
        dve, ready, turned, copied = sem("dve"), sem("ready"), sem("turned"), sem("copied")
        asked, rooted = sem("asked"), sem("rooted")
        loaded, loaded_later, folded = sem("loaded"), sem("loaded_later"), sem("folded")
        made, taken, chain, sent = sem("made"), sem("taken"), sem("chain"), sem("sent")
        src = x
        if norm:
            stats = sb("stats", [P, NT, 6])
            moments = sb("moments", [P, NT, 2])
            rstd = sb("rstd", [P, NT])
            src = normed if normed is not None else sb("normed", [P, NT, D])
        groups = [(t0, min(4, NT - t0)) for t0 in range(0, NT, 4)]
        each = len(projections)
        by_vector = any(bias is not None for _, bias, _, _, _ in projections)
        tables = [(out, table) for _, _, _, out, table in projections if table is not None]

        def take(eng, i, emit):
            t0, w = groups[i]
            for t in range(t0, t0 + w):
                for j in range(each):
                    n = t * each + j
                    eng.wait_ge(made, n + 1)
                    emit(j, t, psP[:, n % 4, 0:projections[j][0].shape[2]]).then_inc(taken, 1)

        with nc.Block() as block:
            @block.sync
            def _(sp):
                for dst, source in loads:
                    sp.dma_start(dst, source, allow_slow_non_contiguous=True).then_inc(loaded, 16)
                for dst, source in later_loads:
                    sp.dma_start(dst, source, allow_slow_non_contiguous=True).then_inc(loaded_later, 16)
                for t0, w in groups if tables else ():
                    sp.wait_ge(taken, (t0 + w) * each)
                    for out, table in tables:
                        sp.dma_start(table.rearrange("(t p) n -> p t n", p=P)[:, t0:t0 + w, :],
                                     out[:, t0:t0 + w, 0:table.shape[1]]).then_inc(sent, 16)
                if loads:
                    sp.wait_ge(loaded, 16 * len(loads))
                if later_loads:
                    sp.wait_ge(loaded_later, 16 * len(later_loads))
                if tables:
                    sp.wait_ge(sent, 16 * len(groups) * len(tables))

            @block.vector
            def _(v):
                step = Steps(nc, v, dve)

                def normalize(i):
                    t0, w = groups[i]
                    for t in range(t0, t0 + w):
                        nc.vector.tensor_scalar(src[:, t, :], x[:, t, :], moments[:, t, 0:1], rstd[:, t:t + 1],
                                                ALU.subtract, ALU.mult).then_inc(ready, 1)

                if norm:
                    row_statistics(nc, v, step, x, stats, moments, rstd, asked, rooted)
                    normalize(0)
                if fold is not None:
                    v.wait_ge(loaded, 16 * len(loads))
                    fold(step)
                    v.sem_inc(folded, 1)
                vector_chain = Steps(nc, v, chain)

                def emit(j, t, got):
                    _, bias, add, out, _ = projections[j]
                    if bias is None:
                        return nc.vector.tensor_copy(out[:, t, :], got)
                    last = nc.vector.tensor_tensor(out[:, t, :], got, bias, ALU.add)
                    if add is not None:
                        vector_chain.link(last)
                        last = nc.vector.tensor_tensor(out[:, t, :], out[:, t, :], add[:, t, :], ALU.add)
                    return last

                if by_vector:
                    v.wait_ge(loaded, 16 * len(loads))
                for i in range(len(groups)):
                    if norm and i + 1 < len(groups):
                        normalize(i + 1)
                    if by_vector and i:
                        take(v, i - 1, emit)
                if by_vector:
                    take(v, len(groups) - 1, emit)

            @block.tensor
            def _(pe):
                def turn(i):
                    t0, w = groups[i]
                    if norm:
                        pe.wait_ge(ready, t0 + w)
                    for k in range(KD):
                        n = i * KD + k
                        wait_after(pe, copied, n - 3)
                        for j in range(w):
                            last = nc.tensor.transpose(psX[:, n % 4, j * P:(j + 1) * P],
                                                       src[:, t0 + j, k * P:(k + 1) * P], c.ident[:, :])
                        last.then_inc(turned, 1)

                def project(i):
                    t0, w = groups[i]
                    pe.wait_ge(copied, (i + 1) * KD)
                    for t in range(t0, t0 + w):
                        for j, (weights, _, _, _, _) in enumerate(projections):
                            n = t * each + j
                            wait_after(pe, taken, n - 3)
                            for k in range(KD):
                                last = nc.tensor.matmul(psP[:, n % 4, 0:weights.shape[2]], xT[:, k, t * P:(t + 1) * P],
                                                        weights[:, k, :], start=(k == 0), stop=(k == KD - 1))
                            last.then_inc(made, 1)

                turn(0)
                turn(1)
                if projections:
                    if fold is not None:
                        pe.wait_ge(folded, 1)
                    elif loads:
                        pe.wait_ge(loaded, 16 * len(loads))
                for i in range(len(groups)):
                    if projections:
                        project(i)
                    if i + 2 < len(groups):
                        turn(i + 2)

            @block.scalar
            def _(act):
                if norm:
                    take_root(nc, act, moments[:, :, 1], rstd[:, :], asked, rooted)

                def copy(i):
                    t0, w = groups[i]
                    for k in range(KD):
                        n = i * KD + k
                        act.wait_ge(turned, n + 1)
                        out = xT[:, k, t0 * P:(t0 + w) * P]
                        if shift is None:
                            nc.scalar.activation(out, psX[:, n % 4, 0:w * P], ACT.Copy).then_inc(copied, 1)
                        else:
                            nc.scalar.activation(out, psX[:, n % 4, 0:w * P], ACT.Identity,
                                                 bias=shift[:, k:k + 1]).then_inc(copied, 1)

                def emit(j, t, got):
                    return nc.scalar.activation(projections[j][3][:, t, :], got, ACT.Copy)

                copy(0)
                copy(1)
                for i in range(len(groups)):
                    if projections and not by_vector:
                        take(act, i, emit)
                    if i + 2 < len(groups):
                        copy(i + 2)


def load_weights(nc, name, loads):
    with ExitStack() as s:
        loaded = s.enter_context(nc.semaphore(f"{name}_loaded"))
        with nc.Block() as block:
            @block.sync
            def _(sp):
                for dst, src in loads:
                    sp.dma_start(dst, src, allow_slow_non_contiguous=True).then_inc(loaded, 16)
                sp.wait_ge(loaded, 16 * len(loads))


def by_halves(w):
    return w.rearrange("(k p) n -> p k n", p=P)


def spread_row(v):
    n = v.shape[0]
    return v.rearrange("(a n) -> a n", a=1).broadcast_to([P, n])


def graph_attention(nc, c, g, name, x, norm, W, att_src, att_dst, bias, heads, scratch, out, load=None, kept_xT=None,
                    more_loads=(), beside=None, normed=None, room=None, reloads=()):
    HC = W.shape[1]
    H = heads
    C = HC // H
    with ExitStack() as s:
        def sb(n, shape, dt=F32):
            return s.enter_context(nc.sbuf_tensor(f"{name}_{n}", shape, dt))

        def sem(n):
            return s.enter_context(nc.semaphore(f"{name}_{n}"))

        rows = sb("noderows", [P, NT, HC + 2 * H])
        node_vals = sb("node_vals", [P, NT, 2 * H])
        node_parts = sb("node_parts", [P, NT, PARTS, 2 * H], BF16)
        kept = sb("kept", [P, g.chunks, HC + 2 * H + 1]) if HC < P else None
        store = kept[:, :, HC:] if HC < P else sb("store", [P, g.chunks, 2 * H + 1])
        bias_row = sb("bias_row", [P, HC])
        table = scratch["table"][0:NP * (HC + H)].rearrange("(n w) -> n w", w=HC + H)
        spill = scratch["spill"][0:g.chunks * P * HC].rearrange("(q p n) -> q p n", p=P, n=QUAD * HC)
        with ExitStack() as w:
            weights = w.enter_context(nc.sbuf_tensor(f"{name}_weights", [P, KD, HC + 2 * H], F32))
            att = w.enter_context(nc.sbuf_tensor(f"{name}_att", [P, 2, HC], F32))
            prod = w.enter_context(nc.sbuf_tensor(f"{name}_prod", [P, 2 * KD, HC], F32))
            xT = kept_xT if kept_xT is not None else w.enter_context(nc.sbuf_tensor(f"{name}_xT", [P, KD, NP], F32))

            def fold(step):
                for n in range(2 * KD):
                    step.mark(nc.vector.tensor_tensor(prod[:, n, :], weights[:, n // 2, 0:HC], att[:, n % 2, :], ALU.mult))
                step.eng.wait_ge(step.sem, step.n)
                for n in range(2 * KD):
                    k, a = n // 2, n % 2
                    step.mark(nc.vector.tensor_reduce(
                        weights[:, k, HC + a * H:HC + (a + 1) * H],
                        prod[:, n, :].rearrange("p (h c) -> p h c", h=H), AX.X, ALU.add))
                step.eng.wait_ge(step.sem, step.n)

            turn_and_project(nc, c, f"{name}_h", x, xT, norm, normed=normed, loads=[
                (weights[:, :, 0:HC], by_halves(W)),
                (att[:, 0, :], spread_row(att_src.rearrange("h c -> (h c)"))),
                (att[:, 1, :], spread_row(att_dst.rearrange("h c -> (h c)"))),
                (bias_row[:, :], spread_row(bias))], later_loads=more_loads, fold=fold,
                projections=[(weights, None, None, rows, table)])
        own = sem("own")
        with nc.Block() as block:
            @block.vector
            def _(v):
                step = Steps(nc, v, own)
                s_part, d_part = rows[:, :, HC:HC + H], rows[:, :, HC + H:HC + 2 * H]
                nc.vector.tensor_copy(node_vals[:, :, 0:H], d_part)
                step.link(nc.vector.tensor_tensor(node_vals[:, :, H:2 * H], s_part, d_part, ALU.add))
                step.link(nc.vector.scalar_tensor_tensor(node_vals[:, :, H:2 * H], node_vals[:, :, H:2 * H], SLOPE,
                                                         node_vals[:, :, H:2 * H], ALU.mult, ALU.max))
                split_parts(step, node_vals[:, :, :], [node_parts[:, :, k, :] for k in range(PARTS)],
                            node_vals[:, :, :])
        gather_scores(nc, c, g, f"{name}_a", table, spill, node_parts, 2 * H, H, HC, store, kept=kept, beside=beside)
        edge_softmax(nc, c, g, f"{name}_b", H, store, True, 1.0, room=room)
        partial = sb("agg", [P, 2 if HC > P else 4, NT, HC + 2 * H + 1])
        agg = partial[:, 0, :, :]
        aggregate(nc, c, g, f"{name}_c", H, HC, spill, store, partial, kept=kept, loads=reloads)
        loops = sb("loops", [P, NT, H])
        recip = sb("recip", [P, NT, H])
        fin, pool_fin, shares = sem("fin"), sem("pool_fin"), sem("shares")
        SPLIT = NT if HC < P else 2 * NT // 3

        def finish(ns, t0, t1, step):
            def per_head(a):
                return a[:, t0:t1, :].rearrange("p t (h c) -> p t h c", h=H)

            def spread(a):
                return a[:, t0:t1, :].unsqueeze(3).broadcast_to([P, t1 - t0, H, C])

            h_rows, mine = per_head(rows[:, :, 0:HC]), rows[:, t0:t1, 0:HC]
            step.link(ns.tensor_tensor(h_rows, h_rows, spread(loops[:, :, :]), ALU.mult))
            step.link(ns.tensor_tensor(mine, mine, agg[:, t0:t1, 0:HC], ALU.add))
            step.link(ns.tensor_tensor(h_rows, h_rows, spread(recip[:, :, :]), ALU.mult))
            step.link(ns.tensor_tensor(mine, mine, bias_row[:, :].unsqueeze(1).broadcast_to([P, t1 - t0, HC]), ALU.add))

        with nc.Block() as block:
            @block.vector
            def _(v):
                step = Steps(nc, v, fin)
                den = agg[:, :, HC:HC + H]
                own_w = agg[:, :, HC + H:HC + 2 * H]
                has = agg[:, :, HC + 2 * H:HC + 2 * H + 1].broadcast_to([P, NT, H])
                step.link(nc.vector.tensor_tensor(loops[:, :, :], own_w, has, ALU.subtract))
                step.link(nc.vector.tensor_scalar(loops[:, :, :], loops[:, :, :], 1.0, None, ALU.add))
                step.link(nc.vector.tensor_tensor(recip[:, :, :], den, loops[:, :, :], ALU.add))
                step.link(nc.vector.tensor_scalar(recip[:, :, :], recip[:, :, :], SOFT_EPS, None, ALU.add))
                step.link(nc.vector.reciprocal(recip[:, :, :], recip[:, :, :]))

                v.sem_inc(shares, 1)
                finish(nc.vector, 0, SPLIT, step)
                v.wait_ge(pool_fin, 1 if HC < P else 4)
                out(step, rows[:, :, 0:HC])

            @block.gpsimd
            def _(pool):
                pool.wait_ge(shares, 1)
                if HC < P:
                    pool.sem_inc(pool_fin, 1)
                else:
                    finish(nc.gpsimd, SPLIT, NT, Steps(nc, pool, pool_fin))

            if load is not None:
                @block.sync
                def _(sp):
                    load(sp)


def relation_attention(nc, c, g, w, xs, scratch):
    H = 4
    C = D // H
    with ExitStack() as s:
        def sb(n, shape, dt=F32):
            return s.enter_context(nc.sbuf_tensor(f"r_{n}", shape, dt))

        def sem(n):
            return s.enter_context(nc.semaphore(f"r_{n}"))

        normed = sb("normed", [P, NT, D])
        relation = sb("relation", [w["L1_gnn_rel_w"].shape[0], C])
        relation_parts = sb("relation_parts", [w["L1_gnn_rel_w"].shape[0], PARTS, C], BF16)
        store = sb("store", [P, g.chunks, H + 1])
        table = scratch["table"][0:NP * 2 * D].rearrange("(n w) -> n w", w=2 * D)
        spill = scratch["spill"][0:g.chunks * P * D].rearrange("(q p n) -> q p n", p=P, n=QUAD * D)
        shift = sb("shift", [P, KD])
        prep = sem("prep")
        split = sem("split")
        with ExitStack() as q:
            query = q.enter_context(nc.sbuf_tensor("r_query", [P, NT, D], F32))
            with ExitStack() as t:
                xT = t.enter_context(nc.sbuf_tensor("r_xT", [P, KD, NP], F32))
                wq = t.enter_context(nc.sbuf_tensor("r_wq", [P, KD, D], F32))
                bq = t.enter_context(nc.sbuf_tensor("r_bq", [P, D], F32))
                wkv = t.enter_context(nc.sbuf_tensor("r_wkv", [P, KD, 2 * D], F32))
                bkv = t.enter_context(nc.sbuf_tensor("r_bkv", [P, 2 * D], F32))
                kv = t.enter_context(nc.sbuf_tensor("r_kv", [P, NT, 2 * D], F32))
                load_weights(nc, "r_w", [
                    (shift[:, :], w["L1_gnn_query_emb"].rearrange("(k p) -> p k", p=P)),
                    (relation[:, :], w["L1_gnn_rel_w"])])
                with nc.Block() as block:
                    @block.vector
                    def _(v):
                        step = Steps(nc, v, prep)
                        step.link(nc.vector.tensor_scalar(shift[:, :], shift[:, :], 0.1, None, ALU.mult))
                        step.link(nc.vector.tensor_scalar(relation[:, :], relation[:, :], 0.2, None, ALU.mult))
                turn_and_project(nc, c, "r_n", xs, xT, True, normed=normed, shift=shift, loads=[
                    (wq[:, :, :], by_halves(w["L1_gnn_Wq"])), (bq[:, :], spread_row(w["L1_gnn_bq"])),
                    (wkv[:, :, 0:D], by_halves(w["L1_gnn_Wk"])), (wkv[:, :, D:2 * D], by_halves(w["L1_gnn_Wv"])),
                    (bkv[:, 0:D], spread_row(w["L1_gnn_bk"])), (bkv[:, D:2 * D], spread_row(w["L1_gnn_bv"]))],
                    projections=[(wq, bq[:, :], None, query, None), (wkv, bkv[:, :], None, kv, table)])
            query_parts = q.enter_context(nc.sbuf_tensor("r_query_parts", [P, NT, PARTS, D], BF16))
            with nc.Block() as block:
                @block.vector
                def _(v):
                    step = Steps(nc, v, split)
                    split_parts(step, query[:, :, :], [query_parts[:, :, k, :] for k in range(PARTS)], query[:, :, :])
                    split_parts(step, relation[:, :], [relation_parts[:, k, :] for k in range(PARTS)], relation[:, :])
            gather_scores(nc, c, g, "r_a", table, spill, query_parts, D, H, D, store, relation=relation_parts)
        edge_softmax(nc, c, g, "r_b", H, store, False, 1.0 / C ** 0.5)
        msgs = sb("msgs", [P, NT, D])
        wo = sb("wo", [P, KD, D])
        rows3 = sb("rows3", [P, 3, D])
        load_weights(nc, "r_o", [(msgs[:, :, :], table.rearrange("(t p) n -> p t n", p=P)[:, :, D:2 * D])])
        with ExitStack() as a:
            partial = a.enter_context(nc.sbuf_tensor("r_agg", [P, 2, NT, D + H + 1], F32))
            agg = partial[:, 0, :, :]
            aggregate(nc, c, g, "r_c", H, D, spill, store, partial)
            lone = a.enter_context(nc.sbuf_tensor("r_lone", [P, NT, 1], F32))
            recip = a.enter_context(nc.sbuf_tensor("r_recip", [P, NT, H], F32))
            fin = sem("fin")
            with nc.Block() as block:
                @block.vector
                def _(v):
                    step = Steps(nc, v, fin)
                    step.link(nc.vector.tensor_scalar(lone[:, :, :], agg[:, :, D + H:D + H + 1], -1.0, 1.0,
                                                      ALU.mult, ALU.add))
                    step.link(nc.vector.tensor_tensor(recip[:, :, :], agg[:, :, D:D + H],
                                                      lone[:, :, :].broadcast_to([P, NT, H]), ALU.add))
                    step.link(nc.vector.reciprocal(recip[:, :, :], recip[:, :, :]))
                    step.mark(nc.vector.tensor_tensor(msgs[:, :, :], msgs[:, :, :],
                                                      lone[:, :, :].broadcast_to([P, NT, D]), ALU.mult))
                    part = agg[:, :, 0:D].rearrange("p t (h c) -> p t h c", h=H)
                    step.link(nc.vector.tensor_tensor(part, part, recip[:, :, :].unsqueeze(3).broadcast_to([P, NT, H, C]),
                                                      ALU.mult))
                    step.link(nc.vector.tensor_tensor(msgs[:, :, :], msgs[:, :, :], agg[:, :, 0:D], ALU.add))
        mT = sb("mT", [P, KD, NP])
        final = sb("final", [P, NT, D])
        turn_and_project(nc, c, "r_m", msgs, mT, False, loads=[
            (wo[:, :, :], by_halves(w["L1_gnn_Wo"])), (rows3[:, 0, :], spread_row(w["L1_gnn_bo"])),
            (rows3[:, 1, :], spread_row(w["L1_gnn_gamma"])), (rows3[:, 2, :], spread_row(w["L1_gnn_beta"]))],
            projections=[(wo, rows3[:, 0, :], normed, final, None)])
        stats, moments, rstd = sb("stats", [P, NT, 6]), sb("moments", [P, NT, 2]), sb("rstd", [P, NT])
        last_norm, asked, rooted = sem("last_norm"), sem("asked"), sem("rooted")
        normalized, pool_rows = sem("normalized"), sem("pool_rows")
        SPLIT = 2 * NT // 3

        def scale_and_add(ns, step, t0, t1):
            for row, op in ((1, ALU.mult), (2, ALU.add)):
                step.link(ns.tensor_tensor(final[:, t0:t1, :], final[:, t0:t1, :],
                                           rows3[:, row, :].unsqueeze(1).broadcast_to([P, t1 - t0, D]), op))
            step.link(ns.tensor_tensor(xs[:, t0:t1, :], xs[:, t0:t1, :], final[:, t0:t1, :], ALU.add))

        with nc.Block() as block:
            @block.vector
            def _(v):
                step = Steps(nc, v, last_norm)
                row_statistics(nc, v, step, final, stats, moments, rstd, asked, rooted)
                for t in range(NT):
                    step.mark(nc.vector.tensor_scalar(final[:, t, :], final[:, t, :], moments[:, t, 0:1],
                                                      rstd[:, t:t + 1], ALU.subtract, ALU.mult))
                v.wait_ge(last_norm, step.n)
                v.sem_inc(normalized, 1)
                scale_and_add(nc.vector, step, 0, SPLIT)
                v.wait_ge(pool_rows, 3)

            @block.gpsimd
            def _(pool):
                pool.wait_ge(normalized, 1)
                scale_and_add(nc.gpsimd, Steps(nc, pool, pool_rows), SPLIT, NT)

            @block.scalar
            def _(act):
                take_root(nc, act, moments[:, :, 1], rstd[:, :], asked, rooted)


def top_two_gates(nc, c, w, xs, xT, g, scratch, gate, loads, beside, expert_weights):
    H, E = 4, 4
    with ExitStack() as s:
        def sb(n, shape, dt=F32):
            return s.enter_context(nc.sbuf_tensor(f"t_{n}", shape, dt))

        HE = H * E
        ln = sb("ln", [P, 2, HE])
        work = sb("work", [P, NT, HE])
        def keep(step, got):
            step.link(nc.vector.tensor_copy(work[:, :, :], got))

        graph_attention(nc, c, g, "t", xs, True, w["L0_ffn_W_gat"], w["L0_ffn_att_src"], w["L0_ffn_att_dst"],
                        w["L0_ffn_b_gat"], H, scratch, keep, kept_xT=xT,
                        more_loads=[(ln[:, 0, :], spread_row(w["L0_ffn_ln_gamma"])),
                                    (ln[:, 1, :], spread_row(w["L0_ffn_ln_beta"]))] + loads, beside=beside,
                        normed=beside.y[:, :, :, :].rearrange("p t e d -> p (t e) d")[:, 0:NT, :],
                        room=(beside.w1, beside.w2), reloads=expert_weights)
        col = sb("col", [P, 12, NT])
        score = sb("score", [P, NT, E])
        picks = sb("picks", [P, 2, NT, E])
        equal = sb("equal", [P, NT, E])
        sq = sb("square", [P, NT, HE])
        gates = s.enter_context(nc.semaphore("t_gates"))
        gap_ready = s.enter_context(nc.semaphore("t_gap_ready"))
        gap_exp = s.enter_context(nc.semaphore("t_gap_exp"))
        asked = s.enter_context(nc.semaphore("t_asked"))
        rooted = s.enter_context(nc.semaphore("t_rooted"))
        with nc.Block() as block:
            mean, var, rstd, top1, top2, seen, free, gap, p2, w1, w2, spare = (col[:, k, :] for k in range(12))

            @block.vector
            def _(v):
                step = Steps(nc, v, gates)

                def wide(a, n):
                    return a.unsqueeze(2).broadcast_to([P, NT, n])

                step.link(nc.vector.tensor_reduce(mean, work[:, :, :], AX.X, ALU.add))
                step.link(nc.vector.tensor_scalar(mean, mean, 1.0 / HE, None, ALU.mult))
                step.link(nc.vector.tensor_tensor(work[:, :, :], work[:, :, :], wide(mean, HE), ALU.subtract))
                step.link(nc.vector.tensor_tensor(sq[:, :, :], work[:, :, :], work[:, :, :], ALU.mult))
                step.link(nc.vector.tensor_reduce(var, sq[:, :, :], AX.X, ALU.add))
                step.link(nc.vector.tensor_scalar(var, var, 1.0 / HE, LN_EPS, ALU.mult, ALU.add))
                inverse_root(nc, v, step, var, rstd, asked, rooted)
                step.link(nc.vector.tensor_tensor(work[:, :, :], work[:, :, :], wide(rstd, HE), ALU.mult))
                for k, op in ((0, ALU.mult), (1, ALU.add)):
                    step.link(nc.vector.tensor_tensor(work[:, :, :], work[:, :, :],
                                                      ln[:, k, :].unsqueeze(1).broadcast_to([P, NT, HE]), op))
                step.link(nc.vector.tensor_reduce(score[:, :, :], work[:, :, :].rearrange("p t (h e) -> p t e h", h=H),
                                                  AX.X, ALU.add))
                step.link(nc.vector.tensor_scalar(score[:, :, :], score[:, :, :], 1.0 / H, None, ALU.mult))
                for n, top in enumerate((top1, top2)):
                    step.link(nc.vector.tensor_reduce(top, score[:, :, :], AX.X, ALU.max))
                    step.link(nc.vector.tensor_tensor(equal[:, :, :], score[:, :, :], wide(top, E), ALU.is_equal))
                    step.link(nc.vector.memset(free, 1.0))
                    for e in range(E):
                        step.link(nc.vector.tensor_tensor(picks[:, n, :, e], equal[:, :, e], free, ALU.mult))
                        step.link(nc.vector.tensor_tensor(free, free, picks[:, n, :, e], ALU.subtract))
                    if n == 0:
                        step.link(nc.vector.scalar_tensor_tensor(score[:, :, :], picks[:, 0, :, :], NEG,
                                                                 score[:, :, :], ALU.mult, ALU.add))
                nc.vector.tensor_tensor(gap, top2, top1, ALU.subtract).then_inc(gap_ready, 1)
                v.wait_ge(gap_exp, 1)
                step.link(nc.vector.tensor_scalar(w1, p2, 1.0, None, ALU.add))
                step.link(nc.vector.reciprocal(w1, w1))
                step.link(nc.vector.tensor_tensor(w2, p2, w1, ALU.mult))
                step.link(nc.vector.tensor_tensor(picks[:, 0, :, :], picks[:, 0, :, :], wide(w1, E), ALU.mult))
                step.link(nc.vector.tensor_tensor(picks[:, 1, :, :], picks[:, 1, :, :], wide(w2, E), ALU.mult))
                step.link(nc.vector.tensor_tensor(gate[:, :, :], picks[:, 0, :, :], picks[:, 1, :, :], ALU.add))

            @block.scalar
            def _(act):
                take_root(nc, act, var, rstd, asked, rooted)
                act.wait_ge(gap_ready, 1)
                nc.scalar.activation(p2, gap, ACT.Exp).then_inc(gap_exp, 1)


def experts(nc, c, name, xT, xs, gate, stages, last_w, last_b, ready_y=None):
    E = gate.shape[2]
    with ExitStack() as s:
        def sb(n, shape, dt=F32):
            return s.enter_context(nc.sbuf_tensor(f"{name}_{n}", shape, dt))

        def sem(n):
            return s.enter_context(nc.semaphore(f"{name}_{n}"))

        gateT = sb("gateT", [E, NP])
        psA = s.enter_context(nc.psum_tensor(f"{name}_psH", [P, 4, 512], F32))
        psB = s.enter_context(nc.psum_tensor(f"{name}_psY", [P, 2, 2, 512], F32))
        turned, copied, biased, taken = sem("turned"), sem("copied"), sem("biased"), sem("taken")
        with nc.Block() as block:
            @block.tensor
            def _(pe):
                for t in range(NT):
                    wait_after(pe, copied, t - 3)
                    nc.tensor.transpose(psA[0:E, t % 4, 0:P], gate[:, t, :], c.ident[:, :]).then_inc(turned, 1)
                for t in range(NT):
                    pe.wait_ge(copied, t + 1)
                    wait_after(pe, taken, t - 1)
                    nc.tensor.matmul(psB[:, t % 2, 0, 0:D], gateT[:, t * P:(t + 1) * P], last_b[:, :], start=True,
                                     stop=True).then_inc(biased, 1)

            @block.scalar
            def _(act):
                for t in range(NT):
                    act.wait_ge(turned, t + 1)
                    nc.scalar.activation(gateT[:, t * P:(t + 1) * P], psA[0:E, t % 4, 0:P], ACT.Copy).then_inc(copied, 1)

            @block.vector
            def _(v):
                for t in range(NT):
                    v.wait_ge(biased, t + 1)
                    nc.vector.tensor_tensor(xs[:, t, :], xs[:, t, :], psB[:, t % 2, 0, 0:D], ALU.add).then_inc(taken, 1)

        B = 4
        L = len(stages)
        outs = [st[0].shape[3] // P for st in stages]
        banks = [sum(outs[:i]) for i in range(L)]
        assert sum(outs) == 4
        bufs = [sb(f"hidden{i}", [P, 2, m, B * P]) for i, m in enumerate(outs)]
        made = [sem(f"made{i}") for i in range(L)]
        shaped = [sem(f"shaped{i}") for i in range(L)]
        finished, added = sem("finished"), sem("added")
        weighed = sem("weighed")
        xs_flat = xs[:, :, :].rearrange("p t d -> p (t d)")
        gate_flat = gate[:, :, :].rearrange("p t e -> p (t e)")
        ready_tiles = 0 if ready_y is None else ready_y.shape[1]
        FIRST = ready_tiles // B
        whole = (NT - ready_tiles) // B
        rest = NT - ready_tiles - whole * B

        def blocks_loop(eng, body):
            body(0, B)
            with eng.Fori(1, whole, 1) as j:
                body(j, B)
            if rest:
                body(whole, rest)

        def staggered(layer_step, last_step):
            for n in range(E + L):
                for layer in range(L):
                    if 0 <= n - layer < E:
                        layer_step(n - layer, layer)
                if last_step is not None and n >= L:
                    last_step(n - L)

        with nc.Block() as block:
            @block.tensor
            def _(pe):
                def body(blk, tiles):
                    def hidden(e, layer):
                        item = blk * E + e
                        weights = stages[layer][0]
                        inputs = weights.shape[2]
                        if layer:
                            pe.wait_ge(shaped[layer - 1], (item + 1) * outs[layer - 1])
                        for m in range(outs[layer]):
                            wait_after(pe, shaped[layer], (item - 1) * outs[layer] + m + 1)
                            for k in range(inputs):
                                if layer == 0:
                                    src = xT[:, k, bass.ds((blk + FIRST) * (B * P), tiles * P)]
                                else:
                                    src = bufs[layer - 1][:, e % 2, k, 0:tiles * P]
                                last = nc.tensor.matmul(psA[:, banks[layer] + m, 0:tiles * P],
                                                        weights[:, e, k, m * P:(m + 1) * P], src,
                                                        start=(k == 0), stop=(k == inputs - 1))
                            last.then_inc(made[layer], 1)

                    def final(e):
                        item = blk * E + e
                        pe.wait_ge(shaped[L - 1], (item + 1) * outs[L - 1])
                        wait_after(pe, added, item - 1)
                        inputs = last_w.shape[2]
                        for t in range(tiles):
                            for k in range(inputs):
                                last = nc.tensor.matmul(psB[:, e % 2, t // 2, (t % 2) * D:(t % 2 + 1) * D],
                                                        bufs[-1][:, e % 2, k, t * P:(t + 1) * P], last_w[:, e, k, :],
                                                        start=(k == 0), stop=(k == inputs - 1))
                        last.then_inc(finished, 1)

                    staggered(hidden, final)
                blocks_loop(pe, body)

            @block.scalar
            def _(act):
                def body(blk, tiles):
                    def shape(e, layer):
                        item = blk * E + e
                        _, func, scale, bias = stages[layer]
                        if layer == L - 1:
                            wait_after(act, finished, item - 1)
                        else:
                            wait_after(act, made[layer + 1], (item - 1) * outs[layer + 1])
                        for m in range(outs[layer]):
                            act.wait_ge(made[layer], item * outs[layer] + m + 1)
                            nc.scalar.activation(
                                bufs[layer][:, e % 2, m, 0:tiles * P], psA[:, banks[layer] + m, 0:tiles * P], func,
                                bias=bias[:, e, m:m + 1],
                                scale=1.0 if scale is None else scale[:, e, m:m + 1]).then_inc(shaped[layer], 1)
                    staggered(shape, None)
                blocks_loop(act, body)

            @block.vector
            def _(v):
                def body(blk, tiles):
                    for e in range(E):
                        item = blk * E + e
                        v.wait_ge(finished, item + 1)
                        wait_after(v, added, item)
                        for t in range(tiles):
                            tile = (blk + FIRST) * B + t
                            rows = xs_flat[:, bass.ds(tile * D, D)]
                            last = nc.vector.scalar_tensor_tensor(
                                rows, psB[:, e % 2, t // 2, (t % 2) * D:(t % 2 + 1) * D],
                                gate_flat[:, bass.ds(tile * E + e, 1)], rows, ALU.mult, ALU.add)
                        last.then_inc(added, 1)

                step = Steps(nc, v, weighed)
                for e in range(E if ready_tiles else 0):
                    for t in range(ready_tiles):
                        step.mark(nc.vector.scalar_tensor_tensor(xs[:, t, :], ready_y[:, t, e, :], gate[:, t, e:e + 1],
                                                                 xs[:, t, :], ALU.mult, ALU.add))
                    v.wait_ge(weighed, step.n)
                blocks_loop(v, body)


def feed_forward_top_two(nc, c, g2, w, xs, scratch):
    E, F = 4, 512
    with ExitStack() as s:
        def sb(n, shape, dt=F32):
            return s.enter_context(nc.sbuf_tensor(f"f_{n}", shape, dt))

        xT = sb("xT", [P, KD, NP])
        gate = sb("gate", [P, NT, E])
        y = sb("y", [P, 3 * 4, E, D])
        w1 = sb("w1", [P, E, KD, F])
        w2 = sb("w2", [P, E, F // P, D])
        b1 = sb("b1", [P, E, F // P])
        b2 = sb("b2", [E, D])
        expert_weights = [
            (w1[:, e, :, :], by_halves(w["L0_ffn_W1"][e])) for e in range(E)] + [
            (w2[:, e, :, :], by_halves(w["L0_ffn_W2"][e])) for e in range(E)]
        top_two_gates(nc, c, w, xs, xT, g2, scratch, gate, expert_weights + [
            (b1[:, :, :], w["L0_ffn_b1"].rearrange("e (m p) -> p e m", p=P)),
            (b2[:, :], w["L0_ffn_b2"])], ExpertsBeside(xT, w1, b1, w2, y), expert_weights)
        experts(nc, c, "f_e", xT, xs, gate, [(w1, ACT.Gelu, None, b1)], w2, b2, ready_y=y)


def feed_forward_all(nc, c, w, xs):
    E = 8
    eps = 0.001
    with ExitStack() as s:
        def sb(n, shape, dt=F32):
            return s.enter_context(nc.sbuf_tensor(f"l_{n}", shape, dt))

        def sem(n):
            return s.enter_context(nc.semaphore(f"l_{n}"))

        xT = sb("xT", [P, KD, NP])
        gate = sb("gate", [P, NT, E])
        wr = sb("wr", [P, KD, E])
        br = sb("br", [P, E])
        w1, w2, wo = (sb(n, [P, E, KD, D]) for n in ("w1", "w2", "wo"))
        bn = sb("bn", [P, 2, 5, E, KD])
        scale = sb("scale", [P, 2, E, KD])
        bias = sb("bias", [P, 2, E, KD])
        bo = sb("bo", [E, D])
        loads = [(bo[:, :], w["L1_ffn_bo"])]
        for e in range(E):
            loads += [(w1[:, e, :, :], by_halves(w["L1_ffn_W1"][e])), (w2[:, e, :, :], by_halves(w["L1_ffn_W2"][e])),
                      (wo[:, e, :, :], by_halves(w["L1_ffn_Wo"][e]))]
        for layer, names in enumerate((("b1", "g1", "be1", "m1", "v1"), ("b2", "g2", "be2", "m2", "v2"))):
            for k, n in enumerate(names):
                loads.append((bn[:, layer, k, :, :], w[f"L1_ffn_{n}"].rearrange("e (m p) -> p e m", p=P)))
        turn_and_project(nc, c, "l_n", xs, xT, True, loads=[
            (wr[:, :, :], by_halves(w["L1_ffn_Wr"])), (br[:, :], spread_row(w["L1_ffn_br"]))], later_loads=loads,
            projections=[(wr, br[:, :], None, gate, None)])
        top = sb("top", [P, NT])
        spread = sb("spread", [P, 2, E, KD])
        norm, shifted, exped, asked, rooted = (sem(n) for n in ("norm", "shifted", "exped", "asked", "rooted"))
        with nc.Block() as block:
            @block.vector
            def _(v):
                step = Steps(nc, v, norm)

                def wide(a):
                    return a.unsqueeze(2).broadcast_to([P, NT, E])

                step.link(nc.vector.tensor_reduce(top[:, :], gate[:, :, :], AX.X, ALU.max))
                nc.vector.tensor_tensor(gate[:, :, :], gate[:, :, :], wide(top[:, :]), ALU.subtract).then_inc(shifted, 1)
                step.link(nc.vector.tensor_scalar(spread[:, :, :, :], bn[:, :, 4, :, :], eps, None, ALU.add))
                inverse_root(nc, v, step, spread[:, :, :, :], scale[:, :, :, :], asked, rooted)
                step.mark(nc.vector.tensor_tensor(bias[:, :, :, :], bn[:, :, 0, :, :], bn[:, :, 3, :, :], ALU.subtract))
                step.link(nc.vector.tensor_tensor(scale[:, :, :, :], scale[:, :, :, :], bn[:, :, 1, :, :], ALU.mult))
                step.link(nc.vector.tensor_tensor(bias[:, :, :, :], bias[:, :, :, :], scale[:, :, :, :], ALU.mult))
                step.link(nc.vector.tensor_tensor(bias[:, :, :, :], bias[:, :, :, :], bn[:, :, 2, :, :], ALU.add))
                v.wait_ge(exped, 1)
                step.link(nc.vector.tensor_reduce(top[:, :], gate[:, :, :], AX.X, ALU.add))
                step.link(nc.vector.reciprocal(top[:, :], top[:, :]))
                step.link(nc.vector.tensor_tensor(gate[:, :, :], gate[:, :, :], wide(top[:, :]), ALU.mult))

            @block.scalar
            def _(act):
                act.wait_ge(shifted, 1)
                nc.scalar.activation(gate[:, :, :], gate[:, :, :], ACT.Exp).then_inc(exped, 1)
                take_root(nc, act, spread[:, :, :, :], scale[:, :, :, :], asked, rooted)
        experts(nc, c, "l_e", xT, xs, gate,
                [(w1, ACT.Relu, scale[:, 0, :, :], bias[:, 0, :, :]), (w2, ACT.Relu, scale[:, 1, :, :], bias[:, 1, :, :])],
                wo, bo)


def two_convolutions(nc, c, g1, w, xs, scratch):
    def relu(step, got):
        step.link(nc.vector.tensor_scalar(xs[:, :, :], got, 0.0, None, ALU.max))

    graph_attention(nc, c, g1, "c1", xs, True, w["L0_gnn_W1"],
                    w["L0_gnn_att_src1"], w["L0_gnn_att_dst1"], w["L0_gnn_b1"], 8, scratch, relu)

    def add(step, got):
        step.eng.wait_ge(back, 32)
        step.link(nc.vector.tensor_tensor(xs[:, :, :], xs[:, :, :], got, ALU.add))

    with ExitStack() as s:
        back = s.enter_context(nc.semaphore("x_back"))
        graph_attention(nc, c, g1, "c2", xs, False, w["L0_gnn_W2"],
                        w["L0_gnn_att_src2"], w["L0_gnn_att_dst2"], w["L0_gnn_b2"], 1, scratch, add,
                        load=lambda sp: load_rows(sp, xs, w["x"], back))


def clear_semaphores(nc):
    ids = sorted({int(x) for x in nc.released_uncleared_semaphores})
    runs = []
    for i in ids:
        if runs and runs[-1].stop == i:
            runs[-1] = range(runs[-1].start, i + 1)
        else:
            runs.append(range(i, i + 1))
    for run in runs:
        nc.all_engine_barrier(sems_to_clear=run)


def gnn_ffn_program(nc, w, out):
    with ExitStack() as ctx:
        g1 = Graph("g1", w["dst"].shape[0], NT, 125, 20)
        g2 = Graph("g2", w["L0_ffn_edge_index"].shape[1], 2048 // P, P, 32)
        c = open_constants(nc, ctx)
        open_graph(nc, ctx, g1, True)
        open_graph(nc, ctx, g2, False)
        scratch = {"table": nc.dram_tensor("table", (NP * 2 * D,), F32).ap(),
                   "spill": nc.dram_tensor("spill", (g1.chunks * P * D,), F32).ap()}
        with ExitStack() as sorting:
            open_sort_constants(nc, sorting, c, g1.chunks)
            make_constants(nc, c)
            for g, dst, src, kind in ((g1, w["dst"], w["src"], w["edge_type_64"]),
                                      (g2, w["L0_ffn_edge_index"][1], w["L0_ffn_edge_index"][0], None)):
                meta = nc.dram_tensor(f"{g.name}_meta", (g.chunks * P + 2, FIELDS), I32).ap()
                packed = nc.dram_tensor("packed_edges", (g.lanes * g.cols // P + 2, P), I32).ap() if g is g1 else None
                sort_edges(nc, c, g, dst, src, kind, meta, packed)
                load_sorted(nc, c, g, meta)
        clear_semaphores(nc)
        xs = ctx.enter_context(nc.sbuf_tensor("xs", [P, NT, D], F32))
        load_x(nc, w["x"], xs)
        two_convolutions(nc, c, g1, w, xs, scratch)
        clear_semaphores(nc)
        feed_forward_top_two(nc, c, g2, w, xs, scratch)
        clear_semaphores(nc)
        relation_attention(nc, c, g1, w, xs, scratch)
        clear_semaphores(nc)
        feed_forward_all(nc, c, w, xs)
        store_x(nc, xs, out)


def kernel(**inputs):
    import concourse.bacc as bacc
    from concourse.bass_utils import run_bass_kernel_spmd

    nc = bacc.Bacc("TRN2", target_bir_lowering=False, num_devices=1)
    arrays, w = {}, {}
    for name, value in inputs.items():
        a = np.ascontiguousarray(value)
        arrays[f"in_{name}"] = a
        w[name] = nc.dram_tensor(f"in_{name}", a.shape, mybir.dt.from_np(a.dtype), kind="ExternalInput").ap()
    out = nc.dram_tensor("out_x", inputs["x"].shape, F32, kind="ExternalOutput").ap()
    gnn_ffn_program(nc, w, out)
    r = run_bass_kernel_spmd(nc, [arrays], core_ids=[0])
    return r.results[0]["out_x"]
```
